# Optimizing a Trainium2 kernel written in Bass

```python
import numpy as np
import jax
import jax.numpy as jnp

def _softmax(x, axis=-1):
    return jax.nn.softmax(x, axis=axis)

def _gelu(x):
    return jax.nn.gelu(x, approximate=True)

def _silu(x):
    return jax.nn.silu(x)

def _sigmoid(x):
    return jax.nn.sigmoid(x)

def _layernorm(x, axis=-1, eps=1e-05):
    m = jnp.mean(x, axis=axis, keepdims=True)
    v = jnp.var(x, axis=axis, keepdims=True)
    return (x - m) / jnp.sqrt(v + eps)

def _scatter_add(tgt, idx, src, axis=0):
    return tgt.at[idx].add(src)

def _segment_sum(src, seg, n):
    return jax.ops.segment_sum(src, seg, n)
kernel_name = 'mk_gnn_resnorm_d2_gnn_r32_27e03a'

def setup_inputs(seed: int=0):
    np.random.seed(seed)
    _w = jnp.asarray

    def _rec_inputs():
        import jax
        import jax.numpy as jnp
        _gk = jax.random.key(seed)
        x = -8.776e-05 + 1 * jax.random.normal(jax.random.fold_in(_gk, 1), (10000, 512), jnp.float32)
        src = jax.random.randint(jax.random.fold_in(_gk, 2), (10000,), 0, 10000, jnp.int32)
        dst = jnp.minimum((10000 * jax.random.uniform(jax.random.fold_in(_gk, 3), (10000,)) ** 2.0).astype(jnp.int32), 9999)
        _o = jnp.argsort(dst, stable=True)
        src = src[_o]
        dst = dst[_o]
        edge_attr_64 = 0.000279952 + 1.00013 * jax.random.normal(jax.random.fold_in(_gk, 12), (10000, 64), jnp.float32)
        return (x, src, dst, edge_attr_64)
    x, src, dst, edge_attr_64 = _rec_inputs()

    def _L0_gnn_setup():
        import jax, jax.numpy as jnp
        import numpy as np
        N_NODES = 10000
        N_EDGES = 5000
        D_IN = 512
        D_HID = 1024
        key = jax.random.key(seed)
        ks = jax.random.split(key, 8)
        feat = jax.random.normal(ks[0], (N_NODES, D_IN), dtype=jnp.float32)
        W1 = jax.random.normal(ks[1], (D_IN, D_HID), dtype=jnp.float32) * (1.0 / np.sqrt(D_IN))
        b1 = jnp.zeros((D_HID,), dtype=jnp.float32)
        W2 = jax.random.normal(ks[2], (D_HID, D_IN), dtype=jnp.float32) * (1.0 / np.sqrt(D_HID))
        b2 = jnp.zeros((D_IN,), dtype=jnp.float32)
        eps = jnp.zeros((1,), dtype=jnp.float32)
        src = jax.random.randint(ks[3], (N_EDGES,), 0, N_NODES, dtype=jnp.int32)
        dst = jax.random.randint(ks[4], (N_EDGES,), 0, N_NODES, dtype=jnp.int32)
        return {'feat': feat, 'W1': W1, 'b1': b1, 'W2': W2, 'b2': b2, 'eps': eps, 'src': src, 'dst': dst}
    _L0_gnn_all = _L0_gnn_setup()
    _L0_gnn_in = {k: v for k, v in _L0_gnn_all.items() if k in ('W1', 'b1', 'W2', 'b2', 'eps')}
    del _L0_gnn_all

    def _L1_gnn_setup():
        import jax, jax.numpy as jnp
        import numpy as np
        N_NODES = 625
        N_EDGES = 10000
        HIDDEN = 512
        EDGE_DIM = 64
        LN_EPS = 1e-05

        def mish(x):
            return x * jnp.tanh(jax.nn.softplus(x))
        key = jax.random.key(seed)
        ks = jax.random.split(key, 8)
        s = lambda fan_in: 1.0 / np.sqrt(fan_in)
        return {'x': jax.random.normal(ks[0], (N_NODES, HIDDEN), dtype=jnp.float32), 'edge_index': jax.random.randint(ks[1], (2, N_EDGES), 0, N_NODES, dtype=jnp.int64), 'edge_attr': jax.random.normal(ks[2], (N_EDGES, EDGE_DIM), dtype=jnp.float32), 'W1': jax.random.normal(ks[3], (2 * HIDDEN + EDGE_DIM, HIDDEN), dtype=jnp.float32) * s(2 * HIDDEN + EDGE_DIM), 'b1': jnp.zeros((HIDDEN,), dtype=jnp.float32), 'W2': jax.random.normal(ks[4], (HIDDEN, HIDDEN), dtype=jnp.float32) * s(HIDDEN), 'b2': jnp.zeros((HIDDEN,), dtype=jnp.float32), 'W3': jax.random.normal(ks[5], (2 * HIDDEN, HIDDEN), dtype=jnp.float32) * s(2 * HIDDEN), 'b3': jnp.zeros((HIDDEN,), dtype=jnp.float32), 'W4': jax.random.normal(ks[6], (HIDDEN, HIDDEN), dtype=jnp.float32) * s(HIDDEN), 'b4': jnp.zeros((HIDDEN,), dtype=jnp.float32), 'gamma': jnp.ones((HIDDEN,), dtype=jnp.float32), 'beta': jnp.zeros((HIDDEN,), dtype=jnp.float32)}
    _L1_gnn_all = _L1_gnn_setup()
    _L1_gnn_in = {k: v for k, v in _L1_gnn_all.items() if k in ('W1', 'b1', 'W2', 'b2', 'W3', 'b3', 'W4', 'b4', 'gamma', 'beta')}
    del _L1_gnn_all
    return {'x': x, 'src': src, 'dst': dst, 'edge_attr_64': edge_attr_64, 'L0_gnn_W1': _L0_gnn_in['W1'], 'L0_gnn_b1': _L0_gnn_in['b1'], 'L0_gnn_W2': _L0_gnn_in['W2'], 'L0_gnn_b2': _L0_gnn_in['b2'], 'L0_gnn_eps': _L0_gnn_in['eps'], 'L1_gnn_W1': _L1_gnn_in['W1'], 'L1_gnn_b1': _L1_gnn_in['b1'], 'L1_gnn_W2': _L1_gnn_in['W2'], 'L1_gnn_b2': _L1_gnn_in['b2'], 'L1_gnn_W3': _L1_gnn_in['W3'], 'L1_gnn_b3': _L1_gnn_in['b3'], 'L1_gnn_W4': _L1_gnn_in['W4'], 'L1_gnn_b4': _L1_gnn_in['b4'], 'L1_gnn_gamma': _L1_gnn_in['gamma'], 'L1_gnn_beta': _L1_gnn_in['beta']}

def reference(x, src, dst, edge_attr_64, L0_gnn_W1, L0_gnn_b1, L0_gnn_W2, L0_gnn_b2, L0_gnn_eps, L1_gnn_W1, L1_gnn_b1, L1_gnn_W2, L1_gnn_b2, L1_gnn_W3, L1_gnn_b3, L1_gnn_W4, L1_gnn_b4, L1_gnn_gamma, L1_gnn_beta):
    import jax
    import jax.numpy as jnp

    def _L0_gnn_ref(feat, W1, b1, W2, b2, eps, src, dst):
        import jax, jax.numpy as jnp
        import numpy as np
        N_NODES = 10000
        N_EDGES = 5000
        D_IN = 512
        D_HID = 1024
        msgs = feat[src]
        neigh = jax.ops.segment_sum(msgs, dst, num_segments=feat.shape[0])
        rst = (1.0 + eps[0]) * feat + neigh
        h = jnp.maximum(rst @ W1 + b1, 0.0)
        h = h @ W2 + b2
        return h + feat

    def _L1_gnn_ref(x, edge_index, edge_attr, W1, b1, W2, b2, W3, b3, W4, b4, gamma, beta):
        import jax, jax.numpy as jnp
        import numpy as np
        N_NODES = 625
        N_EDGES = 10000
        HIDDEN = 512
        EDGE_DIM = 64
        LN_EPS = 1e-05

        def mish(x):
            return x * jnp.tanh(jax.nn.softplus(x))
        src, dst = (edge_index[0], edge_index[1])
        edge_feat = jnp.concatenate([x[src], x[dst], edge_attr], axis=-1)
        h = mish(edge_feat @ W1 + b1)
        messages = mish(h @ W2 + b2)
        agg = jax.ops.segment_sum(messages, dst, num_segments=x.shape[0])
        u = mish(jnp.concatenate([x, agg], axis=-1) @ W3 + b3)
        out = u @ W4 + b4
        y = x + out
        mu = jnp.mean(y, axis=-1, keepdims=True)
        var = jnp.mean(jnp.square(y - mu), axis=-1, keepdims=True)
        return (y - mu) * jax.lax.rsqrt(var + LN_EPS) * gamma + beta
    edge_index = jnp.stack([src, dst])
    x = _layernorm(x + _L0_gnn_ref(x, L0_gnn_W1, L0_gnn_b1, L0_gnn_W2, L0_gnn_b2, L0_gnn_eps, src, dst), axis=-1)
    x = _layernorm(x + _L1_gnn_ref(x, edge_index, edge_attr_64, L1_gnn_W1, L1_gnn_b1, L1_gnn_W2, L1_gnn_b2, L1_gnn_W3, L1_gnn_b3, L1_gnn_W4, L1_gnn_b4, L1_gnn_gamma, L1_gnn_beta), axis=-1)
    return x

_drawn_inputs = setup_inputs


def setup_inputs(seed=0):
    import zlib

    import numpy as np

    out = dict(_drawn_inputs(seed))
    spreads = {'L0_gnn_b1': (0.0, 0.1),
     'L0_gnn_b2': (0.0, 0.1),
     'L1_gnn_b1': (0.0, 0.522),
     'L1_gnn_b2': (0.0, 0.341),
     'L1_gnn_b3': (0.0, 0.1),
     'L1_gnn_b4': (0.0, 0.1),
     'L1_gnn_gamma': (1.0, 0.2),
     'L1_gnn_beta': (0.0, 0.1)}
    factors = {}
    for name, (base, spread) in spreads.items():
        noise = np.random.default_rng([zlib.crc32(name.encode()), seed]).standard_normal(out[name].shape)
        drawn = base * np.exp(spread * noise) if base else spread * noise
        out[name] = jnp.asarray(drawn.astype(out[name].dtype))
    for name, factor in factors.items():
        out[name] = (out[name] * factor).astype(out[name].dtype)
    return out
```

```python
import concourse.bass as bass
from concourse import mybir
from contextlib import ExitStack

F32 = mybir.dt.float32
F32R = mybir.dt.float32r
I32 = mybir.dt.int32
ALU = mybir.AluOpType
ACT = mybir.ActivationFunctionType
AX = mybir.AxisListType

P = 128
D = 512
DH = 1024
DE = 64
N = 10000
TPB = 4
BLK = TPB * P
NBLK = -(-N // BLK)
LASTB = NBLK - 1
LASTROWS = N - LASTB * BLK
NT = -(-N // P)
LN_EPS = 1e-5
ZCAP = 20.0
SEGROWS = (NBLK + 1) * BLK
KD = D // P
KH = DH // P
RSQRT_STEPS = 4


def rows_of(b):
    if isinstance(b, int) and b == LASTB:
        left, out = LASTROWS, []
        while left > 0:
            out.append(min(left, P))
            left -= P
        return out
    return [P] * TPB


def spans_of(b):
    rows = rows_of(b)
    full = sum(r == P for r in rows)
    spans = [(P, 0, full)]
    if full < len(rows):
        spans.append((rows[-1], full, len(rows)))
    return spans


def blocks(eng, f, first=1, end=LASTB):
    for b in range(first):
        f(b)
    with eng.Fori(first, end) as b:
        f(b)
    for b in range(end, NBLK):
        f(b)


def wait(eng, sem, value):
    if not isinstance(value, int) or value > 0:
        eng.wait_ge(sem, value)


def ndma(b):
    return len(spans_of(b))


def gnn_resnorm_kernel(nc, x, src, dst, edge_attr, w1a, b1a, w2a, b2a, eps, w1, b1, w2, b2,
                       w3, b3, w4, b4, gamma, beta, out):
    seg0 = nc.dram_tensor("seg0", (SEGROWS, D), F32, kind="Internal").ap()
    seg1 = nc.dram_tensor("seg1", (SEGROWS, D), F32, kind="Internal").ap()
    x1 = nc.dram_tensor("x1", (N, D), F32, kind="Internal").ap()

    ctx = ExitStack()
    with ctx:
        def maker(stack):
            def sb(name, shape, dt=F32):
                return stack.enter_context(nc.sbuf_tensor(name, shape, dt))

            def sem(name):
                return stack.enter_context(nc.semaphore(name))
            return sb, sem

        sb, sem = maker(ctx)
        WELEMS = 2 * (8 + 4) * D + 2 * D
        W = sb("W", [P, WELEMS], F32R)
        RAWK = 13
        RAW = sb("RAW", [P, RAWK, D])
        ident = sb("ident", [P, P])
        dstF = sb("dstF", [P, NT + 1])
        srcI = sb("srcI", [P, NT + 1], I32)
        dstI = sb("dstI", [P, NT + 1], I32)
        tgt0 = sb("tgt0", [P, NT + 1], I32)
        tgt1 = sb("tgt1", [P, NT + 1], I32)
        bank = [ctx.enter_context(nc.psum_tensor(f"bank{i}", [P, 512], F32)) for i in range(8)]

        two = sb("two", [P, 1])
        ticks = sem("ticks")

        def settle(eng):
            eng.sem_inc(ticks, 1)

        raw1_in, raw2_in = sem("raw1_in"), sem("raw2_in")

        with ExitStack() as ph:
            sb, sem = maker(ph)
            ii = sb("ii", [P, 2, P], I32)
            iF = sb("iF", [P, 2, P])
            idx_blank, idx_in, idx_f, idx_t, idx_done = [sem(f"idx{i}") for i in range(5)]
            id_blank, id_set = sem("id_blank"), sem("id_set")
            with nc.Block() as block:
                @block.sync
                def _(sp):
                    full = N // P
                    sp.wait_ge(idx_blank, 1)
                    for j, a in enumerate((src, dst)):
                        sp.dma_start(ii[0:full, j, :], a[0:full * P].rearrange("(t p) -> t p", p=P)).then_inc(idx_in, 16)
                        sp.dma_start(ii[full:full + 1, j, 0:N - full * P], a[full * P:N].rearrange("(t p) -> t p", t=1)).then_inc(idx_in, 16)

                @block.gpsimd
                def _(pool):
                    nc.gpsimd.memset(ident[:, :], 0.0).then_inc(id_blank, 1)
                    pool.wait_ge(id_blank, 1)
                    nc.gpsimd.affine_select(out=ident[:, :], in_=ident[:, :], compare_op=ALU.not_equal, fill=1.0,
                                            base=0, pattern=[[-1, P]], channel_multiplier=1).then_inc(id_set, 1)

                @block.vector
                def _(dve):
                    nc.vector.memset(ii[:, :, :], -1).then_inc(idx_blank, 1)
                    nc.vector.memset(two[:, :], 2.0)
                    dve.wait_ge(idx_in, 64)
                    nc.vector.tensor_copy(iF[:, :, :], ii[:, :, :]).then_inc(idx_f, 1)
                    dve.wait_ge(idx_t, 1)
                    nc.vector.tensor_copy(dstF[:, :], bank[1][:, 0:NT + 1])
                    nc.vector.tensor_copy(dstI[:, :], bank[1][:, 0:NT + 1])
                    nc.vector.tensor_copy(srcI[:, :], bank[0][:, 0:NT + 1]).then_inc(idx_done, 1)

                @block.tensor
                def _(pe):
                    pe.wait_ge(idx_f, 1)
                    pe.wait_ge(id_set, 1)
                    nc.tensor.transpose(bank[0][:, 0:P], iF[:, 0, :], ident[:, :])
                    nc.tensor.transpose(bank[1][:, 0:P], iF[:, 1, :], ident[:, :]).then_inc(idx_t, 1)

        UNITS = 13
        WHI = W[:, 0:UNITS * D].rearrange("p (u n) -> p u n", n=D)
        WLO = W[:, UNITS * D:2 * UNITS * D].rearrange("p (u n) -> p u n", n=D)

        layer0 = ctx.enter_context(ExitStack())
        WX = layer0.enter_context(nc.sbuf_tensor("WX", [P, 8, D], F32R))
        A1H, A1L = W[:, 0:8 * D].rearrange("p (k n) -> p k n", n=DH), W[:, 8 * D:16 * D].rearrange("p (k n) -> p k n", n=DH)
        A2H, A2L = W[:, 16 * D:24 * D].rearrange("p (k n) -> p k n", n=D), WX[:, :, :]

        with ExitStack() as ph:
            sb, sem = maker(ph)
            zero = sb("zero", [P, TPB, D])
            XG = sb("XG", [P, TPB, D])
            GH = sb("GH", [P, TPB, D], F32R)
            GL = sb("GL", [P, TPB, D], F32R)
            EQ = sb("EQ", [P, TPB, BLK], F32R)
            earlier = sb("earlier", [P, TPB, BLK])
            TM = sb("TM", [P, TPB, BLK])
            DR = sb("DR", [P, BLK], I32)
            SG = sb("SG", [P, TPB, D])
            dup = sb("dup", [P, 2, TPB])
            keep = sb("keep", [P, 2, TPB])
            spare = sb("spare", [P, TPB])
            off = sb("off", [P, 2, TPB])
            move = sb("move", [P, 2, TPB])
            gidx = sb("gidx", [P, TPB], I32)
            sidx = sb("sidx", [P, TPB], I32)
            zero_set, zeroed, spare_set, mask_blank, mask_set = [sem(n) for n in ("zero_set", "zeroed", "spare_set", "mask_blank", "mask_set")]
            dr_in, gidx_set, sidx_set = sem("dr_in"), sem("gidx_set"), sem("sidx_set")
            xg_in = [sem(f"xg_in{r}") for r in range(TPB)]
            gh_set, gl_set, eq_set, tm_set, dup_set, keep_set, off_set, move_set, tgt_set = [
                sem(n) for n in ("gh_set", "gl_set", "eq_set", "tm_set", "dup_set", "keep_set", "off_set", "move_set", "tgt_set")]
            sum_done, sg_set = sem("sum_done"), sem("sg_set")
            w0_in, w0_hi, w0_lo = sem("w0_in"), sem("w0_hi"), sem("w0_lo")
            w0 = [(RAW[:, 0:8, :].rearrange("p (k h) n -> p k (h n)", h=2), A1H, A1L), (RAW[:, 0:8, :], A2H, A2L)]
            scat = [sem(f"scat0_{r}") for r in range(TPB)]

            with nc.Block() as block:
                @block.sync
                def _(sp):
                    r1, r2 = RAW[:, 0:8, :].rearrange("p (k h) n -> p k (h n)", h=2), RAW[:, 0:8, :]
                    sp.dma_start(r1, w1a.rearrange("(k p) n -> p k n", p=P)).then_inc(w0_in, 16)
                    sp.wait_ge(w0_lo, 1)
                    sp.dma_start(r2, w2a.rearrange("(k p) n -> p k n", p=P)).then_inc(w0_in, 16)
                    sp.wait_ge(zero_set, 1)
                    for c in range(SEGROWS // BLK):
                        sp.dma_start(seg0[c * BLK:(c + 1) * BLK, :].rearrange("(p r) d -> p r d", p=P), zero[:, :, :]).then_inc(zeroed, 16)

                    def load(b):
                        n = sum(rows_of(b))
                        wait(sp, eq_set, TPB * b)
                        sp.dma_start(DR[:, 0:n], dst[bass.ds(b * BLK, n)].partition_broadcast(P)).then_inc(dr_in, 16)
                    blocks(sp, load)

                @block.gpsimd
                def _(pool):
                    nc.gpsimd.memset(zero[:, :, :], 0.0).then_inc(zero_set, 1)
                    nc.gpsimd.iota(spare[:, :], pattern=[[P, TPB]], base=N, channel_multiplier=1,
                                   allow_small_or_imprecise_dtypes=True).then_inc(spare_set, 1)
                    nc.gpsimd.memset(earlier[:, :, :], 1.0).then_inc(mask_blank, 1)
                    pool.wait_ge(mask_blank, 1)
                    nc.gpsimd.affine_select(out=earlier[:, :, :], in_=earlier[:, :, :], compare_op=ALU.is_gt, fill=0.0,
                                            base=0, pattern=[[P, TPB], [-1, BLK]], channel_multiplier=1).then_inc(mask_set, 1)

                    def gather(b):
                        rows = rows_of(b)
                        for r in range(TPB):
                            wait(pool, xg_in[r], 16 * b)
                        wait(pool, gl_set, b)
                        nt = len(rows)
                        nc.gpsimd.tensor_copy(gidx[:, 0:nt], srcI[:, bass.ds(b * TPB, nt)]).then_inc(gidx_set, 1)
                        pool.wait_ge(gidx_set, b + 1)
                        settle(pool)
                        for r, n in enumerate(rows):
                            nc.gpsimd.indirect_dma_start(XG[0:n, r, :], None, x[:, :],
                                                         bass.IndirectOffsetOnAxis(gidx[0:n, r:r + 1], 0)).then_inc(xg_in[r], 16)

                    def scatter(b):
                        rows = rows_of(b)
                        nt = len(rows)
                        for r in range(TPB):
                            wait(pool, scat[r], 16 * b)
                        pool.wait_ge(tgt_set, b + 1)
                        nc.gpsimd.tensor_copy(sidx[:, 0:nt], tgt0[:, bass.ds(b * TPB, nt)]).then_inc(sidx_set, 1)
                        pool.wait_ge(sidx_set, b + 1)
                        for r, n in enumerate(rows):
                            pool.wait_ge(sg_set, TPB * b + r + 1)
                            settle(pool)
                            nc.gpsimd.indirect_dma_start(seg0[:, :], bass.IndirectOffsetOnAxis(sidx[0:n, r:r + 1], 0),
                                                         SG[0:n, r, :], None, compute_op=ALU.add).then_inc(scat[r], 16)

                    gather(0)
                    pool.wait_ge(zeroed, 16 * (SEGROWS // BLK))
                    gather(1)
                    scatter(0)
                    with pool.Fori(1, LASTB - 1) as b:
                        gather(b + 1)
                        scatter(b)
                    gather(LASTB)
                    scatter(LASTB - 1)
                    scatter(LASTB)
                    for r in range(TPB):
                        pool.wait_ge(scat[r], 16 * (NBLK if r < len(rows_of(LASTB)) else LASTB))

                @block.scalar
                def _(act):
                    for j, (raw, hi, lo) in enumerate(w0):
                        act.wait_ge(w0_in, 16 * (j + 1))
                        nc.scalar.copy(hi, raw).then_inc(w0_hi, 1)

                    def f(b):
                        nt = len(rows_of(b))
                        for r in range(nt):
                            act.wait_ge(xg_in[r], 16 * b + 16)
                        wait(act, sum_done, TPB * b)
                        nc.scalar.copy(GH[:, 0:nt, :], XG[:, 0:nt, :]).then_inc(gh_set, 1)
                        for r in range(nt):
                            act.wait_ge(sum_done, TPB * b + r + 1)
                            wait(act, scat[r], 16 * b)
                            nc.scalar.copy(SG[:, r, :], bank[r][:, :]).then_inc(sg_set, 1)
                    blocks(act, f)

                @block.vector
                def _(dve):
                    for j, (raw, hi, lo) in enumerate(w0):
                        dve.wait_ge(w0_hi, j + 1)
                        nc.vector.tensor_tensor(lo, raw, hi.bitcast(F32), ALU.subtract).then_inc(w0_lo, 1)
                    dve.wait_ge(mask_set, 1)
                    dve.wait_ge(spare_set, 1)

                    def f(b):
                        nt = len(rows_of(b))
                        dve.wait_ge(gh_set, b + 1)
                        nc.vector.tensor_tensor(GL[:, 0:nt, :], XG[:, 0:nt, :], GH[:, 0:nt, :].bitcast(F32), ALU.subtract).then_inc(gl_set, 1)
                        dve.wait_ge(dr_in, 16 * b + 16)
                        for t in range(TPB):
                            if t < nt:
                                nc.vector.tensor_scalar(EQ[:, t, :], DR[:, :], dstF[:, bass.ds(b * TPB + t, 1)], None, ALU.is_equal).then_inc(eq_set, 1)
                        dve.wait_ge(eq_set, TPB * b + nt)
                        nc.vector.tensor_tensor(TM[:, 0:nt, :], EQ[:, 0:nt, :].bitcast(F32), earlier[:, 0:nt, :], ALU.mult).then_inc(tm_set, 1)
                        dve.wait_ge(tm_set, b + 1)
                        for t in range(nt):
                            nc.vector.tensor_reduce(dup[:, 1, t:t + 1], TM[:, t, t * P:(t + 1) * P], AX.X, ALU.max)
                        nc.vector.tensor_reduce(dup[:, 0, 0:nt], TM[:, 0:nt, :], AX.X, ALU.max).then_inc(dup_set, 1)
                        dve.wait_ge(dup_set, b + 1)
                        for w in range(2):
                            nc.vector.tensor_tensor(off[:, w, 0:nt], spare[:, 0:nt], dstF[:, bass.ds(b * TPB, nt)], ALU.subtract).then_inc(off_set, 1)
                        dve.wait_ge(off_set, 2 * b + 2)
                        nc.vector.tensor_tensor(move[:, :, 0:nt], off[:, :, 0:nt], dup[:, :, 0:nt], ALU.mult).then_inc(move_set, 1)
                        dve.wait_ge(move_set, b + 1)
                        for w, tgt in enumerate((tgt0, tgt1)):
                            last = nc.vector.tensor_tensor(tgt[:, bass.ds(b * TPB, nt)], move[:, w, 0:nt], dstF[:, bass.ds(b * TPB, nt)], ALU.add)
                        last.then_inc(tgt_set, 1)
                    blocks(dve, f)

                @block.tensor
                def _(pe):
                    def f(b):
                        nt = len(rows_of(b))
                        pe.wait_ge(gl_set, b + 1)
                        pe.wait_ge(eq_set, TPB * b + nt)
                        for a in range(nt):
                            wait(pe, sg_set, TPB * (b - 1) + a + 1)
                            for t in range(nt):
                                nc.tensor.matmul(bank[a][:, :], EQ[:, t, a * P:(a + 1) * P], GH[:, t, :], start=t == 0, stop=False)
                                last = nc.tensor.matmul(bank[a][:, :], EQ[:, t, a * P:(a + 1) * P], GL[:, t, :], start=False, stop=t == nt - 1)
                            last.then_inc(sum_done, 1)
                    blocks(pe, f)


        def mm3(acc, ah, al, bh, bl, start, stop):
            nc.tensor.matmul(acc, ah, bh, start=start, stop=False)
            nc.tensor.matmul(acc, ah, bl, start=False, stop=False)
            return nc.tensor.matmul(acc, al, bh, start=False, stop=stop)

        class Norm:
            LINKS = 4 + 3 * RSQRT_STEPS

            def __init__(self, sb, sem, name):
                self.st = sb(name + "_st", [P, TPB, 6])
                self.mv = sb(name + "_mv", [P, TPB, 2])
                self.h, self.y, self.t, self.a = [sb(name + "_" + c, [P, TPB]) for c in "hyta"]
                self.st_set, self.link = sem(name + "_st_set"), sem(name + "_link")

            def blank(self):
                nc.vector.memset(self.mv[:, :, :], 1.0)

            def stats(self, rows):
                self.rows = rows
                return lambda r: nc.vector.bn_stats(self.st[:, r, :], rows[:, r, :])

            def rstd(self, dve, n, nt):
                settle(dve)
                for r in range(nt):
                    last = nc.vector.bn_aggr(self.mv[:, r, :], self.st[:, r, :])
                at = [self.LINKS * n]

                def link(i):
                    at[0] += 1
                    i.then_inc(self.link, 1)
                    dve.wait_ge(self.link, at[0])
                link(last)
                link(nc.vector.tensor_scalar(self.a[:, :], self.mv[:, :, 1], LN_EPS, None, ALU.add))
                nc.vector.tensor_scalar(self.h[:, :], self.a[:, :], -0.5, None, ALU.mult)
                link(nc.vector.tensor_scalar(self.t[:, :].bitcast(I32), self.a[:, :].bitcast(I32), 1, None, ALU.logical_shift_right))
                link(nc.vector.tensor_scalar(self.y[:, :].bitcast(I32), self.t[:, :].bitcast(I32), -1.0, float(0x5f3759df), ALU.mult, ALU.add))
                for _ in range(RSQRT_STEPS):
                    link(nc.vector.tensor_tensor(self.t[:, :], self.y[:, :], self.y[:, :], ALU.mult))
                    link(nc.vector.tensor_tensor(self.t[:, :], self.t[:, :], self.h[:, :], ALU.mult))
                    link(nc.vector.scalar_tensor_tensor(self.y[:, :], self.t[:, :], 1.5, self.y[:, :], ALU.add, ALU.mult))

        class Mish:

            def __init__(self, sb, sem, name, keep_z):
                self.Z, self.N, self.R = [sb(name + c, [P, 2, D]) for c in "ZNR"]
                self.V = sb(name + "V", [P, 2, D]) if keep_z else None
                self.v_set = sem(name + "_v_set") if keep_z else None
                (self.z_set, self.e_set, self.n_set, self.l_set, self.r_set, self.t_set, self.m_set, self.hi_set,
                 self.lo_set) = [sem(f"{name}_{c}_set") for c in ("z", "e", "n", "l", "r", "t", "m", "hi", "lo")]

            def z_col(self, dve, i, s, ps, bias, c):
                wait(dve, self.lo_set, i - 1)
                nc.vector.tensor_scalar(self.Z[:, s, 0:c], ps, bias, ZCAP, ALU.add, ALU.min).then_inc(self.z_set, 1)

            def z_row(self, dve, i, s, ps, bias):
                wait(dve, self.lo_set, i - 1)
                nc.vector.tensor_tensor(self.V[:, s, :], ps, bias, ALU.add).then_inc(self.v_set, 1)
                dve.wait_ge(self.v_set, i + 1)
                nc.vector.tensor_scalar(self.Z[:, s, :], self.V[:, s, :], ZCAP, None, ALU.min).then_inc(self.z_set, 1)

            def e(self, act, i, s, c):
                act.wait_ge(self.z_set, i + 1)
                nc.scalar.activation(self.Z[:, s, 0:c], self.Z[:, s, 0:c], ACT.Exp).then_inc(self.e_set, 1)

            def n(self, dve, i, s, c):
                dve.wait_ge(self.e_set, i + 1)
                z = self.Z[:, s, 0:c]
                nc.vector.scalar_tensor_tensor(self.N[:, s, 0:c], z, 2.0, z, ALU.add, ALU.mult).then_inc(self.n_set, 1)

            def r(self, act, i, s, c):
                act.wait_ge(self.n_set, i + 1)
                nc.scalar.activation(self.R[:, s, 0:c], self.N[:, s, 0:c], ACT.Ln, bias=two[:, 0:1]).then_inc(self.l_set, 1)
                act.wait_ge(self.l_set, i + 1)
                nc.scalar.activation(self.R[:, s, 0:c], self.R[:, s, 0:c], ACT.Exp, scale=-1.0).then_inc(self.r_set, 1)

            def t(self, pool, i, s, c):
                pool.wait_ge(self.r_set, i + 1)
                nc.gpsimd.tensor_tensor(self.N[:, s, 0:c], self.N[:, s, 0:c], self.R[:, s, 0:c], ALU.mult).then_inc(self.t_set, 1)

            def m_col(self, dve, i, s, ps, bias, c):
                dve.wait_ge(self.t_set, i + 1)
                return nc.vector.scalar_tensor_tensor(self.Z[:, s, 0:c], ps, bias, self.N[:, s, 0:c], ALU.add, ALU.mult).then_inc(self.m_set, 1)

            def m_row(self, dve, i, s):
                dve.wait_ge(self.t_set, i + 1)
                return nc.vector.tensor_tensor(self.Z[:, s, :], self.V[:, s, :], self.N[:, s, :], ALU.mult).then_inc(self.m_set, 1)

            def hi(self, act, i, s, out, c):
                act.wait_ge(self.m_set, i + 1)
                nc.scalar.copy(out, self.Z[:, s, 0:c]).then_inc(self.hi_set, 1)

            def lo(self, pool, i, s, out, hi, c):
                pool.wait_ge(self.hi_set, i + 1)
                nc.gpsimd.tensor_tensor(out, self.Z[:, s, 0:c], hi.bitcast(F32), ALU.subtract).then_inc(self.lo_set, 1)

        class Turn:

            def __init__(self, sem, name):
                self.done, self.hi_set, self.lo_set = sem(name + "_done"), sem(name + "_hi"), sem(name + "_lo")

            def pe(self, pe, i, b, rows_buf, ks):
                wait(pe, self.lo_set, i)
                for j, k in enumerate(ks):
                    for r, n in enumerate(rows_of(b)):
                        last = nc.tensor.transpose(bank[j][:, r * P:r * P + n], rows_buf[0:n, r, k * P:(k + 1) * P], ident[0:n, 0:n])
                last.then_inc(self.done, 1)

            def hi(self, act, i, b, XH, ks):
                c = sum(rows_of(b))
                act.wait_ge(self.done, i + 1)
                for j, k in enumerate(ks):
                    last = nc.scalar.copy(XH[:, k, 0:c], bank[j][:, 0:c])
                last.then_inc(self.hi_set, 1)

            def lo(self, dve, i, b, XH, XL, ks):
                c = sum(rows_of(b))
                dve.wait_ge(self.hi_set, i + 1)
                for j, k in enumerate(ks):
                    last = nc.vector.tensor_tensor(XL[:, k, 0:c], bank[j][:, 0:c], XH[:, k, 0:c].bitcast(F32), ALU.subtract)
                last.then_inc(self.lo_set, 1)

        HBANK, YBANK = [bank[2], bank[3]], bank[4:8]

        def load_rows(eng, buf, dram, b, sem_):
            at = 0
            for n, t0, t1 in spans_of(b):
                c = n * (t1 - t0)
                eng.dma_start(buf[0:n, t0:t1, :], dram[bass.ds(b * BLK + at, c), :].rearrange("(t p) d -> p t d", p=n)).then_inc(sem_, 16)
                at += c

        def store_rows(eng, buf, dram, b, sem_):
            at = 0
            for n, t0, t1 in spans_of(b):
                c = n * (t1 - t0)
                eng.dma_start(dram[bass.ds(b * BLK + at, c), :].rearrange("(t p) d -> p t d", p=n), buf[0:n, t0:t1, :]).then_inc(sem_, 16)
                at += c

        def loaded(b):
            return 16 * (b + ndma(b))

        with ExitStack() as ph:
            sb, sem = maker(ph)
            XB, RS, YX = [sb(n, [P, TPB, D]) for n in ("XB", "RS", "YX")]
            XH, XL = [sb(n, [P, KD, BLK], F32R) for n in ("XH", "XL")]
            HH, HL = [sb(n, [P, KH, BLK], F32R) for n in ("HH", "HL")]
            HF = sb("HF", [P, 2, BLK])
            b1c, b2r, eps1, zb = sb("b1c", [P, KH]), sb("b2r", [P, D]), sb("eps1", [P, 1]), sb("zb", [P, TPB, D])
            norm = Norm(sb, sem, "n0")
            turn = Turn(sem, "t0")
            cst, e1_set, zb_set, zeroed = sem("cst0"), sem("e1_set"), sem("zb_set"), sem("zeroed1")
            xb_in, rs_in, yx_in, y_out = sem("xb_in"), sem("rs_in"), sem("yx_in"), sem("y_out")
            rst_set, h_done, f_set, hi_set, lo_set, hl_free = [sem("a_" + n) for n in ("rst_set", "h_done", "f_set", "hi_set", "lo_set", "hl_free")]
            y_done, y_read, x2_set, yp_set, y_set = [sem("a_" + n) for n in ("y_done", "y_read", "x2_set", "yp_set", "y_set")]
            TS = 2
            ALLB = NBLK

            with nc.Block() as block:
                @block.sync
                def _(sp):
                    with nc.allow_non_contiguous_dma(reason="a bias as a column"):
                        sp.dma_start(b1c[:, :], b1a.rearrange("(k p) -> p k", p=P)).then_inc(cst, 16)
                    sp.dma_start(b2r[:, :], b2a.partition_broadcast(P)).then_inc(cst, 16)
                    sp.dma_start(eps1[:, :], eps.partition_broadcast(P)).then_inc(cst, 16)

                    def load(b):
                        wait(sp, rst_set, b)
                        load_rows(sp, XB, x, b, xb_in)
                        wait(sp, turn.done, TS * b)
                        load_rows(sp, RS, seg0, b, rs_in)

                    def loady(b):
                        load_rows(sp, YX, x, b, yx_in)

                    def store(b):
                        sp.wait_ge(y_set, b + 1)
                        store_rows(sp, YX, x1, b, y_out)
                        sp.wait_ge(y_out, loaded(b))

                    load(0)
                    load(1)
                    loady(0)
                    sp.dma_start(RAW[:, 0:8, :], w1[0:8 * P, :].rearrange("(k p) n -> p k n", p=P)).then_inc(raw1_in, 16)
                    for half in range(2):
                        sp.dma_start(RAW[half * DE:(half + 1) * DE, 8, :], w1[8 * P:8 * P + DE, :]).then_inc(raw1_in, 16)
                    sp.dma_start(RAW[:, 9:13, :], w2.rearrange("(k p) n -> p k n", p=P)).then_inc(raw1_in, 16)
                    sp.wait_ge(zb_set, 1)
                    sp.dma_start(seg1[NBLK * BLK:SEGROWS, :].rearrange("(p r) d -> p r d", p=P), zb[:, :, :]).then_inc(zeroed, 16)

                    def body(b):
                        if b is not LASTB:
                            load(b + 1)
                        sp.dma_start(seg1[bass.ds((b - 1) * BLK, BLK), :].rearrange("(p r) d -> p r d", p=P), zb[:, :, :]).then_inc(zeroed, 16)
                        store(b - 1)
                        loady(b)
                    with sp.Fori(1, LASTB - 1) as b:
                        body(b)
                    body(LASTB - 1)
                    body(LASTB)
                    sp.dma_start(seg1[LASTB * BLK:NBLK * BLK, :].rearrange("(p r) d -> p r d", p=P), zb[:, :, :]).then_inc(zeroed, 16)
                    store(LASTB)
                    sp.wait_ge(zeroed, 16 * (NBLK + 1))

                @block.tensor
                def _(pe):
                    def first(b):
                        c = sum(rows_of(b))
                        for m in range(KH):
                            wait(pe, f_set, KH * b + m - 1)
                            for k in range(KD):
                                pe.wait_ge(turn.lo_set, TS * b + k // 2 + 1)
                                last = mm3(HBANK[m % 2][:, 0:c], A1H[:, k, m * P:(m + 1) * P], A1L[:, k, m * P:(m + 1) * P],
                                           XH[:, k, 0:c], XL[:, k, 0:c], k == 0, k == KD - 1)
                            last.then_inc(h_done, 1)

                    def turns(b, j):
                        pe.wait_ge(rst_set, b + 1)
                        turn.pe(pe, TS * b + j, b, RS, (2 * j, 2 * j + 1))

                    def second(b, ks):
                        for k in ks:
                            pe.wait_ge(lo_set, KH * b + k + 1)
                            for r in range(len(rows_of(b))):
                                if k == 0:
                                    wait(pe, y_read, TPB * (b - 1) + r + 1)
                                rows = slice(r * P, (r + 1) * P)
                                last = mm3(YBANK[r][:, :], HH[:, k, rows], HL[:, k, rows], A2H[:, k, :], A2L[:, k, :],
                                           k == 0, k == KH - 1)
                                if k == KH - 1:
                                    last.then_inc(y_done, 1)

                    def body(b):
                        first(b)
                        nxt = b is not LASTB
                        if nxt:
                            turns(b + 1, 0)
                        second(b, range(0, KH // 2))
                        if nxt:
                            turns(b + 1, 1)
                        second(b, range(KH // 2, KH))

                    turns(0, 0)
                    turns(0, 1)
                    body(0)
                    with pe.Fori(1, LASTB - 1) as b:
                        body(b)
                    body(LASTB - 1)
                    body(LASTB)

                @block.scalar
                def _(act):
                    act.wait_ge(cst, 48)

                    def turns(b, j):
                        turn.hi(act, TS * b + j, b, XH, (2 * j, 2 * j + 1))

                    def body(b):
                        c = sum(rows_of(b))
                        for m in range(KH):
                            act.wait_ge(h_done, KH * b + m + 1)
                            wait(act, lo_set, KH * b + m - 1)
                            nc.scalar.activation(HF[:, m % 2, 0:c], HBANK[m % 2][:, 0:c], ACT.Relu, bias=b1c[:, m:m + 1]).then_inc(f_set, 1)
                            act.wait_ge(f_set, KH * b + m + 1)
                            nc.scalar.copy(HH[:, m, 0:c], HF[:, m % 2, 0:c]).then_inc(hi_set, 1)
                        if b is not LASTB:
                            turns(b + 1, 0)
                            turns(b + 1, 1)

                    turns(0, 0)
                    turns(0, 1)
                    body(0)
                    with act.Fori(1, LASTB - 1) as b:
                        body(b)
                    body(LASTB - 1)
                    body(LASTB)

                @block.gpsimd
                def _(pool):
                    nc.gpsimd.memset(zb[:, :, :], 0.0).then_inc(zb_set, 1)
                    pool.wait_ge(cst, 48)

                    def prep(b):
                        nt = len(rows_of(b))
                        pool.wait_ge(yx_in, loaded(b))
                        nc.gpsimd.tensor_tensor(YX[:, 0:nt, :], YX[:, 0:nt, :], YX[:, 0:nt, :], ALU.add).then_inc(x2_set, 1)
                        pool.wait_ge(x2_set, b + 1)
                        for r in range(nt):
                            i = nc.gpsimd.tensor_tensor(YX[:, r, :], YX[:, r, :], b2r[:, :], ALU.add)
                        i.then_inc(yp_set, 1)

                    def body(b):
                        c = sum(rows_of(b))
                        for m in range(KH):
                            pool.wait_ge(hi_set, KH * b + m + 1)
                            nc.gpsimd.tensor_tensor(HL[:, m, 0:c], HF[:, m % 2, 0:c], HH[:, m, 0:c].bitcast(F32), ALU.subtract).then_inc(lo_set, 1)
                        prep(b)
                    blocks(pool, body)

                @block.vector
                def _(dve):
                    norm.blank()
                    dve.wait_ge(cst, 48)
                    nc.vector.tensor_scalar(eps1[:, :], eps1[:, :], 1.0, None, ALU.add).then_inc(e1_set, 1)
                    dve.wait_ge(e1_set, 1)

                    def rst(b):
                        dve.wait_ge(xb_in, loaded(b))
                        dve.wait_ge(rs_in, loaded(b))
                        for n, t0, t1 in spans_of(b):
                            i = nc.vector.scalar_tensor_tensor(RS[0:n, t0:t1, :], XB[0:n, t0:t1, :], eps1[0:n, 0:1], RS[0:n, t0:t1, :], ALU.mult, ALU.add)
                        i.then_inc(rst_set, 1)

                    def turns(b, j):
                        turn.lo(dve, TS * b + j, b, XH, XL, (2 * j, 2 * j + 1))

                    def ys(b):
                        nt = len(rows_of(b))
                        dve.wait_ge(yp_set, b + 1)
                        stats = norm.stats(YX)
                        for r in range(nt):
                            dve.wait_ge(y_done, TPB * b + r + 1)
                            nc.vector.tensor_tensor(YX[:, r, :], YBANK[r][:, :], YX[:, r, :], ALU.add).then_inc(y_read, 1)
                            if r:
                                dve.wait_ge(y_read, TPB * b + r)
                                stats(r - 1)
                        dve.wait_ge(y_read, TPB * b + nt)
                        stats(nt - 1).then_inc(norm.st_set, 1)
                        dve.wait_ge(norm.st_set, b + 1)
                        norm.rstd(dve, b, nt)
                        for r in range(nt):
                            i = nc.vector.tensor_scalar(YX[:, r, :], YX[:, r, :], norm.mv[:, r, 0:1], norm.y[:, r:r + 1], ALU.subtract, ALU.mult)
                        i.then_inc(y_set, 1)

                    rst(0)
                    turns(0, 0)
                    turns(0, 1)

                    def body(b):
                        if b is not 0:
                            ys(b - 1)
                        if b is not LASTB:
                            rst(b + 1)
                            turns(b + 1, 0)
                            turns(b + 1, 1)
                    body(0)
                    with dve.Fori(1, LASTB - 1) as b:
                        body(b)
                    body(LASTB - 1)
                    body(LASTB)
                    ys(LASTB)
        layer0.close()

        with ExitStack() as ph:
            sb, sem = maker(ph)
            UE, U2 = 8, 9
            TS = 5
            XH, XL = [sb("e" + n, [P, 2 * KD, BLK], F32R) for n in ("XH", "XL")]
            ES = sb("ES", [P, BLK], F32R)
            G = [sb(n, [P, TPB, D]) for n in ("GS", "GD")]
            EB = sb("EB", [P, TPB, 2, DE])
            HH, HL = [sb("e" + n, [P, KD, BLK], F32R) for n in ("HH", "HL")]
            MH, ML = [sb(n, [P, TPB, D], F32R) for n in ("MH", "ML")]
            SG = sb("eSG", [P, TPB, D])
            EQ = sb("eEQ", [P, TPB, P], F32R)
            DR = sb("eDR", [P, BLK], I32)
            b1c, b2r = sb("eb1c", [P, KD]), sb("eb2r", [P, D])
            gidx, sidx = sb("egidx", [P, 2, TPB], I32), sb("esidx", [P, TPB], I32)
            hid, msg = Mish(sb, sem, "hid", False), Mish(sb, sem, "msg", True)
            turn = Turn(sem, "t1")
            cst, eb_in, dr_in, gidx_set, sidx_set = [sem("e_" + n) for n in ("cst", "eb_in", "dr_in", "gidx_set", "sidx_set")]
            g_in = [[sem(f"g{j}_in{r}") for r in range(TPB)] for j in range(2)]
            scat = [sem(f"scat1_{r}") for r in range(TPB)]
            w_hi, w_lo = sem("e_w_hi"), sem("e_w_lo")
            bank_free = [sem(f"e_bank{j}_free") for j in range(2)]
            h_done, y_done, s_done, sg_set, eq_set, msg_read = [sem("e_" + n) for n in ("h_done", "y_done", "s_done", "sg_set", "eq_set", "msg_read")]
            CHUNKS = [(0, 3), (3, 6), (6, 9), (9, 13)]

            def hi_(b, m):
                return KD * b + m

            def qi_(b, r):
                return TPB * b + r

            def used(b, j):
                return j if b is 0 else 4 * b - 2 + j

            def turn_src(i):
                return G[i // 2], (2 * (i % 2), 2 * (i % 2) + 1), (2 * i, 2 * i + 1)

            def loop(eng, f):
                f(0)
                f(1)
                f(2)
                with eng.Fori(3, LASTB - 1) as b:
                    f(b)
                for b in range(LASTB - 1, NBLK + 1):
                    f(b)

            def live(b):
                return not isinstance(b, int) or 0 <= b < NBLK

            with nc.Block() as block:
                @block.sync
                def _(sp):
                    with nc.allow_non_contiguous_dma(reason="a bias as a column"):
                        sp.dma_start(b1c[:, :], b1.rearrange("(k p) -> p k", p=P)).then_inc(cst, 16)
                    sp.dma_start(b2r[:, :], b2.partition_broadcast(P)).then_inc(cst, 16)

                    def attrs(b):
                        at = 0
                        for n, t0, t1 in spans_of(b):
                            c = n * (t1 - t0)
                            for j in range(2):
                                sp.dma_start(EB[0:n, t0:t1, j, :], edge_attr[bass.ds(b * BLK + at, c), :].rearrange("(t p) d -> p t d", p=n)).then_inc(eb_in, 16)
                            at += c

                    def body(b):
                        if live(b + 1):
                            wait(sp, turn.done, TS * (b + 1))
                            attrs(b + 1)
                        if live(b):
                            wait(sp, eq_set, TPB * b)
                            n = sum(rows_of(b))
                            sp.dma_start(DR[:, 0:n], dst[bass.ds(b * BLK, n)].partition_broadcast(P)).then_inc(dr_in, 16)
                        if b is 0:
                            sp.wait_ge(w_lo, len(CHUNKS))
                            sp.dma_start(RAW[:, 0:8, :], w3.rearrange("(k p) n -> p k n", p=P)).then_inc(raw2_in, 16)
                            sp.dma_start(RAW[:, 8:12, :], w4.rearrange("(k p) n -> p k n", p=P)).then_inc(raw2_in, 16)
                    attrs(0)
                    loop(sp, body)

                @block.gpsimd
                def _(pool):
                    pool.wait_ge(raw1_in, 64)

                    def stage_idx(b):
                        nt = len(rows_of(b))
                        for j in range(2):
                            for r in range(TPB):
                                wait(pool, g_in[j][r], 16 * b)
                            i = nc.gpsimd.tensor_copy(gidx[:, j, 0:nt], (srcI, dstI)[j][:, bass.ds(b * TPB, nt)])
                        i.then_inc(gidx_set, 1)

                    def gather(b, j, r):
                        rows = rows_of(b)
                        if r >= len(rows):
                            return
                        n = rows[r]
                        if r == 0:
                            wait(pool, turn.done, TS * (b - 1) + 2 * (j + 1))
                            pool.wait_ge(gidx_set, b + 1)
                            settle(pool)
                        nc.gpsimd.indirect_dma_start(G[j][0:n, r, :], None, x1[:, :],
                                                     bass.IndirectOffsetOnAxis(gidx[0:n, j, r:r + 1], 0)).then_inc(g_in[j][r], 16)

                    def scatter(b, r):
                        rows = rows_of(b)
                        if r >= len(rows):
                            return
                        n = rows[r]
                        if r == 0:
                            wait(pool, scat[TPB - 1], 16 * b)
                            nc.gpsimd.tensor_copy(sidx[:, 0:len(rows)], tgt1[:, bass.ds(b * TPB, len(rows))]).then_inc(sidx_set, 1)
                            pool.wait_ge(sidx_set, b + 1)
                        else:
                            pool.wait_ge(scat[r - 1], 16 * (b + 1))
                        pool.wait_ge(sg_set, qi_(b, r) + 1)
                        settle(pool)
                        nc.gpsimd.indirect_dma_start(seg1[:, :], bass.IndirectOffsetOnAxis(sidx[0:n, r:r + 1], 0),
                                                     SG[0:n, r, :], None, compute_op=ALU.add).then_inc(scat[r], 16)

                    def hid_t(b, m):
                        if live(b):
                            hid.t(pool, hi_(b, m), m % 2, sum(rows_of(b)))

                    def hid_lo(b, m):
                        if live(b):
                            c = sum(rows_of(b))
                            hid.lo(pool, hi_(b, m), m % 2, HL[:, m, 0:c], HH[:, m, 0:c], c)

                    def msg_t(b, r):
                        if live(b) and r < len(rows_of(b)):
                            msg.t(pool, qi_(b, r), r % 2, D)

                    def msg_lo(b, r):
                        if live(b) and r < len(rows_of(b)):
                            msg.lo(pool, qi_(b, r), r % 2, ML[:, r, :], MH[:, r, :], D)

                    def body(b):
                        nxt = live(b + 1)
                        if nxt:
                            stage_idx(b + 1)
                        for s in range(TPB):
                            if nxt:
                                gather(b + 1, 0, s)
                            if s:
                                hid_lo(b, s - 1)
                            msg_t(b - 1, s)
                            if live(b - 2):
                                scatter(b - 2, s)
                            if nxt:
                                gather(b + 1, 1, s)
                            hid_t(b, s)
                            msg_lo(b - 1, s)
                        hid_lo(b, TPB - 1)

                    stage_idx(0)
                    for j in range(2):
                        for r in range(TPB):
                            gather(0, j, r)
                    for n, (u0, u1) in enumerate(CHUNKS):
                        if n % 2:
                            pool.wait_ge(w_hi, n + 1)
                            nc.gpsimd.tensor_tensor(WLO[:, u0:u1, :], RAW[:, u0:u1, :], WHI[:, u0:u1, :].bitcast(F32), ALU.subtract).then_inc(w_lo, 1)
                    loop(pool, body)
                    for r in range(TPB):
                        scatter(LASTB, r)
                    for r in range(TPB):
                        pool.wait_ge(scat[r], 16 * (NBLK if r < len(rows_of(LASTB)) else LASTB))

                @block.scalar
                def _(act):
                    act.wait_ge(raw1_in, 64)
                    for u0, u1 in CHUNKS:
                        nc.scalar.copy(WHI[:, u0:u1, :], RAW[:, u0:u1, :]).then_inc(w_hi, 1)

                    def turns(b, i):
                        if live(b):
                            turn.hi(act, TS * b + i, b, XH, turn_src(i)[2])

                    def attr_hi(b):
                        if live(b):
                            c = sum(rows_of(b))
                            act.wait_ge(turn.done, TS * b + TS)
                            nc.scalar.copy(ES[:, 0:c], bank[0][:, 0:c]).then_inc(turn.hi_set, 1)

                    def h_(f, b, m):
                        if live(b):
                            c = sum(rows_of(b))
                            if f == "hi":
                                hid.hi(act, hi_(b, m), m % 2, HH[:, m, 0:c], c)
                            else:
                                (hid.e if f == "e" else hid.r)(act, hi_(b, m), m % 2, c)

                    def q_(f, b, r):
                        if live(b) and r < len(rows_of(b)):
                            if f == "hi":
                                msg.hi(act, qi_(b, r), r % 2, MH[:, r, :], D)
                            else:
                                (msg.e if f == "e" else msg.r)(act, qi_(b, r), r % 2, D)

                    def sums(b, r):
                        if live(b) and r < len(rows_of(b)):
                            act.wait_ge(s_done, qi_(b, r) + 1)
                            wait(act, scat[r], 16 * b)
                            nc.scalar.copy(SG[:, r, :], HBANK[r % 2][:, :]).then_inc(sg_set, 1)
                            act.wait_ge(sg_set, qi_(b, r) + 1)
                            act.sem_inc(bank_free[r % 2], 1)

                    def body(b):
                        for s in range(TPB):
                            q_("e", b - 1, s)
                            if s:
                                h_("r", b, s - 1)
                                q_("hi", b - 1, s - 1)
                            h_("e", b, s)
                            q_("r", b - 1, s)
                            if s:
                                h_("hi", b, s - 1)
                        turns(b + 1, 0)
                        h_("r", b, TPB - 1)
                        q_("hi", b - 1, TPB - 1)
                        turns(b + 1, 1)
                        h_("hi", b, TPB - 1)
                        turns(b + 1, 2)
                        sums(b - 1, 0)
                        sums(b - 1, 1)
                        turns(b + 1, 3)
                        sums(b - 1, 2)
                        sums(b - 1, 3)
                        attr_hi(b + 1)

                    for i in range(TS - 1):
                        turns(0, i)
                    attr_hi(0)
                    loop(act, body)

                @block.vector
                def _(dve):
                    nc.vector.memset(WLO[DE:P, UE, :].bitcast(F32), 0.0)
                    for n, (u0, u1) in enumerate(CHUNKS):
                        if n % 2 == 0:
                            dve.wait_ge(w_hi, n + 1)
                            if u1 == UE + 1:
                                nc.vector.tensor_tensor(WLO[:, u0:UE, :], RAW[:, u0:UE, :], WHI[:, u0:UE, :].bitcast(F32), ALU.subtract)
                                nc.vector.tensor_tensor(WLO[0:DE, UE, :], RAW[0:DE, UE, :], WHI[0:DE, UE, :].bitcast(F32), ALU.subtract).then_inc(w_lo, 1)
                            else:
                                nc.vector.tensor_tensor(WLO[:, u0:u1, :], RAW[:, u0:u1, :], WHI[:, u0:u1, :].bitcast(F32), ALU.subtract).then_inc(w_lo, 1)
                    dve.wait_ge(cst, 32)

                    def turns(b, i):
                        if live(b):
                            turn.lo(dve, TS * b + i, b, XH, XL, turn_src(i)[2])

                    def attr_lo(b):
                        if live(b):
                            c = sum(rows_of(b))
                            dve.wait_ge(turn.hi_set, TS * b + TS)
                            nc.vector.tensor_tensor(ES[DE:P, 0:c], bank[0][DE:P, 0:c], ES[DE:P, 0:c].bitcast(F32), ALU.subtract).then_inc(turn.lo_set, 1)

                    def h_z(b, m):
                        if live(b):
                            c = sum(rows_of(b))
                            dve.wait_ge(h_done, hi_(b, m) + 1)
                            hid.z_col(dve, hi_(b, m), m % 2, HBANK[m % 2][:, 0:c], b1c[:, m:m + 1], c)

                    def h_n(b, m):
                        if live(b):
                            hid.n(dve, hi_(b, m), m % 2, sum(rows_of(b)))

                    def h_m(b, m):
                        if live(b):
                            c = sum(rows_of(b))
                            hid.m_col(dve, hi_(b, m), m % 2, HBANK[m % 2][:, 0:c], b1c[:, m:m + 1], c)
                            dve.wait_ge(hid.m_set, hi_(b, m) + 1)
                            dve.sem_inc(bank_free[m % 2], 1)

                    def q_z(b, r):
                        if live(b) and r < len(rows_of(b)):
                            dve.wait_ge(y_done, qi_(b, r) + 1)
                            msg.z_row(dve, qi_(b, r), r % 2, YBANK[r][:, :], b2r[:, :])

                    def q_n(b, r):
                        if live(b) and r < len(rows_of(b)):
                            msg.n(dve, qi_(b, r), r % 2, D)

                    def q_m(b, r):
                        if live(b) and r < len(rows_of(b)):
                            msg.m_row(dve, qi_(b, r), r % 2)

                    def same(b):
                        if live(b):
                            dve.wait_ge(dr_in, 16 * (b + 1))
                            for r in range(len(rows_of(b))):
                                nc.vector.tensor_scalar(EQ[:, r, :], DR[:, r * P:(r + 1) * P], dstF[:, bass.ds(b * TPB + r, 1)], None, ALU.is_equal).then_inc(eq_set, 1)

                    def body(b):
                        for s in range(TPB):
                            q_z(b - 1, s)
                            if s:
                                h_n(b, s - 1)
                                q_m(b - 1, s - 1)
                            h_z(b, s)
                            q_n(b - 1, s)
                            if s:
                                h_m(b, s - 1)
                        h_n(b, TPB - 1)
                        q_m(b - 1, TPB - 1)
                        turns(b + 1, 0)
                        h_m(b, TPB - 1)
                        same(b - 1)
                        turns(b + 1, 1)
                        turns(b + 1, 2)
                        turns(b + 1, 3)
                        attr_lo(b + 1)

                    for i in range(TS - 1):
                        turns(0, i)
                    attr_lo(0)
                    loop(dve, body)

                @block.tensor
                def _(pe):
                    def turns(b, i):
                        if not live(b):
                            return
                        buf, ks, _ = turn_src(i)
                        if i % 2 == 0:
                            for r in range(len(rows_of(b))):
                                pe.wait_ge(g_in[i // 2][r], 16 * (b + 1))
                        turn.pe(pe, TS * b + i, b, buf, ks)

                    def attr_turn(b):
                        if live(b):
                            pe.wait_ge(eb_in, 2 * loaded(b))
                            wait(pe, turn.lo_set, TS * b + TS - 1)
                            for r, n in enumerate(rows_of(b)):
                                last = nc.tensor.transpose(bank[0][:, r * P:r * P + n], EB[0:n, r, :, :].rearrange("p j d -> p (j d)"), ident[0:n, 0:n])
                            last.then_inc(turn.done, 1)

                    def first(b):
                        if not live(b):
                            return
                        c = sum(rows_of(b))
                        for m in range(KD):
                            cols = slice(m * P, (m + 1) * P)
                            acc = HBANK[m % 2][:, 0:c]
                            wait(pe, bank_free[m % 2], used(b, m // 2))
                            for k in range(2 * KD):
                                if m == 0 and k % 2 == 0:
                                    pe.wait_ge(turn.lo_set, TS * b + k // 2 + 1)
                                mm3(acc, WHI[:, k, cols], WLO[:, k, cols], XH[:, k, 0:c], XL[:, k, 0:c], k == 0, False)
                            if m == 0:
                                pe.wait_ge(turn.lo_set, TS * b + TS)
                            nc.tensor.matmul(acc, WHI[:, UE, cols], ES[:, 0:c], start=False, stop=False)
                            nc.tensor.matmul(acc, WLO[:, UE, cols], ES[:, 0:c], start=False, stop=True).then_inc(h_done, 1)

                    def second(b, k):
                        if not live(b):
                            return
                        pe.wait_ge(hid.lo_set, hi_(b, k) + 1)
                        for r in range(len(rows_of(b))):
                            if k == 0:
                                wait(pe, msg.v_set, qi_(b - 1, r) + 1)
                            rows = slice(r * P, (r + 1) * P)
                            last = mm3(YBANK[r][:, :], HH[:, k, rows], HL[:, k, rows], WHI[:, U2 + k, :], WLO[:, U2 + k, :], k == 0, k == KD - 1)
                            if k == KD - 1:
                                last.then_inc(y_done, 1)

                    def sums(b, r):
                        if live(b) and r < len(rows_of(b)):
                            pe.wait_ge(msg.lo_set, qi_(b, r) + 1)
                            pe.wait_ge(eq_set, qi_(b, r) + 1)
                            wait(pe, bank_free[r % 2], used(b + 1, 2 + r // 2) - (2 if b is LASTB else 0))
                            acc = HBANK[r % 2][:, :]
                            nc.tensor.matmul(acc, EQ[:, r, :], MH[:, r, :], start=True, stop=False)
                            nc.tensor.matmul(acc, EQ[:, r, :], ML[:, r, :], start=False, stop=True).then_inc(s_done, 1)

                    def body(b):
                        first(b)
                        turns(b + 1, 0)
                        second(b, 0)
                        turns(b + 1, 1)
                        second(b, 1)
                        turns(b + 1, 2)
                        second(b, 2)
                        sums(b - 1, 0)
                        sums(b - 1, 1)
                        turns(b + 1, 3)
                        second(b, 3)
                        sums(b - 1, 2)
                        sums(b - 1, 3)
                        attr_turn(b + 1)

                    for i in range(TS - 1):
                        turns(0, i)
                    attr_turn(0)
                    pe.wait_ge(w_lo, len(CHUNKS))
                    loop(pe, body)

        with ExitStack() as ph:
            sb, sem = maker(ph)
            U4 = 8
            TS = 4
            ROWS = [sb(n, [P, TPB, D]) for n in ("NB", "AB")]
            YX, YO = [sb("n" + n, [P, TPB, D]) for n in ("YX", "YO")]
            XH, XL = [sb("n" + n, [P, 2 * KD, BLK], F32R) for n in ("XH", "XL")]
            HH, HL = [sb("n" + n, [P, KD, BLK], F32R) for n in ("HH", "HL")]
            b3c, b4r, gam, bet = sb("b3c", [P, KD]), sb("b4r", [P, D]), sb("gam", [P, D]), sb("bet", [P, D])
            hid = Mish(sb, sem, "nhid", False)
            norm, norm2 = Norm(sb, sem, "n1"), Norm(sb, sem, "n2")
            turn = Turn(sem, "t2")
            cst, yx_in, y_out = [sem("n_" + n) for n in ("cst", "yx_in", "y_out")]
            rows_in = [sem(f"n_rows{j}_in") for j in range(2)]
            w_hi, w_lo = sem("n_w_hi"), sem("n_w_lo")
            h_done, y_done, y_read, yo_set, yx_set, y_set, g_set, s_set, hm_read = [
                sem("n_" + n) for n in ("h_done", "y_done", "y_read", "yo_set", "yx_set", "y_set", "g_set", "s_set", "hm_read")]
            CHUNKS = [(0, 3), (3, 6), (6, 9), (9, 12)]

            def hi_(b, m):
                return KD * b + m

            def turn_src(i):
                return ROWS[i // 2], (2 * (i % 2), 2 * (i % 2) + 1), (2 * i, 2 * i + 1)

            def loop(eng, f):
                f(0)
                with eng.Fori(1, LASTB - 1) as b:
                    f(b)
                for b in range(LASTB - 1, NBLK + 1):
                    f(b)

            def live(b):
                return not isinstance(b, int) or 0 <= b < NBLK

            with nc.Block() as block:
                @block.sync
                def _(sp):
                    with nc.allow_non_contiguous_dma(reason="a bias as a column"):
                        sp.dma_start(b3c[:, :], b3.rearrange("(k p) -> p k", p=P)).then_inc(cst, 16)
                    for row, a in ((b4r, b4), (gam, gamma), (bet, beta)):
                        sp.dma_start(row[:, :], a.partition_broadcast(P)).then_inc(cst, 16)

                    def load(b):
                        for j, a in enumerate((x1, seg1)):
                            wait(sp, turn.done, TS * (b - 1) + 2 * (j + 1) if b is not 0 else 0)
                            load_rows(sp, ROWS[j], a, b, rows_in[j])

                    def body(b):
                        if live(b + 1):
                            load(b + 1)
                        if live(b - 1):
                            sp.wait_ge(y_set, b)
                            store_rows(sp, YO, out, b - 1, y_out)
                            if live(b):
                                load_rows(sp, YX, x1, b, yx_in)
                    load(0)
                    load_rows(sp, YX, x1, 0, yx_in)
                    loop(sp, body)
                    sp.wait_ge(y_out, loaded(LASTB))

                @block.gpsimd
                def _(pool):
                    for n, (u0, u1) in enumerate(CHUNKS):
                        if n % 2:
                            pool.wait_ge(w_hi, n + 1)
                            nc.gpsimd.tensor_tensor(WLO[:, u0:u1, :], RAW[:, u0:u1, :], WHI[:, u0:u1, :].bitcast(F32), ALU.subtract).then_inc(w_lo, 1)
                    pool.wait_ge(cst, 64)

                    def prep(b):
                        nt = len(rows_of(b))
                        pool.wait_ge(yx_in, loaded(b))
                        wait(pool, y_out, 16 * b)
                        for r in range(nt):
                            i = nc.gpsimd.tensor_tensor(YO[:, r, :], YX[:, r, :], b4r[:, :], ALU.add)
                        i.then_inc(yo_set, 1)
                        pool.wait_ge(yo_set, b + 1)
                        for r in range(nt):
                            i = nc.gpsimd.tensor_tensor(YX[:, r, :], YX[:, r, :], bet[:, :], ALU.add)
                        i.then_inc(yx_set, 1)

                    def body(b):
                        if not live(b):
                            return
                        c = sum(rows_of(b))
                        for s in range(KD):
                            hid.t(pool, hi_(b, s), s % 2, c)
                            hid.lo(pool, hi_(b, s), s % 2, HL[:, s, 0:c], HH[:, s, 0:c], c)
                        prep(b)
                    loop(pool, body)

                @block.scalar
                def _(act):
                    act.wait_ge(raw2_in, 32)
                    for u0, u1 in CHUNKS:
                        nc.scalar.copy(WHI[:, u0:u1, :], RAW[:, u0:u1, :]).then_inc(w_hi, 1)

                    def turns(b, i):
                        if live(b):
                            turn.hi(act, TS * b + i, b, XH, turn_src(i)[2])

                    def body(b):
                        if not live(b):
                            return
                        c = sum(rows_of(b))
                        for s in range(KD):
                            hid.e(act, hi_(b, s), s % 2, c)
                            hid.r(act, hi_(b, s), s % 2, c)
                            if s == KD - 1:
                                turns(b + 1, 0)
                            hid.hi(act, hi_(b, s), s % 2, HH[:, s, 0:c], c)
                        for i in range(1, TS):
                            turns(b + 1, i)

                    for i in range(TS):
                        turns(0, i)
                    loop(act, body)

                @block.vector
                def _(dve):
                    norm.blank()
                    norm2.blank()
                    for n, (u0, u1) in enumerate(CHUNKS):
                        if n % 2 == 0:
                            dve.wait_ge(w_hi, n + 1)
                            nc.vector.tensor_tensor(WLO[:, u0:u1, :], RAW[:, u0:u1, :], WHI[:, u0:u1, :].bitcast(F32), ALU.subtract).then_inc(w_lo, 1)
                    dve.wait_ge(cst, 64)

                    def turns(b, i):
                        if live(b):
                            turn.lo(dve, TS * b + i, b, XH, XL, turn_src(i)[2])

                    def y_tile(b, r):
                        if live(b) and r < len(rows_of(b)):
                            if r == 0:
                                dve.wait_ge(yx_set, b + 1)
                            dve.wait_ge(y_done, TPB * b + r + 1)
                            nc.vector.tensor_tensor(YO[:, r, :], YBANK[r][:, :], YO[:, r, :], ALU.add).then_inc(y_read, 1)
                            dve.wait_ge(y_read, TPB * b + r + 1)
                            nc.vector.bn_stats(norm.st[:, r, :], YO[:, r, :]).then_inc(norm.st_set, 1)

                    def finish(b):
                        if not live(b):
                            return
                        nt = len(rows_of(b))
                        dve.wait_ge(norm.st_set, TPB * b + nt)
                        norm.rstd(dve, b, nt)
                        for r in range(nt):
                            i = nc.vector.scalar_tensor_tensor(YO[:, r, :], YO[:, r, :], norm.mv[:, r, 0:1], gam[:, :], ALU.subtract, ALU.mult)
                        i.then_inc(g_set, 1)
                        dve.wait_ge(g_set, b + 1)
                        for r in range(nt):
                            i = nc.vector.scalar_tensor_tensor(YO[:, r, :], YO[:, r, :], norm.y[:, r:r + 1], YX[:, r, :], ALU.mult, ALU.add)
                        i.then_inc(s_set, 1)
                        dve.wait_ge(s_set, b + 1)
                        for r in range(nt):
                            i = nc.vector.bn_stats(norm2.st[:, r, :], YO[:, r, :])
                        i.then_inc(norm2.st_set, 1)
                        dve.wait_ge(norm2.st_set, b + 1)
                        norm2.rstd(dve, b, nt)
                        for r in range(nt):
                            i = nc.vector.tensor_scalar(YO[:, r, :], YO[:, r, :], norm2.mv[:, r, 0:1], norm2.y[:, r:r + 1], ALU.subtract, ALU.mult)
                        i.then_inc(y_set, 1)

                    def body(b):
                        c = sum(rows_of(b)) if live(b) else 0
                        for s in range(KD):
                            y_tile(b - 1, s)
                            if live(b):
                                dve.wait_ge(h_done, hi_(b, s) + 1)
                                hid.z_col(dve, hi_(b, s), s % 2, HBANK[s % 2][:, 0:c], b3c[:, s:s + 1], c)
                                hid.n(dve, hi_(b, s), s % 2, c)
                                if s == KD - 1:
                                    turns(b + 1, 0)
                                hid.m_col(dve, hi_(b, s), s % 2, HBANK[s % 2][:, 0:c], b3c[:, s:s + 1], c)
                        for i in range(1, TS):
                            turns(b + 1, i)
                        finish(b - 1)

                    for i in range(TS):
                        turns(0, i)
                    loop(dve, body)

                @block.tensor
                def _(pe):
                    def turns(b, i):
                        if live(b):
                            buf, ks, _ = turn_src(i)
                            pe.wait_ge(rows_in[i // 2], loaded(b))
                            turn.pe(pe, TS * b + i, b, buf, ks)

                    def body(b):
                        if not live(b):
                            return
                        c = sum(rows_of(b))
                        for m in range(KD):
                            cols = slice(m * P, (m + 1) * P)
                            wait(pe, hid.m_set, hi_(b, m) - 1)
                            for k in range(2 * KD):
                                if m == 0 and k % 2 == 0:
                                    pe.wait_ge(turn.lo_set, TS * b + k // 2 + 1)
                                last = mm3(HBANK[m % 2][:, 0:c], WHI[:, k, cols], WLO[:, k, cols], XH[:, k, 0:c], XL[:, k, 0:c], k == 0, k == 2 * KD - 1)
                            last.then_inc(h_done, 1)
                        for k in range(KD):
                            turns(b + 1, k)
                            pe.wait_ge(hid.lo_set, hi_(b, k) + 1)
                            for r in range(len(rows_of(b))):
                                if k == 0:
                                    wait(pe, y_read, TPB * (b - 1) + r + 1)
                                rows = slice(r * P, (r + 1) * P)
                                last = mm3(YBANK[r][:, :], HH[:, k, rows], HL[:, k, rows], WHI[:, U4 + k, :], WLO[:, U4 + k, :], k == 0, k == KD - 1)
                                if k == KD - 1:
                                    last.then_inc(y_done, 1)

                    for i in range(TS):
                        turns(0, i)
                    pe.wait_ge(w_lo, len(CHUNKS))
                    loop(pe, body)


_INS = ['x', 'src', 'dst', 'edge_attr_64', 'L0_gnn_W1', 'L0_gnn_b1', 'L0_gnn_W2', 'L0_gnn_b2', 'L0_gnn_eps',
        'L1_gnn_W1', 'L1_gnn_b1', 'L1_gnn_W2', 'L1_gnn_b2', 'L1_gnn_W3', 'L1_gnn_b3', 'L1_gnn_W4', 'L1_gnn_b4',
        'L1_gnn_gamma', 'L1_gnn_beta']
_OUTS = [((N, D), 'float32')]


def kernel(**inputs):
    import numpy as _np
    import concourse.bacc as _bacc
    from concourse import mybir as _mybir
    from concourse.bass_utils import run_bass_kernel_spmd as _run

    nc = _bacc.Bacc("TRN2", target_bir_lowering=False, num_devices=1)
    arrays, args = {}, []
    for name in _INS:
        a = _np.ascontiguousarray(inputs[name])
        arrays[f"in_{name}_dram"] = a
        args.append(nc.dram_tensor(f"in_{name}_dram", a.shape, _mybir.dt.from_np(a.dtype), kind="ExternalInput").ap())
    for i, (shape, dtype) in enumerate(_OUTS):
        dt = _mybir.dt.from_np(_np.dtype(dtype))
        args.append(nc.dram_tensor(f"out_{i}_dram", shape, dt, kind="ExternalOutput").ap())
    gnn_resnorm_kernel(nc, *args)
    r = _run(nc, [arrays], core_ids=[0])
    got = tuple(r.results[0][f"out_{i}_dram"] for i in range(len(_OUTS)))
    return got[0]
```

```python
import concourse.bass as bass
from concourse import mybir
from contextlib import ExitStack

F32 = mybir.dt.float32
F32R = mybir.dt.float32r
I32 = mybir.dt.int32
ALU = mybir.AluOpType
ACT = mybir.ActivationFunctionType
AX = mybir.AxisListType

P = 128
D = 512
DH = 1024
DE = 64
N = 10000
TPB = 4
BLK = TPB * P
NBLK = -(-N // BLK)
LASTB = NBLK - 1
LASTROWS = N - LASTB * BLK
NT = -(-N // P)
LN_EPS = 1e-5
ZCAP = 20.0
SEGROWS = (NBLK + 1) * BLK
KD = D // P
KH = DH // P
RSQRT_STEPS = 4


def rows_of(b):
    if isinstance(b, int) and b == LASTB:
        left, out = LASTROWS, []
        while left > 0:
            out.append(min(left, P))
            left -= P
        return out
    return [P] * TPB


def spans_of(b):
    rows = rows_of(b)
    full = sum(r == P for r in rows)
    spans = [(P, 0, full)]
    if full < len(rows):
        spans.append((rows[-1], full, len(rows)))
    return spans


def blocks(eng, f, first=1, end=LASTB):
    for b in range(first):
        f(b)
    with eng.Fori(first, end) as b:
        f(b)
    for b in range(end, NBLK):
        f(b)


def wait(eng, sem, value):
    if not isinstance(value, int) or value > 0:
        eng.wait_ge(sem, value)


def ndma(b):
    return len(spans_of(b))


def gnn_resnorm_kernel(nc, x, src, dst, edge_attr, w1a, b1a, w2a, b2a, eps, w1, b1, w2, b2,
                       w3, b3, w4, b4, gamma, beta, out):
    seg0 = nc.dram_tensor("seg0", (SEGROWS, D), F32, kind="Internal").ap()
    seg1 = nc.dram_tensor("seg1", (SEGROWS, D), F32, kind="Internal").ap()
    x1 = nc.dram_tensor("x1", (N, D), F32, kind="Internal").ap()

    ctx = ExitStack()
    with ctx:
        def maker(stack):
            def sb(name, shape, dt=F32):
                return stack.enter_context(nc.sbuf_tensor(name, shape, dt))

            def sem(name):
                return stack.enter_context(nc.semaphore(name))
            return sb, sem

        sb, sem = maker(ctx)
        WELEMS = 2 * (8 + 4) * D + 2 * D
        W = sb("W", [P, WELEMS], F32R)
        RAWK = 13
        RAW = sb("RAW", [P, RAWK, D])
        ident = sb("ident", [P, P])
        dstF = sb("dstF", [P, NT + 1])
        srcI = sb("srcI", [P, NT + 1], I32)
        dstI = sb("dstI", [P, NT + 1], I32)
        tgt0 = sb("tgt0", [P, NT + 1], I32)
        tgt1 = sb("tgt1", [P, NT + 1], I32)
        bank = [ctx.enter_context(nc.psum_tensor(f"bank{i}", [P, 512], F32)) for i in range(8)]

        two = sb("two", [P, 1])
        ticks = sem("ticks")

        def settle(eng):
            eng.sem_inc(ticks, 1)

        raw1_in, raw2_in = sem("raw1_in"), sem("raw2_in")

        with ExitStack() as ph:
            sb, sem = maker(ph)
            ii = sb("ii", [P, 2, P], I32)
            iF = sb("iF", [P, 2, P])
            idx_blank, idx_in, idx_f, idx_t, idx_done = [sem(f"idx{i}") for i in range(5)]
            id_blank, id_set = sem("id_blank"), sem("id_set")
            with nc.Block() as block:
                @block.sync
                def _(sp):
                    full = N // P
                    sp.wait_ge(idx_blank, 1)
                    for j, a in enumerate((src, dst)):
                        sp.dma_start(ii[0:full, j, :], a[0:full * P].rearrange("(t p) -> t p", p=P)).then_inc(idx_in, 16)
                        sp.dma_start(ii[full:full + 1, j, 0:N - full * P], a[full * P:N].rearrange("(t p) -> t p", t=1)).then_inc(idx_in, 16)

                @block.gpsimd
                def _(pool):
                    nc.gpsimd.memset(ident[:, :], 0.0).then_inc(id_blank, 1)
                    pool.wait_ge(id_blank, 1)
                    nc.gpsimd.affine_select(out=ident[:, :], in_=ident[:, :], compare_op=ALU.not_equal, fill=1.0,
                                            base=0, pattern=[[-1, P]], channel_multiplier=1).then_inc(id_set, 1)

                @block.vector
                def _(dve):
                    nc.vector.memset(ii[:, :, :], -1).then_inc(idx_blank, 1)
                    nc.vector.memset(two[:, :], 2.0)
                    dve.wait_ge(idx_in, 64)
                    nc.vector.tensor_copy(iF[:, :, :], ii[:, :, :]).then_inc(idx_f, 1)
                    dve.wait_ge(idx_t, 1)
                    nc.vector.tensor_copy(dstF[:, :], bank[1][:, 0:NT + 1])
                    nc.vector.tensor_copy(dstI[:, :], bank[1][:, 0:NT + 1])
                    nc.vector.tensor_copy(srcI[:, :], bank[0][:, 0:NT + 1]).then_inc(idx_done, 1)

                @block.tensor
                def _(pe):
                    pe.wait_ge(idx_f, 1)
                    pe.wait_ge(id_set, 1)
                    nc.tensor.transpose(bank[0][:, 0:P], iF[:, 0, :], ident[:, :])
                    nc.tensor.transpose(bank[1][:, 0:P], iF[:, 1, :], ident[:, :]).then_inc(idx_t, 1)

        UNITS = 13
        WHI = W[:, 0:UNITS * D].rearrange("p (u n) -> p u n", n=D)
        WLO = W[:, UNITS * D:2 * UNITS * D].rearrange("p (u n) -> p u n", n=D)

        layer0 = ctx.enter_context(ExitStack())
        WX = layer0.enter_context(nc.sbuf_tensor("WX", [P, 8, D], F32R))
        A1H, A1L = W[:, 0:8 * D].rearrange("p (k n) -> p k n", n=DH), W[:, 8 * D:16 * D].rearrange("p (k n) -> p k n", n=DH)
        A2H, A2L = W[:, 16 * D:24 * D].rearrange("p (k n) -> p k n", n=D), WX[:, :, :]

        with ExitStack() as ph:
            sb, sem = maker(ph)
            zero = sb("zero", [P, TPB, D])
            XG = sb("XG", [P, TPB, D])
            GH = sb("GH", [P, TPB, D], F32R)
            GL = sb("GL", [P, TPB, D], F32R)
            EQ = sb("EQ", [P, TPB, BLK], F32R)
            earlier = sb("earlier", [P, TPB, BLK])
            TM = sb("TM", [P, TPB, BLK])
            DR = sb("DR", [P, BLK], I32)
            SG = sb("SG", [P, TPB, D])
            dup = sb("dup", [P, 2, TPB])
            keep = sb("keep", [P, 2, TPB])
            spare = sb("spare", [P, TPB])
            off = sb("off", [P, 2, TPB])
            move = sb("move", [P, 2, TPB])
            gidx = sb("gidx", [P, TPB], I32)
            sidx = sb("sidx", [P, TPB], I32)
            zero_set, zeroed, spare_set, mask_blank, mask_set = [sem(n) for n in ("zero_set", "zeroed", "spare_set", "mask_blank", "mask_set")]
            dr_in, gidx_set, sidx_set = sem("dr_in"), sem("gidx_set"), sem("sidx_set")
            xg_in = [sem(f"xg_in{r}") for r in range(TPB)]
            gh_set, gl_set, eq_set, tm_set, dup_set, keep_set, off_set, move_set, tgt_set = [
                sem(n) for n in ("gh_set", "gl_set", "eq_set", "tm_set", "dup_set", "keep_set", "off_set", "move_set", "tgt_set")]
            sum_done, sg_set = sem("sum_done"), sem("sg_set")
            w0_in, w0_hi, w0_lo = sem("w0_in"), sem("w0_hi"), sem("w0_lo")
            w0 = [(RAW[:, 0:8, :].rearrange("p (k h) n -> p k (h n)", h=2), A1H, A1L), (RAW[:, 0:8, :], A2H, A2L)]
            scat = [sem(f"scat0_{r}") for r in range(TPB)]

            with nc.Block() as block:
                @block.sync
                def _(sp):
                    r1, r2 = RAW[:, 0:8, :].rearrange("p (k h) n -> p k (h n)", h=2), RAW[:, 0:8, :]
                    sp.dma_start(r1, w1a.rearrange("(k p) n -> p k n", p=P)).then_inc(w0_in, 16)
                    sp.wait_ge(w0_lo, 1)
                    sp.dma_start(r2, w2a.rearrange("(k p) n -> p k n", p=P)).then_inc(w0_in, 16)
                    sp.wait_ge(zero_set, 1)
                    for c in range(SEGROWS // BLK):
                        sp.dma_start(seg0[c * BLK:(c + 1) * BLK, :].rearrange("(p r) d -> p r d", p=P), zero[:, :, :]).then_inc(zeroed, 16)

                    def load(b):
                        n = sum(rows_of(b))
                        wait(sp, eq_set, TPB * b)
                        sp.dma_start(DR[:, 0:n], dst[bass.ds(b * BLK, n)].partition_broadcast(P)).then_inc(dr_in, 16)
                    blocks(sp, load)

                @block.gpsimd
                def _(pool):
                    nc.gpsimd.memset(zero[:, :, :], 0.0).then_inc(zero_set, 1)
                    nc.gpsimd.iota(spare[:, :], pattern=[[P, TPB]], base=N, channel_multiplier=1,
                                   allow_small_or_imprecise_dtypes=True).then_inc(spare_set, 1)
                    nc.gpsimd.memset(earlier[:, :, :], 1.0).then_inc(mask_blank, 1)
                    pool.wait_ge(mask_blank, 1)
                    nc.gpsimd.affine_select(out=earlier[:, :, :], in_=earlier[:, :, :], compare_op=ALU.is_gt, fill=0.0,
                                            base=0, pattern=[[P, TPB], [-1, BLK]], channel_multiplier=1).then_inc(mask_set, 1)

                    def gather(b):
                        rows = rows_of(b)
                        for r in range(TPB):
                            wait(pool, xg_in[r], 16 * b)
                        wait(pool, gl_set, b)
                        nt = len(rows)
                        nc.gpsimd.tensor_copy(gidx[:, 0:nt], srcI[:, bass.ds(b * TPB, nt)]).then_inc(gidx_set, 1)
                        pool.wait_ge(gidx_set, b + 1)
                        settle(pool)
                        for r, n in enumerate(rows):
                            nc.gpsimd.indirect_dma_start(XG[0:n, r, :], None, x[:, :],
                                                         bass.IndirectOffsetOnAxis(gidx[0:n, r:r + 1], 0)).then_inc(xg_in[r], 16)

                    def scatter(b):
                        rows = rows_of(b)
                        nt = len(rows)
                        for r in range(TPB):
                            wait(pool, scat[r], 16 * b)
                        pool.wait_ge(tgt_set, b + 1)
                        nc.gpsimd.tensor_copy(sidx[:, 0:nt], tgt0[:, bass.ds(b * TPB, nt)]).then_inc(sidx_set, 1)
                        pool.wait_ge(sidx_set, b + 1)
                        for r, n in enumerate(rows):
                            pool.wait_ge(sg_set, TPB * b + r + 1)
                            settle(pool)
                            nc.gpsimd.indirect_dma_start(seg0[:, :], bass.IndirectOffsetOnAxis(sidx[0:n, r:r + 1], 0),
                                                         SG[0:n, r, :], None, compute_op=ALU.add).then_inc(scat[r], 16)

                    gather(0)
                    pool.wait_ge(zeroed, 16 * (SEGROWS // BLK))
                    gather(1)
                    scatter(0)
                    with pool.Fori(1, LASTB - 1) as b:
                        gather(b + 1)
                        scatter(b)
                    gather(LASTB)
                    scatter(LASTB - 1)
                    scatter(LASTB)
                    for r in range(TPB):
                        pool.wait_ge(scat[r], 16 * (NBLK if r < len(rows_of(LASTB)) else LASTB))

                @block.scalar
                def _(act):
                    for j, (raw, hi, lo) in enumerate(w0):
                        act.wait_ge(w0_in, 16 * (j + 1))
                        nc.scalar.copy(hi, raw).then_inc(w0_hi, 1)

                    def f(b):
                        nt = len(rows_of(b))
                        for r in range(nt):
                            act.wait_ge(xg_in[r], 16 * b + 16)
                        wait(act, sum_done, TPB * b)
                        nc.scalar.copy(GH[:, 0:nt, :], XG[:, 0:nt, :]).then_inc(gh_set, 1)
                        for r in range(nt):
                            act.wait_ge(sum_done, TPB * b + r + 1)
                            wait(act, scat[r], 16 * b)
                            nc.scalar.copy(SG[:, r, :], bank[r][:, :]).then_inc(sg_set, 1)
                    blocks(act, f)

                @block.vector
                def _(dve):
                    for j, (raw, hi, lo) in enumerate(w0):
                        dve.wait_ge(w0_hi, j + 1)
                        nc.vector.tensor_tensor(lo, raw, hi.bitcast(F32), ALU.subtract).then_inc(w0_lo, 1)
                    dve.wait_ge(mask_set, 1)
                    dve.wait_ge(spare_set, 1)

                    def f(b):
                        nt = len(rows_of(b))
                        dve.wait_ge(gh_set, b + 1)
                        nc.vector.tensor_tensor(GL[:, 0:nt, :], XG[:, 0:nt, :], GH[:, 0:nt, :].bitcast(F32), ALU.subtract).then_inc(gl_set, 1)
                        dve.wait_ge(dr_in, 16 * b + 16)
                        for t in range(TPB):
                            if t < nt:
                                nc.vector.tensor_scalar(EQ[:, t, :], DR[:, :], dstF[:, bass.ds(b * TPB + t, 1)], None, ALU.is_equal).then_inc(eq_set, 1)
                        dve.wait_ge(eq_set, TPB * b + nt)
                        nc.vector.tensor_tensor(TM[:, 0:nt, :], EQ[:, 0:nt, :].bitcast(F32), earlier[:, 0:nt, :], ALU.mult).then_inc(tm_set, 1)
                        dve.wait_ge(tm_set, b + 1)
                        for t in range(nt):
                            nc.vector.tensor_reduce(dup[:, 1, t:t + 1], TM[:, t, t * P:(t + 1) * P], AX.X, ALU.max)
                        nc.vector.tensor_reduce(dup[:, 0, 0:nt], TM[:, 0:nt, :], AX.X, ALU.max).then_inc(dup_set, 1)
                        dve.wait_ge(dup_set, b + 1)
                        for w in range(2):
                            nc.vector.tensor_tensor(off[:, w, 0:nt], spare[:, 0:nt], dstF[:, bass.ds(b * TPB, nt)], ALU.subtract).then_inc(off_set, 1)
                        dve.wait_ge(off_set, 2 * b + 2)
                        nc.vector.tensor_tensor(move[:, :, 0:nt], off[:, :, 0:nt], dup[:, :, 0:nt], ALU.mult).then_inc(move_set, 1)
                        dve.wait_ge(move_set, b + 1)
                        for w, tgt in enumerate((tgt0, tgt1)):
                            last = nc.vector.tensor_tensor(tgt[:, bass.ds(b * TPB, nt)], move[:, w, 0:nt], dstF[:, bass.ds(b * TPB, nt)], ALU.add)
                        last.then_inc(tgt_set, 1)
                    blocks(dve, f)

                @block.tensor
                def _(pe):
                    def f(b):
                        nt = len(rows_of(b))
                        pe.wait_ge(gl_set, b + 1)
                        pe.wait_ge(eq_set, TPB * b + nt)
                        for a in range(nt):
                            wait(pe, sg_set, TPB * (b - 1) + a + 1)
                            for t in range(nt):
                                nc.tensor.matmul(bank[a][:, :], EQ[:, t, a * P:(a + 1) * P], GH[:, t, :], start=t == 0, stop=False)
                                last = nc.tensor.matmul(bank[a][:, :], EQ[:, t, a * P:(a + 1) * P], GL[:, t, :], start=False, stop=t == nt - 1)
                            last.then_inc(sum_done, 1)
                    blocks(pe, f)


        def mm3(acc, ah, al, bh, bl, start, stop):
            nc.tensor.matmul(acc, ah, bh, start=start, stop=False)
            nc.tensor.matmul(acc, ah, bl, start=False, stop=False)
            return nc.tensor.matmul(acc, al, bh, start=False, stop=stop)

        class Norm:
            LINKS = 4 + 3 * RSQRT_STEPS

            def __init__(self, sb, sem, name):
                self.st = sb(name + "_st", [P, TPB, 6])
                self.mv = sb(name + "_mv", [P, TPB, 2])
                self.h, self.y, self.t, self.a = [sb(name + "_" + c, [P, TPB]) for c in "hyta"]
                self.nm = sb(name + "_nm", [P, TPB])
                self.st_set, self.link, self.set = sem(name + "_st_set"), sem(name + "_link"), sem(name + "_set")

            def blank(self):
                nc.vector.memset(self.mv[:, :, :], 1.0)

            def stats(self, rows):
                self.rows = rows
                return lambda r: nc.vector.bn_stats(self.st[:, r, :], rows[:, r, :])

            def rstd(self, dve, n, nt):
                settle(dve)
                for r in range(nt):
                    last = nc.vector.bn_aggr(self.mv[:, r, :], self.st[:, r, :])
                at = [self.LINKS * n]

                def link(i):
                    at[0] += 1
                    i.then_inc(self.link, 1)
                    dve.wait_ge(self.link, at[0])
                link(last)
                link(nc.vector.tensor_scalar(self.a[:, :], self.mv[:, :, 1], LN_EPS, None, ALU.add))
                nc.vector.tensor_scalar(self.h[:, :], self.a[:, :], -0.5, None, ALU.mult)
                link(nc.vector.tensor_scalar(self.t[:, :].bitcast(I32), self.a[:, :].bitcast(I32), 1, None, ALU.logical_shift_right))
                link(nc.vector.tensor_scalar(self.y[:, :].bitcast(I32), self.t[:, :].bitcast(I32), -1.0, float(0x5f3759df), ALU.mult, ALU.add))
                for _ in range(RSQRT_STEPS):
                    link(nc.vector.tensor_tensor(self.t[:, :], self.y[:, :], self.y[:, :], ALU.mult))
                    link(nc.vector.tensor_tensor(self.t[:, :], self.t[:, :], self.h[:, :], ALU.mult))
                    link(nc.vector.scalar_tensor_tensor(self.y[:, :], self.t[:, :], 1.5, self.y[:, :], ALU.add, ALU.mult))
                nc.vector.scalar_tensor_tensor(self.nm[:, :], self.mv[:, :, 0], -1.0, self.y[:, :], ALU.mult, ALU.mult).then_inc(self.set, 1)

        class Mish:

            def __init__(self, sb, sem, name, V=None):
                self.V = V if V is not None else sb(name + "V", [P, 2, D])
                self.Z, self.N, self.R = [sb(name + c, [P, 2, D]) for c in "ZNR"]
                (self.v_set, self.z_set, self.e_set, self.n_set, self.l_set, self.r_set, self.t_set, self.m_set, self.hi_set,
                 self.lo_set) = [sem(f"{name}_{c}_set") for c in ("v", "z", "e", "n", "l", "r", "t", "m", "hi", "lo")]

            def cap(self, dve, i, s, c):
                dve.wait_ge(self.v_set, i + 1)
                nc.vector.tensor_scalar(self.Z[:, s, 0:c], self.V[:, s, 0:c], ZCAP, None, ALU.min).then_inc(self.z_set, 1)

            def z_col(self, dve, i, s, ps, bias, c):
                wait(dve, self.lo_set, i - 1)
                nc.vector.tensor_scalar(self.V[:, s, 0:c], ps, bias, None, ALU.add).then_inc(self.v_set, 1)
                self.cap(dve, i, s, c)

            def z_row(self, dve, i, s, ps, bias):
                wait(dve, self.lo_set, i - 1)
                nc.vector.tensor_tensor(self.V[:, s, :], ps, bias, ALU.add).then_inc(self.v_set, 1)
                self.cap(dve, i, s, D)

            def e(self, act, i, s, c):
                act.wait_ge(self.z_set, i + 1)
                nc.scalar.activation(self.Z[:, s, 0:c], self.Z[:, s, 0:c], ACT.Exp).then_inc(self.e_set, 1)

            def n(self, dve, i, s, c):
                dve.wait_ge(self.e_set, i + 1)
                z = self.Z[:, s, 0:c]
                nc.vector.scalar_tensor_tensor(self.N[:, s, 0:c], z, 2.0, z, ALU.add, ALU.mult).then_inc(self.n_set, 1)

            def r(self, act, i, s, c):
                act.wait_ge(self.n_set, i + 1)
                nc.scalar.activation(self.R[:, s, 0:c], self.N[:, s, 0:c], ACT.Ln, bias=two[:, 0:1]).then_inc(self.l_set, 1)
                act.wait_ge(self.l_set, i + 1)
                nc.scalar.activation(self.R[:, s, 0:c], self.R[:, s, 0:c], ACT.Exp, scale=-1.0).then_inc(self.r_set, 1)

            def t(self, pool, i, s, c):
                pool.wait_ge(self.r_set, i + 1)
                nc.gpsimd.tensor_tensor(self.N[:, s, 0:c], self.N[:, s, 0:c], self.R[:, s, 0:c], ALU.mult).then_inc(self.t_set, 1)

            def m(self, dve, i, s, c):
                dve.wait_ge(self.t_set, i + 1)
                nc.vector.tensor_tensor(self.Z[:, s, 0:c], self.V[:, s, 0:c], self.N[:, s, 0:c], ALU.mult).then_inc(self.m_set, 1)

            def hi(self, act, i, s, out, c):
                act.wait_ge(self.m_set, i + 1)
                nc.scalar.copy(out, self.Z[:, s, 0:c]).then_inc(self.hi_set, 1)

            def lo(self, eng, i, s, out, hi, c):
                eng.wait_ge(self.hi_set, i + 1)
                eng.tensor_tensor(out, self.Z[:, s, 0:c], hi.bitcast(F32), ALU.subtract).then_inc(self.lo_set, 1)

        class Turn:

            def __init__(self, sem, name):
                self.done, self.hi_set, self.lo_set = sem(name + "_done"), sem(name + "_hi"), sem(name + "_lo")

            def pe(self, pe, i, b, rows_buf, ks):
                wait(pe, self.lo_set, i)
                for j, k in enumerate(ks):
                    for r, n in enumerate(rows_of(b)):
                        last = nc.tensor.transpose(bank[j][:, r * P:r * P + n], rows_buf[0:n, r, k * P:(k + 1) * P], ident[0:n, 0:n])
                last.then_inc(self.done, 1)

            def hi(self, act, i, b, XH, ks):
                c = sum(rows_of(b))
                act.wait_ge(self.done, i + 1)
                for j, k in enumerate(ks):
                    last = nc.scalar.copy(XH[:, k, 0:c], bank[j][:, 0:c])
                last.then_inc(self.hi_set, 1)

            def lo(self, dve, i, b, XH, XL, ks):
                c = sum(rows_of(b))
                dve.wait_ge(self.hi_set, i + 1)
                for j, k in enumerate(ks):
                    last = nc.vector.tensor_tensor(XL[:, k, 0:c], bank[j][:, 0:c], XH[:, k, 0:c].bitcast(F32), ALU.subtract)
                last.then_inc(self.lo_set, 1)

        HBANK, YBANK = [bank[2], bank[3]], bank[4:8]

        def load_rows(eng, buf, dram, b, sem_):
            at = 0
            for n, t0, t1 in spans_of(b):
                c = n * (t1 - t0)
                eng.dma_start(buf[0:n, t0:t1, :], dram[bass.ds(b * BLK + at, c), :].rearrange("(t p) d -> p t d", p=n)).then_inc(sem_, 16)
                at += c

        def store_rows(eng, buf, dram, b, sem_):
            at = 0
            for n, t0, t1 in spans_of(b):
                c = n * (t1 - t0)
                eng.dma_start(dram[bass.ds(b * BLK + at, c), :].rearrange("(t p) d -> p t d", p=n), buf[0:n, t0:t1, :]).then_inc(sem_, 16)
                at += c

        def loaded(b):
            return 16 * (b + ndma(b))

        with ExitStack() as ph:
            sb, sem = maker(ph)
            XB, RS, YX = [sb(n, [P, TPB, D]) for n in ("XB", "RS", "YX")]
            XH, XL = [sb(n, [P, KD, BLK], F32R) for n in ("XH", "XL")]
            HH, HL = [sb(n, [P, KH, BLK], F32R) for n in ("HH", "HL")]
            HF = sb("HF", [P, 2, BLK])
            b1c, b2r, eps1, zb = sb("b1c", [P, KH]), sb("b2r", [P, D]), sb("eps1", [P, 1]), sb("zb", [P, TPB, D])
            norm = Norm(sb, sem, "n0")
            turn = Turn(sem, "t0")
            cst, e1_set, zb_set, zeroed = sem("cst0"), sem("e1_set"), sem("zb_set"), sem("zeroed1")
            xb_in, rs_in, yx_in, y_out = sem("xb_in"), sem("rs_in"), sem("yx_in"), sem("y_out")
            rst_set, h_done, f_set, hi_set, lo_set, hl_free = [sem("a_" + n) for n in ("rst_set", "h_done", "f_set", "hi_set", "lo_set", "hl_free")]
            y_done, y_read, x2_set, yp_set, y_set = [sem("a_" + n) for n in ("y_done", "y_read", "x2_set", "yp_set", "y_set")]
            TS = 2
            ALLB = NBLK

            with nc.Block() as block:
                @block.sync
                def _(sp):
                    with nc.allow_non_contiguous_dma(reason="a bias as a column"):
                        sp.dma_start(b1c[:, :], b1a.rearrange("(k p) -> p k", p=P)).then_inc(cst, 16)
                    sp.dma_start(b2r[:, :], b2a.partition_broadcast(P)).then_inc(cst, 16)
                    sp.dma_start(eps1[:, :], eps.partition_broadcast(P)).then_inc(cst, 16)

                    def load(b):
                        wait(sp, rst_set, b)
                        load_rows(sp, XB, x, b, xb_in)
                        wait(sp, turn.done, TS * b)
                        load_rows(sp, RS, seg0, b, rs_in)

                    def loady(b):
                        load_rows(sp, YX, x, b, yx_in)

                    def store(b):
                        sp.wait_ge(y_set, b + 1)
                        store_rows(sp, YX, x1, b, y_out)
                        sp.wait_ge(y_out, loaded(b))

                    load(0)
                    load(1)
                    loady(0)
                    sp.dma_start(RAW[:, 0:8, :], w1[0:8 * P, :].rearrange("(k p) n -> p k n", p=P)).then_inc(raw1_in, 16)
                    for half in range(2):
                        sp.dma_start(RAW[half * DE:(half + 1) * DE, 8, :], w1[8 * P:8 * P + DE, :]).then_inc(raw1_in, 16)
                    sp.dma_start(RAW[:, 9:13, :], w2.rearrange("(k p) n -> p k n", p=P)).then_inc(raw1_in, 16)
                    sp.wait_ge(zb_set, 1)
                    sp.dma_start(seg1[NBLK * BLK:SEGROWS, :].rearrange("(p r) d -> p r d", p=P), zb[:, :, :]).then_inc(zeroed, 16)

                    def body(b):
                        if b is not LASTB:
                            load(b + 1)
                        sp.dma_start(seg1[bass.ds((b - 1) * BLK, BLK), :].rearrange("(p r) d -> p r d", p=P), zb[:, :, :]).then_inc(zeroed, 16)
                        store(b - 1)
                        loady(b)
                    with sp.Fori(1, LASTB - 1) as b:
                        body(b)
                    body(LASTB - 1)
                    body(LASTB)
                    sp.dma_start(seg1[LASTB * BLK:NBLK * BLK, :].rearrange("(p r) d -> p r d", p=P), zb[:, :, :]).then_inc(zeroed, 16)
                    store(LASTB)
                    sp.wait_ge(zeroed, 16 * (NBLK + 1))

                @block.tensor
                def _(pe):
                    def first(b):
                        c = sum(rows_of(b))
                        for m in range(KH):
                            wait(pe, f_set, KH * b + m - 1)
                            for k in range(KD):
                                pe.wait_ge(turn.lo_set, TS * b + k // 2 + 1)
                                last = mm3(HBANK[m % 2][:, 0:c], A1H[:, k, m * P:(m + 1) * P], A1L[:, k, m * P:(m + 1) * P],
                                           XH[:, k, 0:c], XL[:, k, 0:c], k == 0, k == KD - 1)
                            last.then_inc(h_done, 1)

                    def turns(b, j):
                        pe.wait_ge(rst_set, b + 1)
                        turn.pe(pe, TS * b + j, b, RS, (2 * j, 2 * j + 1))

                    def second(b, ks):
                        for k in ks:
                            pe.wait_ge(lo_set, KH * b + k + 1)
                            for r in range(len(rows_of(b))):
                                if k == 0:
                                    wait(pe, y_read, TPB * (b - 1) + r + 1)
                                rows = slice(r * P, (r + 1) * P)
                                last = mm3(YBANK[r][:, :], HH[:, k, rows], HL[:, k, rows], A2H[:, k, :], A2L[:, k, :],
                                           k == 0, k == KH - 1)
                                if k == KH - 1:
                                    last.then_inc(y_done, 1)

                    def body(b):
                        first(b)
                        nxt = b is not LASTB
                        if nxt:
                            turns(b + 1, 0)
                        second(b, range(0, KH // 2))
                        if nxt:
                            turns(b + 1, 1)
                        second(b, range(KH // 2, KH))

                    turns(0, 0)
                    turns(0, 1)
                    body(0)
                    with pe.Fori(1, LASTB - 1) as b:
                        body(b)
                    body(LASTB - 1)
                    body(LASTB)

                @block.scalar
                def _(act):
                    act.wait_ge(cst, 48)

                    def turns(b, j):
                        turn.hi(act, TS * b + j, b, XH, (2 * j, 2 * j + 1))

                    def body(b):
                        c = sum(rows_of(b))
                        for m in range(KH):
                            act.wait_ge(h_done, KH * b + m + 1)
                            wait(act, lo_set, KH * b + m - 1)
                            nc.scalar.activation(HF[:, m % 2, 0:c], HBANK[m % 2][:, 0:c], ACT.Relu, bias=b1c[:, m:m + 1]).then_inc(f_set, 1)
                            act.wait_ge(f_set, KH * b + m + 1)
                            nc.scalar.copy(HH[:, m, 0:c], HF[:, m % 2, 0:c]).then_inc(hi_set, 1)
                        if b is not LASTB:
                            turns(b + 1, 0)
                            turns(b + 1, 1)

                    turns(0, 0)
                    turns(0, 1)
                    body(0)
                    with act.Fori(1, LASTB - 1) as b:
                        body(b)
                    body(LASTB - 1)
                    body(LASTB)

                @block.gpsimd
                def _(pool):
                    nc.gpsimd.memset(zb[:, :, :], 0.0).then_inc(zb_set, 1)
                    pool.wait_ge(cst, 48)

                    def prep(b):
                        nt = len(rows_of(b))
                        pool.wait_ge(yx_in, loaded(b))
                        nc.gpsimd.tensor_tensor(YX[:, 0:nt, :], YX[:, 0:nt, :], YX[:, 0:nt, :], ALU.add).then_inc(x2_set, 1)
                        pool.wait_ge(x2_set, b + 1)
                        for r in range(nt):
                            i = nc.gpsimd.tensor_tensor(YX[:, r, :], YX[:, r, :], b2r[:, :], ALU.add)
                        i.then_inc(yp_set, 1)

                    def body(b):
                        c = sum(rows_of(b))
                        for m in range(KH):
                            pool.wait_ge(hi_set, KH * b + m + 1)
                            nc.gpsimd.tensor_tensor(HL[:, m, 0:c], HF[:, m % 2, 0:c], HH[:, m, 0:c].bitcast(F32), ALU.subtract).then_inc(lo_set, 1)
                        prep(b)
                    blocks(pool, body)

                @block.vector
                def _(dve):
                    norm.blank()
                    dve.wait_ge(cst, 48)
                    nc.vector.tensor_scalar(eps1[:, :], eps1[:, :], 1.0, None, ALU.add).then_inc(e1_set, 1)
                    dve.wait_ge(e1_set, 1)

                    def rst(b):
                        dve.wait_ge(xb_in, loaded(b))
                        dve.wait_ge(rs_in, loaded(b))
                        for n, t0, t1 in spans_of(b):
                            i = nc.vector.scalar_tensor_tensor(RS[0:n, t0:t1, :], XB[0:n, t0:t1, :], eps1[0:n, 0:1], RS[0:n, t0:t1, :], ALU.mult, ALU.add)
                        i.then_inc(rst_set, 1)

                    def turns(b, j):
                        turn.lo(dve, TS * b + j, b, XH, XL, (2 * j, 2 * j + 1))

                    def ys(b):
                        nt = len(rows_of(b))
                        dve.wait_ge(yp_set, b + 1)
                        stats = norm.stats(YX)
                        for r in range(nt):
                            dve.wait_ge(y_done, TPB * b + r + 1)
                            nc.vector.tensor_tensor(YX[:, r, :], YBANK[r][:, :], YX[:, r, :], ALU.add).then_inc(y_read, 1)
                            if r:
                                dve.wait_ge(y_read, TPB * b + r)
                                stats(r - 1)
                        dve.wait_ge(y_read, TPB * b + nt)
                        stats(nt - 1).then_inc(norm.st_set, 1)
                        dve.wait_ge(norm.st_set, b + 1)
                        norm.rstd(dve, b, nt)
                        for r in range(nt):
                            i = nc.vector.tensor_scalar(YX[:, r, :], YX[:, r, :], norm.mv[:, r, 0:1], norm.y[:, r:r + 1], ALU.subtract, ALU.mult)
                        i.then_inc(y_set, 1)

                    rst(0)
                    turns(0, 0)
                    turns(0, 1)

                    def body(b):
                        if b is not 0:
                            ys(b - 1)
                        if b is not LASTB:
                            rst(b + 1)
                            turns(b + 1, 0)
                            turns(b + 1, 1)
                    body(0)
                    with dve.Fori(1, LASTB - 1) as b:
                        body(b)
                    body(LASTB - 1)
                    body(LASTB)
                    ys(LASTB)
        layer0.close()

        with ExitStack() as ph:
            sb, sem = maker(ph)
            UE, U2 = 8, 9
            TS = 5
            XH, XL = [sb("e" + n, [P, 2 * KD, BLK], F32R) for n in ("XH", "XL")]
            ES = sb("ES", [P, BLK], F32R)
            G = [sb(n, [P, TPB, D]) for n in ("GS", "GD")]
            EB = sb("EB", [P, TPB, 2, DE])
            HH, HL = [sb("e" + n, [P, KD, BLK], F32R) for n in ("HH", "HL")]
            MH, ML = [sb(n, [P, TPB, D], F32R) for n in ("MH", "ML")]
            SG = sb("eSG", [P, TPB, D])
            EQ = sb("eEQ", [P, TPB, P], F32R)
            DR = sb("eDR", [P, BLK], I32)
            b1c, b2r = sb("eb1c", [P, KD]), sb("eb2r", [P, D])
            gidx, sidx = sb("egidx", [P, 2, TPB], I32), sb("esidx", [P, TPB], I32)
            hid, msg = Mish(sb, sem, "hid", RAW[:, 11:13, :]), Mish(sb, sem, "msg")
            turn = Turn(sem, "t1")
            cst, eb_in, dr_in, gidx_set, sidx_set = [sem("e_" + n) for n in ("cst", "eb_in", "dr_in", "gidx_set", "sidx_set")]
            g_in = [[sem(f"g{j}_in{r}") for r in range(TPB)] for j in range(2)]
            scat = [sem(f"scat1_{r}") for r in range(TPB)]
            w_hi, w_lo = sem("e_w_hi"), sem("e_w_lo")
            bank_free = [sem(f"e_bank{j}_free") for j in range(2)]
            h_done, y_done, s_done, sg_set, eq_set, msg_read = [sem("e_" + n) for n in ("h_done", "y_done", "s_done", "sg_set", "eq_set", "msg_read")]
            CHUNKS = [(0, 3), (3, 6), (6, 9), (9, 13)]

            def hi_(b, m):
                return KD * b + m

            def qi_(b, r):
                return TPB * b + r

            def used(b, j):
                return j if b is 0 else 4 * b - 2 + j

            def turn_src(i):
                return G[i // 2], (2 * (i % 2), 2 * (i % 2) + 1), (2 * i, 2 * i + 1)

            def loop(eng, f):
                f(0)
                f(1)
                f(2)
                with eng.Fori(3, LASTB - 1) as b:
                    f(b)
                for b in range(LASTB - 1, NBLK + 1):
                    f(b)

            def live(b):
                return not isinstance(b, int) or 0 <= b < NBLK

            with nc.Block() as block:
                @block.sync
                def _(sp):
                    with nc.allow_non_contiguous_dma(reason="a bias as a column"):
                        sp.dma_start(b1c[:, :], b1.rearrange("(k p) -> p k", p=P)).then_inc(cst, 16)
                    sp.dma_start(b2r[:, :], b2.partition_broadcast(P)).then_inc(cst, 16)

                    def attrs(b):
                        at = 0
                        for n, t0, t1 in spans_of(b):
                            c = n * (t1 - t0)
                            for j in range(2):
                                sp.dma_start(EB[0:n, t0:t1, j, :], edge_attr[bass.ds(b * BLK + at, c), :].rearrange("(t p) d -> p t d", p=n)).then_inc(eb_in, 16)
                            at += c

                    def body(b):
                        if live(b + 1):
                            wait(sp, turn.done, TS * (b + 1))
                            attrs(b + 1)
                        if live(b):
                            wait(sp, eq_set, TPB * b)
                            n = sum(rows_of(b))
                            sp.dma_start(DR[:, 0:n], dst[bass.ds(b * BLK, n)].partition_broadcast(P)).then_inc(dr_in, 16)
                        if b is 0:
                            sp.wait_ge(w_lo, len(CHUNKS))
                            sp.dma_start(RAW[:, 0:8, :], w3.rearrange("(k p) n -> p k n", p=P)).then_inc(raw2_in, 16)
                            sp.dma_start(RAW[:, 8:11, :], w4[0:3 * P, :].rearrange("(k p) n -> p k n", p=P)).then_inc(raw2_in, 16)
                    attrs(0)
                    loop(sp, body)

                @block.gpsimd
                def _(pool):
                    pool.wait_ge(raw1_in, 64)

                    def stage_idx(b):
                        nt = len(rows_of(b))
                        for j in range(2):
                            for r in range(TPB):
                                wait(pool, g_in[j][r], 16 * b)
                            i = nc.gpsimd.tensor_copy(gidx[:, j, 0:nt], (srcI, dstI)[j][:, bass.ds(b * TPB, nt)])
                        i.then_inc(gidx_set, 1)

                    def gather(b, j, r):
                        rows = rows_of(b)
                        if r >= len(rows):
                            return
                        n = rows[r]
                        if r == 0:
                            wait(pool, turn.done, TS * (b - 1) + 2 * (j + 1))
                            pool.wait_ge(gidx_set, b + 1)
                            settle(pool)
                        nc.gpsimd.indirect_dma_start(G[j][0:n, r, :], None, x1[:, :],
                                                     bass.IndirectOffsetOnAxis(gidx[0:n, j, r:r + 1], 0)).then_inc(g_in[j][r], 16)

                    def scatter(b, r):
                        rows = rows_of(b)
                        if r >= len(rows):
                            return
                        n = rows[r]
                        if r == 0:
                            wait(pool, scat[TPB - 1], 16 * b)
                            nc.gpsimd.tensor_copy(sidx[:, 0:len(rows)], tgt1[:, bass.ds(b * TPB, len(rows))]).then_inc(sidx_set, 1)
                            pool.wait_ge(sidx_set, b + 1)
                        else:
                            pool.wait_ge(scat[r - 1], 16 * (b + 1))
                        pool.wait_ge(sg_set, qi_(b, r) + 1)
                        settle(pool)
                        nc.gpsimd.indirect_dma_start(seg1[:, :], bass.IndirectOffsetOnAxis(sidx[0:n, r:r + 1], 0),
                                                     SG[0:n, r, :], None, compute_op=ALU.add).then_inc(scat[r], 16)

                    def hid_t(b, m):
                        if live(b):
                            hid.t(pool, hi_(b, m), m % 2, sum(rows_of(b)))

                    def hid_lo(b, m):
                        if live(b):
                            c = sum(rows_of(b))
                            hid.lo(pool, hi_(b, m), m % 2, HL[:, m, 0:c], HH[:, m, 0:c], c)

                    def msg_t(b, r):
                        if live(b) and r < len(rows_of(b)):
                            msg.t(pool, qi_(b, r), r % 2, D)

                    def body(b):
                        nxt = live(b + 1)

                        def g(j, r):
                            if nxt:
                                gather(b + 1, j, r)

                        def sc(r):
                            if live(b - 2):
                                scatter(b - 2, r)
                        if nxt:
                            stage_idx(b + 1)
                        msg_t(b - 1, 0)
                        g(0, 0)
                        msg_t(b - 1, 1)
                        g(0, 1)
                        sc(0)
                        hid_t(b, 0)
                        g(0, 2)
                        msg_t(b - 1, 2)
                        g(0, 3)
                        sc(1)
                        hid_t(b, 1)
                        g(1, 0)
                        hid_lo(b, 0)
                        msg_t(b - 1, 3)
                        g(1, 1)
                        hid_t(b, 2)
                        hid_lo(b, 1)
                        g(1, 2)
                        g(1, 3)
                        hid_t(b, 3)
                        sc(2)
                        hid_lo(b, 2)
                        hid_lo(b, 3)
                        sc(3)

                    stage_idx(0)
                    for j in range(2):
                        for r in range(TPB):
                            gather(0, j, r)
                    for n, (u0, u1) in enumerate(CHUNKS):
                        if n % 2:
                            pool.wait_ge(w_hi, n + 1)
                            nc.gpsimd.tensor_tensor(WLO[:, u0:u1, :], RAW[:, u0:u1, :], WHI[:, u0:u1, :].bitcast(F32), ALU.subtract).then_inc(w_lo, 1)
                    loop(pool, body)
                    for r in range(TPB):
                        scatter(LASTB, r)
                    for r in range(TPB):
                        pool.wait_ge(scat[r], 16 * (NBLK if r < len(rows_of(LASTB)) else LASTB))

                @block.scalar
                def _(act):
                    nc.scalar.preload_act_table_set("natural_log_exp_and_others")
                    act.wait_ge(raw1_in, 64)
                    for u0, u1 in CHUNKS:
                        nc.scalar.copy(WHI[:, u0:u1, :], RAW[:, u0:u1, :]).then_inc(w_hi, 1)

                    def turns(b, i):
                        if live(b):
                            turn.hi(act, TS * b + i, b, XH, turn_src(i)[2])

                    def attr_hi(b):
                        if live(b):
                            c = sum(rows_of(b))
                            act.wait_ge(turn.done, TS * b + TS)
                            nc.scalar.copy(ES[:, 0:c], bank[0][:, 0:c]).then_inc(turn.hi_set, 1)

                    def h_(f, b, m):
                        if live(b):
                            c = sum(rows_of(b))
                            if f == "hi":
                                hid.hi(act, hi_(b, m), m % 2, HH[:, m, 0:c], c)
                            else:
                                (hid.e if f == "e" else hid.r)(act, hi_(b, m), m % 2, c)

                    def q_(f, b, r):
                        if live(b) and r < len(rows_of(b)):
                            if f == "hi":
                                msg.hi(act, qi_(b, r), r % 2, MH[:, r, :], D)
                            else:
                                (msg.e if f == "e" else msg.r)(act, qi_(b, r), r % 2, D)

                    def sums(b, r):
                        if live(b) and r < len(rows_of(b)):
                            act.wait_ge(s_done, qi_(b, r) + 1)
                            wait(act, scat[r], 16 * b)
                            nc.scalar.copy(SG[:, r, :], HBANK[r % 2][:, :]).then_inc(sg_set, 1)
                            act.wait_ge(sg_set, qi_(b, r) + 1)
                            act.sem_inc(bank_free[r % 2], 1)

                    def body(b):
                        q_("e", b - 1, 0)
                        q_("e", b - 1, 1)
                        q_("r", b - 1, 0)
                        q_("r", b - 1, 1)
                        q_("hi", b - 1, 0)
                        h_("e", b, 0)
                        q_("hi", b - 1, 1)
                        h_("r", b, 0)
                        q_("e", b - 1, 2)
                        q_("r", b - 1, 2)
                        h_("e", b, 1)
                        h_("hi", b, 0)
                        h_("r", b, 1)
                        q_("e", b - 1, 3)
                        q_("hi", b - 1, 2)
                        q_("r", b - 1, 3)
                        h_("e", b, 2)
                        h_("hi", b, 1)
                        h_("r", b, 2)
                        q_("hi", b - 1, 3)
                        h_("e", b, 3)
                        h_("hi", b, 2)
                        turns(b + 1, 0)
                        h_("r", b, 3)
                        turns(b + 1, 1)
                        h_("hi", b, 3)
                        turns(b + 1, 2)
                        sums(b - 1, 0)
                        sums(b - 1, 1)
                        turns(b + 1, 3)
                        sums(b - 1, 2)
                        sums(b - 1, 3)
                        attr_hi(b + 1)

                    for i in range(TS - 1):
                        turns(0, i)
                    attr_hi(0)
                    loop(act, body)

                @block.vector
                def _(dve):
                    nc.vector.memset(WLO[DE:P, UE, :].bitcast(F32), 0.0)
                    for n, (u0, u1) in enumerate(CHUNKS):
                        if n % 2 == 0:
                            dve.wait_ge(w_hi, n + 1)
                            if u1 == UE + 1:
                                nc.vector.tensor_tensor(WLO[:, u0:UE, :], RAW[:, u0:UE, :], WHI[:, u0:UE, :].bitcast(F32), ALU.subtract)
                                nc.vector.tensor_tensor(WLO[0:DE, UE, :], RAW[0:DE, UE, :], WHI[0:DE, UE, :].bitcast(F32), ALU.subtract).then_inc(w_lo, 1)
                            else:
                                nc.vector.tensor_tensor(WLO[:, u0:u1, :], RAW[:, u0:u1, :], WHI[:, u0:u1, :].bitcast(F32), ALU.subtract).then_inc(w_lo, 1)
                    dve.wait_ge(cst, 32)

                    def turns(b, i):
                        if live(b):
                            turn.lo(dve, TS * b + i, b, XH, XL, turn_src(i)[2])

                    def attr_lo(b):
                        if live(b):
                            c = sum(rows_of(b))
                            dve.wait_ge(turn.hi_set, TS * b + TS)
                            nc.vector.tensor_tensor(ES[DE:P, 0:c], bank[0][DE:P, 0:c], ES[DE:P, 0:c].bitcast(F32), ALU.subtract).then_inc(turn.lo_set, 1)

                    def h_z(b, m):
                        if live(b):
                            c = sum(rows_of(b))
                            dve.wait_ge(h_done, hi_(b, m) + 1)
                            hid.z_col(dve, hi_(b, m), m % 2, HBANK[m % 2][:, 0:c], b1c[:, m:m + 1], c)
                            dve.sem_inc(bank_free[m % 2], 1)

                    def h_n(b, m):
                        if live(b):
                            hid.n(dve, hi_(b, m), m % 2, sum(rows_of(b)))

                    def h_m(b, m):
                        if live(b):
                            hid.m(dve, hi_(b, m), m % 2, sum(rows_of(b)))

                    def q_z(b, r):
                        if live(b) and r < len(rows_of(b)):
                            dve.wait_ge(y_done, qi_(b, r) + 1)
                            msg.z_row(dve, qi_(b, r), r % 2, YBANK[r][:, :], b2r[:, :])

                    def q_n(b, r):
                        if live(b) and r < len(rows_of(b)):
                            msg.n(dve, qi_(b, r), r % 2, D)

                    def q_m(b, r):
                        if live(b) and r < len(rows_of(b)):
                            msg.m(dve, qi_(b, r), r % 2, D)

                    def q_lo(b, r):
                        if live(b) and r < len(rows_of(b)):
                            msg.lo(nc.vector, qi_(b, r), r % 2, ML[:, r, :], MH[:, r, :], D)

                    def same(b):
                        if live(b):
                            dve.wait_ge(dr_in, 16 * (b + 1))
                            for r in range(len(rows_of(b))):
                                nc.vector.tensor_scalar(EQ[:, r, :], DR[:, r * P:(r + 1) * P], dstF[:, bass.ds(b * TPB + r, 1)], None, ALU.is_equal).then_inc(eq_set, 1)

                    def body(b):
                        q_z(b - 1, 0)
                        q_z(b - 1, 1)
                        q_n(b - 1, 0)
                        q_n(b - 1, 1)
                        q_m(b - 1, 0)
                        q_lo(b - 1, 0)
                        q_m(b - 1, 1)
                        h_z(b, 0)
                        q_z(b - 1, 2)
                        h_n(b, 0)
                        q_lo(b - 1, 1)
                        q_n(b - 1, 2)
                        h_m(b, 0)
                        h_z(b, 1)
                        q_m(b - 1, 2)
                        h_n(b, 1)
                        q_z(b - 1, 3)
                        q_lo(b - 1, 2)
                        h_m(b, 1)
                        q_n(b - 1, 3)
                        h_z(b, 2)
                        q_m(b - 1, 3)
                        h_n(b, 2)
                        q_lo(b - 1, 3)
                        h_m(b, 2)
                        same(b - 1)
                        h_z(b, 3)
                        h_n(b, 3)
                        turns(b + 1, 0)
                        h_m(b, 3)
                        turns(b + 1, 1)
                        turns(b + 1, 2)
                        turns(b + 1, 3)
                        attr_lo(b + 1)

                    for i in range(TS - 1):
                        turns(0, i)
                    attr_lo(0)
                    loop(dve, body)

                @block.tensor
                def _(pe):
                    def turns(b, i):
                        if not live(b):
                            return
                        buf, ks, _ = turn_src(i)
                        if i % 2 == 0:
                            for r in range(len(rows_of(b))):
                                pe.wait_ge(g_in[i // 2][r], 16 * (b + 1))
                        turn.pe(pe, TS * b + i, b, buf, ks)

                    def attr_turn(b):
                        if live(b):
                            pe.wait_ge(eb_in, 2 * loaded(b))
                            wait(pe, turn.lo_set, TS * b + TS - 1)
                            for r, n in enumerate(rows_of(b)):
                                last = nc.tensor.transpose(bank[0][:, r * P:r * P + n], EB[0:n, r, :, :].rearrange("p j d -> p (j d)"), ident[0:n, 0:n])
                            last.then_inc(turn.done, 1)

                    def first(b):
                        if not live(b):
                            return
                        c = sum(rows_of(b))
                        for m in range(KD):
                            cols = slice(m * P, (m + 1) * P)
                            acc = HBANK[m % 2][:, 0:c]
                            wait(pe, bank_free[m % 2], used(b, m // 2))
                            for k in range(2 * KD):
                                if m == 0 and k % 2 == 0:
                                    pe.wait_ge(turn.lo_set, TS * b + k // 2 + 1)
                                mm3(acc, WHI[:, k, cols], WLO[:, k, cols], XH[:, k, 0:c], XL[:, k, 0:c], k == 0, False)
                            if m == 0:
                                pe.wait_ge(turn.lo_set, TS * b + TS)
                            nc.tensor.matmul(acc, WHI[:, UE, cols], ES[:, 0:c], start=False, stop=False)
                            nc.tensor.matmul(acc, WLO[:, UE, cols], ES[:, 0:c], start=False, stop=True).then_inc(h_done, 1)

                    def second(b, k):
                        if not live(b):
                            return
                        pe.wait_ge(hid.lo_set, hi_(b, k) + 1)
                        for r in range(len(rows_of(b))):
                            if k == 0:
                                wait(pe, msg.v_set, qi_(b - 1, r) + 1)
                            rows = slice(r * P, (r + 1) * P)
                            last = mm3(YBANK[r][:, :], HH[:, k, rows], HL[:, k, rows], WHI[:, U2 + k, :], WLO[:, U2 + k, :], k == 0, k == KD - 1)
                            if k == KD - 1:
                                last.then_inc(y_done, 1)

                    def sums(b, r):
                        if live(b) and r < len(rows_of(b)):
                            pe.wait_ge(msg.lo_set, qi_(b, r) + 1)
                            pe.wait_ge(eq_set, qi_(b, r) + 1)
                            wait(pe, bank_free[r % 2], used(b + 1, 2 + r // 2) - (2 if b is LASTB else 0))
                            acc = HBANK[r % 2][:, :]
                            nc.tensor.matmul(acc, EQ[:, r, :], MH[:, r, :], start=True, stop=False)
                            nc.tensor.matmul(acc, EQ[:, r, :], ML[:, r, :], start=False, stop=True).then_inc(s_done, 1)

                    def body(b):
                        first(b)
                        turns(b + 1, 0)
                        second(b, 0)
                        turns(b + 1, 1)
                        second(b, 1)
                        turns(b + 1, 2)
                        second(b, 2)
                        sums(b - 1, 0)
                        sums(b - 1, 1)
                        turns(b + 1, 3)
                        second(b, 3)
                        sums(b - 1, 2)
                        sums(b - 1, 3)
                        attr_turn(b + 1)

                    for i in range(TS - 1):
                        turns(0, i)
                    attr_turn(0)
                    pe.wait_ge(w_lo, len(CHUNKS))
                    loop(pe, body)

        with ExitStack() as ph:
            sb, sem = maker(ph)
            U4 = 8
            TS = 4
            ROWS = [sb(n, [P, TPB, D]) for n in ("NB", "AB")]
            YX, YO, Y, OUT = [sb("n" + n, [P, TPB, D]) for n in ("YX", "YO", "Y", "OUT")]
            XH, XL = [sb("n" + n, [P, 2 * KD, BLK], F32R) for n in ("XH", "XL")]
            HH, HL = [sb("n" + n, [P, KD, BLK], F32R) for n in ("HH", "HL")]
            b3c, b4r, gam, bet = sb("b3c", [P, KD]), sb("b4r", [P, D]), sb("gam", [P, D]), sb("bet", [P, D])
            hid = Mish(sb, sem, "nhid")
            norm, norm2 = Norm(sb, sem, "n1"), Norm(sb, sem, "n2")
            turn = Turn(sem, "t2")
            cst, yx_in, y_out = [sem("n_" + n) for n in ("cst", "yx_in", "y_out")]
            rows_in = [sem(f"n_rows{j}_in") for j in range(2)]
            w_hi, w_lo = sem("n_w_hi"), sem("n_w_lo")
            h_done, y_done, y_read, yo_set, yx_set, y_set, g_set, s_set, norm_set = [
                sem("n_" + n) for n in ("h_done", "y_done", "y_read", "yo_set", "yx_set", "y_set", "g_set", "s_set", "norm_set")]
            CHUNKS = [(0, 3), (3, 6), (6, 9), (9, 12)]

            def hi_(b, m):
                return KD * b + m

            def turn_src(i):
                return ROWS[i // 2], (2 * (i % 2), 2 * (i % 2) + 1), (2 * i, 2 * i + 1)

            def loop(eng, f):
                f(0)
                f(1)
                with eng.Fori(2, LASTB - 1) as b:
                    f(b)
                for b in range(LASTB - 1, NBLK + 1):
                    f(b)

            def live(b):
                return not isinstance(b, int) or 0 <= b < NBLK

            def rows_done(b, r=None):
                return TPB * b + (len(rows_of(b)) if r is None else r + 1)

            with nc.Block() as block:
                @block.sync
                def _(sp):
                    with nc.allow_non_contiguous_dma(reason="a bias as a column"):
                        sp.dma_start(b3c[:, :], b3.rearrange("(k p) -> p k", p=P)).then_inc(cst, 16)
                    for row, a in ((b4r, b4), (gam, gamma), (bet, beta)):
                        sp.dma_start(row[:, :], a.partition_broadcast(P)).then_inc(cst, 16)

                    def load(b):
                        for j, a in enumerate((x1, seg1)):
                            wait(sp, turn.done, TS * (b - 1) + 2 * (j + 1))
                            if j == 0:
                                settle(sp)
                                wait(sp, yo_set, b)
                            settle(sp)
                            load_rows(sp, ROWS[j], a, b, rows_in[j])

                    def body(b):
                        if live(b + 1):
                            load(b + 1)
                        if live(b - 1) and live(b):
                            sp.wait_ge(s_set, rows_done(b - 1))
                            settle(sp)
                            load_rows(sp, YX, x1, b, yx_in)
                        if live(b - 1):
                            sp.wait_ge(y_set, rows_done(b - 1))
                            store_rows(sp, OUT, out, b - 1, y_out)
                    load(0)
                    load_rows(sp, YX, x1, 0, yx_in)
                    sp.dma_start(RAW[:, 11, :], w4[3 * P:4 * P, :]).then_inc(raw2_in, 16)
                    loop(sp, body)
                    sp.wait_ge(y_out, loaded(LASTB))

                @block.gpsimd
                def _(pool):
                    for n, (u0, u1) in enumerate(CHUNKS):
                        if n % 2:
                            pool.wait_ge(w_hi, n + 1)
                            nc.gpsimd.tensor_tensor(WLO[:, u0:u1, :], RAW[:, u0:u1, :], WHI[:, u0:u1, :].bitcast(F32), ALU.subtract).then_inc(w_lo, 1)
                    pool.wait_ge(cst, 64)

                    def with_b4(b):
                        if live(b):
                            pool.wait_ge(rows_in[0], loaded(b))
                            for r in range(len(rows_of(b))):
                                wait(pool, y_read, rows_done(b - 1, r))
                                i = nc.gpsimd.tensor_tensor(YO[:, r, :], ROWS[0][:, r, :], b4r[:, :], ALU.add)
                            i.then_inc(yo_set, 1)

                    def with_beta(b):
                        if live(b):
                            pool.wait_ge(yx_in, loaded(b))
                            for r in range(len(rows_of(b))):
                                i = nc.gpsimd.tensor_tensor(YX[:, r, :], YX[:, r, :], bet[:, :], ALU.add)
                            i.then_inc(yx_set, 1)

                    def times_gamma(b):
                        if live(b):
                            for r in range(len(rows_of(b))):
                                pool.wait_ge(norm_set, rows_done(b, r))
                                nc.gpsimd.tensor_tensor(Y[:, r, :], Y[:, r, :], gam[:, :], ALU.mult).then_inc(g_set, 1)

                    def t(b, m):
                        if live(b):
                            hid.t(pool, hi_(b, m), m % 2, sum(rows_of(b)))

                    def lo(b, m):
                        if live(b):
                            c = sum(rows_of(b))
                            hid.lo(nc.gpsimd, hi_(b, m), m % 2, HL[:, m, 0:c], HH[:, m, 0:c], c)

                    def body(b):
                        with_b4(b)
                        t(b, 0)
                        times_gamma(b - 1)
                        t(b, 1)
                        lo(b, 0)
                        t(b, 2)
                        lo(b, 1)
                        t(b, 3)
                        lo(b, 2)
                        lo(b, 3)
                        with_beta(b)
                    loop(pool, body)

                @block.scalar
                def _(act):
                    nc.scalar.preload_act_table_set("natural_log_exp_and_others")
                    act.wait_ge(raw2_in, 48)
                    for u0, u1 in CHUNKS:
                        nc.scalar.copy(WHI[:, u0:u1, :], RAW[:, u0:u1, :]).then_inc(w_hi, 1)

                    def turns(b, i):
                        if live(b):
                            turn.hi(act, TS * b + i, b, XH, turn_src(i)[2])

                    def h_(f, b, m):
                        if live(b):
                            c = sum(rows_of(b))
                            if f == "hi":
                                hid.hi(act, hi_(b, m), m % 2, HH[:, m, 0:c], c)
                            else:
                                (hid.e if f == "e" else hid.r)(act, hi_(b, m), m % 2, c)

                    def normed(b, nrm, sem_, to, n):
                        if live(b):
                            act.wait_ge(nrm.set, b + 1)
                            if n == 2:
                                wait(act, y_out, 16 * b)
                            for r in range(len(rows_of(b))):
                                nc.scalar.activation(to[:, r, :], Y[:, r, :], ACT.Identity, bias=nrm.nm[:, r:r + 1], scale=nrm.y[:, r:r + 1]).then_inc(sem_, 1)

                    def body(b):
                        h_("e", b, 0)
                        h_("r", b, 0)
                        normed(b - 1, norm, norm_set, Y, 1)
                        h_("e", b, 1)
                        h_("hi", b, 0)
                        h_("r", b, 1)
                        h_("e", b, 2)
                        h_("hi", b, 1)
                        h_("r", b, 2)
                        h_("e", b, 3)
                        h_("hi", b, 2)
                        if live(b):
                            turns(b + 1, 0)
                        h_("r", b, 3)
                        if live(b):
                            turns(b + 1, 1)
                        h_("hi", b, 3)
                        if live(b):
                            turns(b + 1, 2)
                        normed(b - 1, norm2, y_set, OUT, 2)
                        if live(b):
                            turns(b + 1, 3)

                    for i in range(TS):
                        turns(0, i)
                    loop(act, body)

                @block.vector
                def _(dve):
                    norm.blank()
                    norm2.blank()
                    for n, (u0, u1) in enumerate(CHUNKS):
                        if n % 2 == 0:
                            dve.wait_ge(w_hi, n + 1)
                            nc.vector.tensor_tensor(WLO[:, u0:u1, :], RAW[:, u0:u1, :], WHI[:, u0:u1, :].bitcast(F32), ALU.subtract).then_inc(w_lo, 1)
                    dve.wait_ge(cst, 64)

                    def turns(b, i):
                        if live(b):
                            turn.lo(dve, TS * b + i, b, XH, XL, turn_src(i)[2])

                    def y_tiles(b):
                        if live(b):
                            dve.wait_ge(yo_set, b + 1)
                            nt = len(rows_of(b))
                            for r in range(nt + 1):
                                if r < nt:
                                    wait(dve, y_set, rows_done(b - 1, r))
                                    dve.wait_ge(y_done, rows_done(b, r))
                                    nc.vector.tensor_tensor(Y[:, r, :], YBANK[r][:, :], YO[:, r, :], ALU.add).then_inc(y_read, 1)
                                if r:
                                    dve.wait_ge(y_read, rows_done(b, r - 1))
                                    nc.vector.bn_stats(norm.st[:, r - 1, :], Y[:, r - 1, :]).then_inc(norm.st_set, 1)

                    def scales(b, nrm):
                        if live(b):
                            dve.wait_ge(nrm.st_set, rows_done(b))
                            nrm.rstd(dve, b, len(rows_of(b)))

                    def added(b, rs):
                        if live(b):
                            nt = len(rows_of(b))
                            if rs[0] == 0:
                                dve.wait_ge(yx_set, b + 1)
                            for r in rs:
                                if r < nt:
                                    dve.wait_ge(g_set, rows_done(b, r))
                                    nc.vector.tensor_tensor(Y[:, r, :], Y[:, r, :], YX[:, r, :], ALU.add).then_inc(s_set, 1)
                            for r in rs:
                                if r < nt:
                                    dve.wait_ge(s_set, rows_done(b, r))
                                    nc.vector.bn_stats(norm2.st[:, r, :], Y[:, r, :]).then_inc(norm2.st_set, 1)

                    def z(b, m):
                        if live(b):
                            c = sum(rows_of(b))
                            dve.wait_ge(h_done, hi_(b, m) + 1)
                            hid.z_col(dve, hi_(b, m), m % 2, HBANK[m % 2][:, 0:c], b3c[:, m:m + 1], c)

                    def n(b, m):
                        if live(b):
                            hid.n(dve, hi_(b, m), m % 2, sum(rows_of(b)))

                    def m_(b, m):
                        if live(b):
                            hid.m(dve, hi_(b, m), m % 2, sum(rows_of(b)))

                    def body(b):
                        y_tiles(b - 1)
                        z(b, 0)
                        n(b, 0)
                        scales(b - 1, norm)
                        m_(b, 0)
                        z(b, 1)
                        n(b, 1)
                        added(b - 1, (0, 1))
                        m_(b, 1)
                        z(b, 2)
                        n(b, 2)
                        added(b - 1, (2, 3))
                        m_(b, 2)
                        z(b, 3)
                        n(b, 3)
                        if live(b):
                            turns(b + 1, 0)
                        m_(b, 3)
                        if live(b):
                            turns(b + 1, 1)
                        scales(b - 1, norm2)
                        if live(b):
                            turns(b + 1, 2)
                            turns(b + 1, 3)

                    for i in range(TS):
                        turns(0, i)
                    loop(dve, body)

                @block.tensor
                def _(pe):
                    def turns(b, i):
                        if live(b):
                            buf, ks, _ = turn_src(i)
                            pe.wait_ge(rows_in[i // 2], loaded(b))
                            turn.pe(pe, TS * b + i, b, buf, ks)

                    def body(b):
                        if not live(b):
                            return
                        c = sum(rows_of(b))
                        for m in range(KD):
                            cols = slice(m * P, (m + 1) * P)
                            wait(pe, hid.v_set, hi_(b, m) - 1)
                            for k in range(2 * KD):
                                if m == 0 and k % 2 == 0:
                                    pe.wait_ge(turn.lo_set, TS * b + k // 2 + 1)
                                last = mm3(HBANK[m % 2][:, 0:c], WHI[:, k, cols], WLO[:, k, cols], XH[:, k, 0:c], XL[:, k, 0:c], k == 0, k == 2 * KD - 1)
                            last.then_inc(h_done, 1)
                        for k in range(KD):
                            turns(b + 1, k)
                            pe.wait_ge(hid.lo_set, hi_(b, k) + 1)
                            for r in range(len(rows_of(b))):
                                if k == 0:
                                    wait(pe, y_read, rows_done(b - 1, r))
                                rows = slice(r * P, (r + 1) * P)
                                last = mm3(YBANK[r][:, :], HH[:, k, rows], HL[:, k, rows], WHI[:, U4 + k, :], WLO[:, U4 + k, :], k == 0, k == KD - 1)
                                if k == KD - 1:
                                    last.then_inc(y_done, 1)

                    for i in range(TS):
                        turns(0, i)
                    pe.wait_ge(w_lo, len(CHUNKS))
                    loop(pe, body)


_INS = ['x', 'src', 'dst', 'edge_attr_64', 'L0_gnn_W1', 'L0_gnn_b1', 'L0_gnn_W2', 'L0_gnn_b2', 'L0_gnn_eps',
        'L1_gnn_W1', 'L1_gnn_b1', 'L1_gnn_W2', 'L1_gnn_b2', 'L1_gnn_W3', 'L1_gnn_b3', 'L1_gnn_W4', 'L1_gnn_b4',
        'L1_gnn_gamma', 'L1_gnn_beta']
_OUTS = [((N, D), 'float32')]


def kernel(**inputs):
    import numpy as _np
    import concourse.bacc as _bacc
    from concourse import mybir as _mybir
    from concourse.bass_utils import run_bass_kernel_spmd as _run

    nc = _bacc.Bacc("TRN2", target_bir_lowering=False, num_devices=1)
    arrays, args = {}, []
    for name in _INS:
        a = _np.ascontiguousarray(inputs[name])
        arrays[f"in_{name}_dram"] = a
        args.append(nc.dram_tensor(f"in_{name}_dram", a.shape, _mybir.dt.from_np(a.dtype), kind="ExternalInput").ap())
    for i, (shape, dtype) in enumerate(_OUTS):
        dt = _mybir.dt.from_np(_np.dtype(dtype))
        args.append(nc.dram_tensor(f"out_{i}_dram", shape, dt, kind="ExternalOutput").ap())
    gnn_resnorm_kernel(nc, *args)
    r = _run(nc, [arrays], core_ids=[0])
    got = tuple(r.results[0][f"out_{i}_dram"] for i in range(len(_OUTS)))
    return got[0]
```

```python
import concourse.bass as bass
from concourse import mybir
from contextlib import ExitStack

F32 = mybir.dt.float32
F32R = mybir.dt.float32r
I32 = mybir.dt.int32
ALU = mybir.AluOpType
ACT = mybir.ActivationFunctionType
AX = mybir.AxisListType

P = 128
D = 512
DH = 1024
DE = 64
N = 10000
TPB = 4
BLK = TPB * P
NBLK = -(-N // BLK)
LASTB = NBLK - 1
LASTROWS = N - LASTB * BLK
NT = -(-N // P)
LN_EPS = 1e-5
ZCAP = 20.0
SEGROWS = (NBLK + 1) * BLK
KD = D // P
KH = DH // P
RSQRT_STEPS = 3


def rows_of(b):
    if isinstance(b, int) and b == LASTB:
        left, out = LASTROWS, []
        while left > 0:
            out.append(min(left, P))
            left -= P
        return out
    return [P] * TPB


def spans_of(b):
    rows = rows_of(b)
    full = sum(r == P for r in rows)
    spans = [(P, 0, full)]
    if full < len(rows):
        spans.append((rows[-1], full, len(rows)))
    return spans


def blocks(eng, f, first=1, end=LASTB):
    for b in range(first):
        f(b)
    with eng.Fori(first, end) as b:
        f(b)
    for b in range(end, NBLK):
        f(b)


def wait(eng, sem, value):
    if not isinstance(value, int) or value > 0:
        eng.wait_ge(sem, value)


def ndma(b):
    return len(spans_of(b))


def gnn_resnorm_kernel(nc, x, src, dst, edge_attr, w1a, b1a, w2a, b2a, eps, w1, b1, w2, b2,
                       w3, b3, w4, b4, gamma, beta, out):
    seg0 = nc.dram_tensor("seg0", (SEGROWS, D), F32, kind="Internal").ap()
    seg1 = nc.dram_tensor("seg1", (SEGROWS, D), F32, kind="Internal").ap()
    x1 = nc.dram_tensor("x1", (N, D), F32, kind="Internal").ap()

    ctx = ExitStack()
    with ctx:
        def maker(stack):
            def sb(name, shape, dt=F32):
                return stack.enter_context(nc.sbuf_tensor(name, shape, dt))

            def sem(name):
                return stack.enter_context(nc.semaphore(name))
            return sb, sem

        sb, sem = maker(ctx)
        WELEMS = 2 * (8 + 4) * D + 2 * D
        W = sb("W", [P, WELEMS], F32R)
        RAWK = 13
        RAW = sb("RAW", [P, RAWK, D])
        ident = sb("ident", [P, P])
        dstF = sb("dstF", [P, NT + 1])
        srcI = sb("srcI", [P, NT + 1], I32)
        dstI = sb("dstI", [P, NT + 1], I32)
        tgt0 = sb("tgt0", [P, NT + 1], I32)
        tgt1 = sb("tgt1", [P, NT + 1], I32)
        bank = [ctx.enter_context(nc.psum_tensor(f"bank{i}", [P, 512], F32)) for i in range(8)]

        two = sb("two", [P, 1])
        ticks = sem("ticks")

        def settle(eng):
            eng.sem_inc(ticks, 1)

        xb_in = sem("xb_in")
        XB0 = RAW[:, 8:8 + TPB, :]
        raw1_in, raw2_in = sem("raw1_in"), sem("raw2_in")

        with ExitStack() as ph:
            sb, sem = maker(ph)
            ii = sb("ii", [P, 2, P], I32)
            iF = sb("iF", [P, 2, P])
            idx_blank, idx_in, idx_f, idx_t, idx_done = [sem(f"idx{i}") for i in range(5)]
            id_blank, id_set = sem("id_blank"), sem("id_set")
            with nc.Block() as block:
                @block.sync
                def _(sp):
                    full = N // P
                    sp.wait_ge(idx_blank, 1)
                    for j, a in enumerate((src, dst)):
                        sp.dma_start(ii[0:full, j, :], a[0:full * P].rearrange("(t p) -> t p", p=P)).then_inc(idx_in, 16)
                        sp.dma_start(ii[full:full + 1, j, 0:N - full * P], a[full * P:N].rearrange("(t p) -> t p", t=1)).then_inc(idx_in, 16)

                @block.gpsimd
                def _(pool):
                    nc.gpsimd.memset(ident[:, :], 0.0).then_inc(id_blank, 1)
                    pool.wait_ge(id_blank, 1)
                    nc.gpsimd.affine_select(out=ident[:, :], in_=ident[:, :], compare_op=ALU.not_equal, fill=1.0,
                                            base=0, pattern=[[-1, P]], channel_multiplier=1).then_inc(id_set, 1)

                @block.vector
                def _(dve):
                    nc.vector.memset(ii[:, :, :], -1).then_inc(idx_blank, 1)
                    nc.vector.memset(two[:, :], 2.0)
                    dve.wait_ge(idx_in, 64)
                    nc.vector.tensor_copy(iF[:, :, :], ii[:, :, :]).then_inc(idx_f, 1)
                    dve.wait_ge(idx_t, 1)
                    nc.vector.tensor_copy(dstF[:, :], bank[1][:, 0:NT + 1])
                    nc.vector.tensor_copy(dstI[:, :], bank[1][:, 0:NT + 1])
                    nc.vector.tensor_copy(srcI[:, :], bank[0][:, 0:NT + 1]).then_inc(idx_done, 1)

                @block.tensor
                def _(pe):
                    pe.wait_ge(idx_f, 1)
                    pe.wait_ge(id_set, 1)
                    nc.tensor.transpose(bank[0][:, 0:P], iF[:, 0, :], ident[:, :])
                    nc.tensor.transpose(bank[1][:, 0:P], iF[:, 1, :], ident[:, :]).then_inc(idx_t, 1)

        UNITS = 13
        WHI = W[:, 0:UNITS * D].rearrange("p (u n) -> p u n", n=D)
        WLO = W[:, UNITS * D:2 * UNITS * D].rearrange("p (u n) -> p u n", n=D)

        layer0 = ctx.enter_context(ExitStack())
        WX = layer0.enter_context(nc.sbuf_tensor("WX", [P, 8, D], F32R))
        A1H, A1L = W[:, 0:8 * D].rearrange("p (k n) -> p k n", n=DH), W[:, 8 * D:16 * D].rearrange("p (k n) -> p k n", n=DH)
        A2H, A2L = W[:, 16 * D:24 * D].rearrange("p (k n) -> p k n", n=D), WX[:, :, :]

        with ExitStack() as ph:
            sb, sem = maker(ph)
            XG = sb("XG", [P, 2, TPB, D])
            GH = sb("GH", [P, 2, TPB, D], F32R)
            GL = sb("GL", [P, 2, TPB, D], F32R)
            EQ = sb("EQ", [P, 2, TPB, BLK], F32R)
            SG = sb("SG", [P, 2, TPB, D])
            zero = SG[:, 1, :, :]
            earlier = sb("earlier", [P, P])
            TM = sb("TM", [P, TPB, P])
            DR = sb("DR", [P, BLK], I32)
            own = sb("own", [P, TPB])
            prior = sb("prior", [P, TPB])
            both = sb("both", [P, TPB])
            spare = sb("spare", [P, TPB])
            off = sb("off", [P, TPB])
            move = sb("move", [P, 2, TPB])
            gidx = sb("gidx", [P, 2, TPB], I32)
            sidx = sb("sidx", [P, TPB], I32)
            zero_set, zeroed, spare_set, mask_blank, mask_set = [sem(n) for n in ("zero_set", "zeroed", "spare_set", "mask_blank", "mask_set")]
            dr_in, gidx_set, sidx_set = sem("dr_in"), sem("gidx_set"), sem("sidx_set")
            xg_in = [[sem(f"xg{s}_in{r}") for r in range(TPB)] for s in range(2)]
            gh_set, gl_set, eq_set, tm_set, dup_set, both_set, move_set, tgt_set = [
                sem(n) for n in ("gh_set", "gl_set", "eq_set", "tm_set", "dup_set", "both_set", "move_set", "tgt_set")]
            sum_done, sg_set = sem("sum_done"), sem("sg_set")
            w0_in, w0_hi, w0_lo = sem("w0_in"), sem("w0_hi"), sem("w0_lo")
            w0 = [(RAW[:, 0:8, :].rearrange("p (k h) n -> p k (h n)", h=2), A1H, A1L), (RAW[:, 0:8, :], A2H, A2L)]
            scat = [sem(f"scat0_{r}") for r in range(TPB)]

            def tile(b, r):
                return TPB * b + r + 1

            def pairs(eng, f):
                for b in range(4):
                    f(b, b % 2, b // 2)
                with eng.Fori(2, (LASTB - 1) // 2) as i:
                    f(i * 2, 0, i)
                    f(i * 2 + 1, 1, i)
                for b in range(LASTB // 2 * 2, NBLK + 1):
                    f(b, b % 2, b // 2)

            def live(b):
                return not isinstance(b, int) or 0 <= b < NBLK

            with nc.Block() as block:
                @block.sync
                def _(sp):
                    r1, r2 = RAW[:, 0:8, :].rearrange("p (k h) n -> p k (h n)", h=2), RAW[:, 0:8, :]

                    def load(b, s, h):
                        if live(b):
                            n = sum(rows_of(b))
                            wait(sp, eq_set, TPB * b)
                            sp.dma_start(DR[:, 0:n], dst[bass.ds(b * BLK, n)].partition_broadcast(P)).then_inc(dr_in, 16)
                        if b is 2:
                            sp.wait_ge(zeroed, 16 * (SEGROWS // BLK))
                            sp.dma_start(XB0, x[0:BLK, :].rearrange("(t p) d -> p t d", p=P)).then_inc(xb_in, 16)
                            sp.dma_start(r1, w1a.rearrange("(k p) n -> p k n", p=P)).then_inc(w0_in, 16)
                        if isinstance(b, int) and b == LASTB - 1:
                            sp.wait_ge(w0_lo, 1)
                            sp.dma_start(r2, w2a.rearrange("(k p) n -> p k n", p=P)).then_inc(w0_in, 16)
                    pairs(sp, load)

                @block.gpsimd
                def _(pool):
                    nc.gpsimd.memset(zero, 0.0).then_inc(zero_set, 1)

                    def gather(b, s, h):
                        rows = rows_of(b)
                        nt = len(rows)
                        for r in range(TPB):
                            wait(pool, xg_in[s][r], 16 * h)
                        nc.gpsimd.tensor_copy(gidx[:, s, 0:nt], srcI[:, bass.ds(b * TPB, nt)]).then_inc(gidx_set, 1)
                        pool.wait_ge(gidx_set, b + 1)
                        for r, n in enumerate(rows):
                            wait(pool, gl_set, tile(b - 2, r))
                            settle(pool)
                            nc.gpsimd.indirect_dma_start(XG[0:n, s, r, :], None, x[:, :],
                                                         bass.IndirectOffsetOnAxis(gidx[0:n, s, r:r + 1], 0)).then_inc(xg_in[s][r], 16)

                    def scatter(b, s):
                        rows = rows_of(b)
                        nt = len(rows)
                        for r in range(TPB):
                            wait(pool, scat[r], 16 * b)
                        pool.wait_ge(tgt_set, b + 1)
                        nc.gpsimd.tensor_copy(sidx[:, 0:nt], tgt0[:, bass.ds(b * TPB, nt)]).then_inc(sidx_set, 1)
                        pool.wait_ge(sidx_set, b + 1)
                        if b is 0:
                            pool.wait_ge(zeroed, 16 * (SEGROWS // BLK))
                        for r, n in enumerate(rows):
                            pool.wait_ge(sg_set, tile(b, r))
                            settle(pool)
                            nc.gpsimd.indirect_dma_start(seg0[:, :], bass.IndirectOffsetOnAxis(sidx[0:n, r:r + 1], 0),
                                                         SG[0:n, s, r, :], None, compute_op=ALU.add).then_inc(scat[r], 16)

                    gather(0, 0, 0)
                    nc.gpsimd.iota(spare[:, :], pattern=[[P, TPB]], base=N, channel_multiplier=1,
                                   allow_small_or_imprecise_dtypes=True).then_inc(spare_set, 1)
                    nc.gpsimd.memset(earlier[:, :], 1.0).then_inc(mask_blank, 1)
                    pool.wait_ge(mask_blank, 1)
                    nc.gpsimd.affine_select(out=earlier[:, :], in_=earlier[:, :], compare_op=ALU.is_gt, fill=0.0,
                                            base=0, pattern=[[-1, P]], channel_multiplier=1).then_inc(mask_set, 1)

                    def body(b, s, h):
                        if live(b + 1):
                            gather(b + 1, 1 - s, h + s)
                        if live(b - 1):
                            scatter(b - 1, 1 - s)
                    pairs(pool, body)
                    for r in range(TPB):
                        pool.wait_ge(scat[r], 16 * (NBLK if r < len(rows_of(LASTB)) else LASTB))

                @block.scalar
                def _(act):
                    def split(j):
                        raw, hi, lo = w0[j]
                        act.wait_ge(w0_in, 16 * (j + 1))
                        nc.scalar.copy(hi, raw).then_inc(w0_hi, 1)

                    def body(b, s, h):
                        for r in range(TPB):
                            if live(b) and r < len(rows_of(b)):
                                act.wait_ge(xg_in[s][r], 16 * h + 16)
                                wait(act, sum_done, TPB * (b - 1))
                                nc.scalar.copy(GH[:, s, r, :], XG[:, s, r, :]).then_inc(gh_set, 1)
                            if live(b - 1) and r < len(rows_of(b - 1)):
                                act.wait_ge(sum_done, tile(b - 1, r))
                                wait(act, scat[r], 16 * (b - 2))
                                nc.scalar.copy(SG[:, 1 - s, r, :], bank[4 * (1 - s) + r][:, :]).then_inc(sg_set, 1)
                        if b is 1:
                            act.wait_ge(zeroed, 16 * (SEGROWS // BLK))
                        if b is 3:
                            split(0)
                    act.wait_ge(zero_set, 1)
                    for c in range(SEGROWS // BLK):
                        act.dma_start(seg0[c * BLK:(c + 1) * BLK, :].rearrange("(p r) d -> p r d", p=P), zero).then_inc(zeroed, 16)
                    pairs(act, body)
                    split(1)

                @block.vector
                def _(dve):
                    def split(j):
                        raw, hi, lo = w0[j]
                        dve.wait_ge(w0_hi, j + 1)
                        nc.vector.tensor_tensor(lo, raw, hi.bitcast(F32), ALU.subtract).then_inc(w0_lo, 1)

                    def body(b, s, h):
                        if not live(b):
                            return
                        nt = len(rows_of(b))
                        at = bass.ds(b * TPB, nt)
                        dve.wait_ge(dr_in, 16 * b + 16)
                        wait(dve, sum_done, TPB * (b - 1))
                        for t in range(nt):
                            nc.vector.tensor_scalar(EQ[:, s, t, 0:(t + 1) * P], DR[:, 0:(t + 1) * P], dstF[:, bass.ds(b * TPB + t, 1)],
                                                    None, ALU.is_equal).then_inc(eq_set, 1)
                        for t in range(nt):
                            dve.wait_ge(eq_set, tile(b, t))
                            i = nc.vector.tensor_tensor(TM[:, t, :], EQ[:, s, t, t * P:(t + 1) * P].bitcast(F32), earlier[:, :], ALU.mult)
                        i.then_inc(tm_set, 1)
                        for t in range(1, nt):
                            nc.vector.tensor_reduce(prior[:, t:t + 1], EQ[:, s, t, 0:t * P].bitcast(F32), AX.X, ALU.max)
                        nc.vector.tensor_tensor(off[:, 0:nt], spare[:, 0:nt], dstF[:, at], ALU.subtract)
                        dve.wait_ge(tm_set, b + 1)
                        nc.vector.tensor_reduce(own[:, 0:nt], TM[:, 0:nt, :], AX.X, ALU.max).then_inc(dup_set, 1)
                        dve.wait_ge(dup_set, b + 1)
                        nc.vector.tensor_tensor(both[:, 0:nt], own[:, 0:nt], prior[:, 0:nt], ALU.max).then_inc(both_set, 1)
                        nc.vector.tensor_tensor(move[:, 1, 0:nt], off[:, 0:nt], own[:, 0:nt], ALU.mult)
                        dve.wait_ge(both_set, b + 1)
                        nc.vector.tensor_tensor(move[:, 0, 0:nt], off[:, 0:nt], both[:, 0:nt], ALU.mult).then_inc(move_set, 1)
                        dve.wait_ge(move_set, b + 1)
                        for w, tgt in enumerate((tgt0, tgt1)):
                            i = nc.vector.tensor_tensor(tgt[:, at], move[:, w, 0:nt], dstF[:, at], ALU.add)
                        i.then_inc(tgt_set, 1)
                        for r in range(nt):
                            dve.wait_ge(gh_set, tile(b, r))
                            nc.vector.tensor_tensor(GL[:, s, r, :], XG[:, s, r, :], GH[:, s, r, :].bitcast(F32), ALU.subtract).then_inc(gl_set, 1)
                        if b is 3:
                            split(0)

                    nc.vector.memset(prior[:, :], 0.0)
                    dve.wait_ge(mask_set, 1)
                    dve.wait_ge(spare_set, 1)
                    pairs(dve, body)
                    split(1)

                @block.tensor
                def _(pe):
                    def body(b, s, h):
                        if not live(b):
                            return
                        nt = len(rows_of(b))
                        pe.wait_ge(gl_set, tile(b, nt - 1))
                        pe.wait_ge(eq_set, tile(b, nt - 1))
                        for a in range(nt):
                            wait(pe, sg_set, tile(b - 2, a))
                            for t in range(a, nt):
                                same = EQ[:, s, t, a * P:(a + 1) * P]
                                nc.tensor.matmul(bank[4 * s + a][:, :], same, GH[:, s, t, :], start=t == a, stop=False)
                                last = nc.tensor.matmul(bank[4 * s + a][:, :], same, GL[:, s, t, :], start=False, stop=t == nt - 1)
                            last.then_inc(sum_done, 1)
                    pairs(pe, body)

        def mm3(acc, ah, al, bh, bl, start, stop):
            nc.tensor.matmul(acc, ah, bh, start=start, stop=False)
            nc.tensor.matmul(acc, ah, bl, start=False, stop=False)
            return nc.tensor.matmul(acc, al, bh, start=False, stop=stop)

        class Norm:
            LINKS = 4 + 3 * RSQRT_STEPS

            def __init__(self, sb, sem, name):
                self.st = sb(name + "_st", [P, TPB, 6])
                self.mv = sb(name + "_mv", [P, TPB, 2])
                self.h, self.y, self.t, self.a = [sb(name + "_" + c, [P, TPB]) for c in "hyta"]
                self.nm = sb(name + "_nm", [P, TPB])
                self.st_set, self.link, self.set = sem(name + "_st_set"), sem(name + "_link"), sem(name + "_set")

            def blank(self):
                nc.vector.memset(self.mv[:, :, :], 1.0)

            def stats(self, rows):
                return lambda r: nc.vector.bn_stats(self.st[:, r, :], rows[:, r, :])

            def rstd(self, dve, n, nt):
                settle(dve)
                for r in range(nt):
                    last = nc.vector.bn_aggr(self.mv[:, r, :], self.st[:, r, :])
                at = [self.LINKS * n]

                def link(i):
                    at[0] += 1
                    i.then_inc(self.link, 1)
                    dve.wait_ge(self.link, at[0])
                link(last)
                link(nc.vector.tensor_scalar(self.a[:, :], self.mv[:, :, 1], LN_EPS, None, ALU.add))
                nc.vector.tensor_scalar(self.h[:, :], self.a[:, :], -0.5, None, ALU.mult)
                link(nc.vector.tensor_scalar(self.t[:, :].bitcast(I32), self.a[:, :].bitcast(I32), 1, None, ALU.logical_shift_right))
                link(nc.vector.tensor_scalar(self.y[:, :].bitcast(I32), self.t[:, :].bitcast(I32), -1.0, float(0x5f3759df), ALU.mult, ALU.add))
                for _ in range(RSQRT_STEPS):
                    link(nc.vector.tensor_tensor(self.t[:, :], self.y[:, :], self.y[:, :], ALU.mult))
                    link(nc.vector.tensor_tensor(self.t[:, :], self.t[:, :], self.h[:, :], ALU.mult))
                    link(nc.vector.scalar_tensor_tensor(self.y[:, :], self.t[:, :], 1.5, self.y[:, :], ALU.add, ALU.mult))
                nc.vector.scalar_tensor_tensor(self.nm[:, :], self.mv[:, :, 0], -1.0, self.y[:, :], ALU.mult, ALU.mult).then_inc(self.set, 1)

        class Mish:

            def __init__(self, sb, sem, name, V=None):
                self.V = V if V is not None else sb(name + "V", [P, 2, D])
                self.Z, self.N, self.R = [sb(name + c, [P, 2, D]) for c in "ZNR"]
                (self.v_set, self.z_set, self.e_set, self.n_set, self.l_set, self.r_set, self.t_set, self.m_set, self.hi_set,
                 self.lo_set) = [sem(f"{name}_{c}_set") for c in ("v", "z", "e", "n", "l", "r", "t", "m", "hi", "lo")]

            def cap(self, dve, i, s, c):
                dve.wait_ge(self.v_set, i + 1)
                nc.vector.tensor_scalar(self.Z[:, s, 0:c], self.V[:, s, 0:c], ZCAP, None, ALU.min).then_inc(self.z_set, 1)

            def z_col(self, dve, i, s, ps, bias, c):
                wait(dve, self.lo_set, i - 1)
                nc.vector.tensor_scalar(self.V[:, s, 0:c], ps, bias, None, ALU.add).then_inc(self.v_set, 1)
                self.cap(dve, i, s, c)

            def z_row(self, dve, i, s, ps, bias):
                wait(dve, self.lo_set, i - 1)
                nc.vector.tensor_tensor(self.V[:, s, :], ps, bias, ALU.add).then_inc(self.v_set, 1)
                self.cap(dve, i, s, D)

            def e(self, act, i, s, c):
                act.wait_ge(self.z_set, i + 1)
                nc.scalar.activation(self.Z[:, s, 0:c], self.Z[:, s, 0:c], ACT.Exp).then_inc(self.e_set, 1)

            def n(self, dve, i, s, c):
                dve.wait_ge(self.e_set, i + 1)
                z = self.Z[:, s, 0:c]
                nc.vector.scalar_tensor_tensor(self.N[:, s, 0:c], z, 2.0, z, ALU.add, ALU.mult).then_inc(self.n_set, 1)

            def r(self, act, i, s, c):
                act.wait_ge(self.n_set, i + 1)
                nc.scalar.activation(self.R[:, s, 0:c], self.N[:, s, 0:c], ACT.Ln, bias=two[:, 0:1]).then_inc(self.l_set, 1)
                act.wait_ge(self.l_set, i + 1)
                nc.scalar.activation(self.R[:, s, 0:c], self.R[:, s, 0:c], ACT.Exp, scale=-1.0).then_inc(self.r_set, 1)

            def t(self, pool, i, s, c):
                pool.wait_ge(self.r_set, i + 1)
                nc.gpsimd.tensor_tensor(self.N[:, s, 0:c], self.N[:, s, 0:c], self.R[:, s, 0:c], ALU.mult).then_inc(self.t_set, 1)

            def m(self, dve, i, s, c):
                dve.wait_ge(self.t_set, i + 1)
                nc.vector.tensor_tensor(self.Z[:, s, 0:c], self.V[:, s, 0:c], self.N[:, s, 0:c], ALU.mult).then_inc(self.m_set, 1)

            def hi(self, act, i, s, out, c):
                act.wait_ge(self.m_set, i + 1)
                nc.scalar.copy(out, self.Z[:, s, 0:c]).then_inc(self.hi_set, 1)

            def lo(self, eng, i, s, out, hi, c):
                eng.wait_ge(self.hi_set, i + 1)
                eng.tensor_tensor(out, self.Z[:, s, 0:c], hi.bitcast(F32), ALU.subtract).then_inc(self.lo_set, 1)

        class Turn:

            def __init__(self, sem, name):
                self.done, self.hi_set, self.lo_set = sem(name + "_done"), sem(name + "_hi"), sem(name + "_lo")

            def pe(self, pe, i, b, rows_buf, ks, new, at=0):
                for j, k in enumerate(ks):
                    if at == 0:
                        wait(pe, self.lo_set, i if new else i + j - 1)
                    for r, n in enumerate(rows_of(b)):
                        last = nc.tensor.transpose(bank[at + j][:, r * P:r * P + n], rows_buf[0:n, r, k * P:(k + 1) * P], ident[0:n, 0:n])
                    last.then_inc(self.done, 1)

            def hi(self, act, i, b, XH, ks, at=0):
                c = sum(rows_of(b))
                for j, k in enumerate(ks):
                    act.wait_ge(self.done, i + j + 1)
                    nc.scalar.copy(XH[:, k, 0:c], bank[at + j][:, 0:c]).then_inc(self.hi_set, 1)

            def lo(self, dve, i, b, XH, XL, ks, at=0):
                c = sum(rows_of(b))
                for j, k in enumerate(ks):
                    dve.wait_ge(self.hi_set, i + j + 1)
                    nc.vector.tensor_tensor(XL[:, k, 0:c], bank[at + j][:, 0:c], XH[:, k, 0:c].bitcast(F32), ALU.subtract).then_inc(self.lo_set, 1)

        HBANK, YBANK = [bank[2], bank[3]], bank[4:8]

        def load_rows(eng, buf, dram, b, sem_):
            at = 0
            for n, t0, t1 in spans_of(b):
                c = n * (t1 - t0)
                eng.dma_start(buf[0:n, t0:t1, :], dram[bass.ds(b * BLK + at, c), :].rearrange("(t p) d -> p t d", p=n)).then_inc(sem_, 16)
                at += c

        def store_rows(eng, buf, dram, b, sem_):
            at = 0
            for n, t0, t1 in spans_of(b):
                c = n * (t1 - t0)
                eng.dma_start(dram[bass.ds(b * BLK + at, c), :].rearrange("(t p) d -> p t d", p=n), buf[0:n, t0:t1, :]).then_inc(sem_, 16)
                at += c

        def loaded(b):
            return 16 * (b + ndma(b))

        with ExitStack() as ph:
            sb, sem = maker(ph)
            XB, RS, YX = [sb(n, [P, TPB, D]) for n in ("XB", "RS", "YX")]
            XH, XL = [sb(n, [P, KD, BLK], F32R) for n in ("XH", "XL")]
            HH, HL = [sb(n, [P, KH, BLK], F32R) for n in ("HH", "HL")]
            HF = sb("HF", [P, 2, BLK])
            b1c, b2r, eps1, zb = sb("b1c", [P, KH]), sb("b2r", [P, D]), sb("eps1", [P, 1]), sb("zb", [P, TPB, D])
            norm = Norm(sb, sem, "n0")
            turn = Turn(sem, "t0")
            cst, e1_set, zb_set, zeroed = sem("cst0"), sem("e1_set"), sem("zb_set"), sem("zeroed1")
            rs_in, yx_in, y_out = sem("rs_in"), sem("yx_in"), sem("y_out")
            rst_set, h_done, f_set, hi_set, lo_set = [sem("a_" + n) for n in ("rst_set", "h_done", "f_set", "hi_set", "lo_set")]
            y_done, y_read, x2_set, yp_set, y_set = [sem("a_" + n) for n in ("y_done", "y_read", "x2_set", "yp_set", "y_set")]
            TS = KD

            with nc.Block() as block:
                @block.sync
                def _(sp):
                    def load(b):
                        if b is not 0:
                            sp.wait_ge(rst_set, b)
                            load_rows(sp, XB, x, b, xb_in)
                        wait(sp, turn.done, TS * b)
                        load_rows(sp, RS, seg0, b, rs_in)

                    def loady(b):
                        load_rows(sp, YX, x, b, yx_in)

                    def store(b):
                        sp.wait_ge(y_set, b + 1)
                        store_rows(sp, YX, x1, b, y_out)
                        sp.wait_ge(y_out, loaded(b))

                    load(0)
                    with nc.allow_non_contiguous_dma(reason="a bias as a column"):
                        sp.dma_start(b1c[:, :], b1a.rearrange("(k p) -> p k", p=P)).then_inc(cst, 16)
                    sp.dma_start(b2r[:, :], b2a.partition_broadcast(P)).then_inc(cst, 16)
                    sp.dma_start(eps1[:, :], eps.partition_broadcast(P)).then_inc(cst, 16)
                    load(1)
                    loady(0)
                    sp.dma_start(RAW[:, 0:8, :], w1[0:8 * P, :].rearrange("(k p) n -> p k n", p=P)).then_inc(raw1_in, 16)
                    for half in range(2):
                        sp.dma_start(RAW[half * DE:(half + 1) * DE, 8, :], w1[8 * P:8 * P + DE, :]).then_inc(raw1_in, 16)
                    sp.dma_start(RAW[:, 9:13, :], w2.rearrange("(k p) n -> p k n", p=P)).then_inc(raw1_in, 16)
                    sp.wait_ge(zb_set, 1)
                    sp.dma_start(seg1[NBLK * BLK:SEGROWS, :].rearrange("(p r) d -> p r d", p=P), zb[:, :, :]).then_inc(zeroed, 16)

                    def body(b):
                        if b is not LASTB:
                            load(b + 1)
                        sp.dma_start(seg1[bass.ds((b - 1) * BLK, BLK), :].rearrange("(p r) d -> p r d", p=P), zb[:, :, :]).then_inc(zeroed, 16)
                        store(b - 1)
                        loady(b)
                    with sp.Fori(1, LASTB - 1) as b:
                        body(b)
                    body(LASTB - 1)
                    body(LASTB)
                    sp.dma_start(seg1[LASTB * BLK:NBLK * BLK, :].rearrange("(p r) d -> p r d", p=P), zb[:, :, :]).then_inc(zeroed, 16)
                    store(LASTB)
                    sp.wait_ge(zeroed, 16 * (NBLK + 1))

                @block.tensor
                def _(pe):
                    def first(b):
                        c = sum(rows_of(b))
                        for m in range(KH):
                            wait(pe, f_set, KH * b + m - 1)
                            if b is 0 and m == 0:
                                pe.wait_ge(turn.lo_set, 4)
                            for k in range(KD):
                                pe.wait_ge(turn.lo_set, TS * b + k + 1)
                                last = mm3(HBANK[m % 2][:, 0:c], A1H[:, k, m * P:(m + 1) * P], A1L[:, k, m * P:(m + 1) * P],
                                           XH[:, k, 0:c], XL[:, k, 0:c], k == 0, k == KD - 1)
                            last.then_inc(h_done, 1)

                    def turns(b, j):
                        pe.wait_ge(rst_set, b + 1)
                        turn.pe(pe, TS * b + 2 * j, b, RS, (2 * j, 2 * j + 1), j == 0, 2 * j if b is 0 else 0)

                    def second(b, ks):
                        for k in ks:
                            pe.wait_ge(lo_set, KH * b + k + 1)
                            for r in range(len(rows_of(b))):
                                if k == 0:
                                    wait(pe, y_read, TPB * (b - 1) + r + 1)
                                rows = slice(r * P, (r + 1) * P)
                                last = mm3(YBANK[r][:, :], HH[:, k, rows], HL[:, k, rows], A2H[:, k, :], A2L[:, k, :],
                                           k == 0, k == KH - 1)
                                if k == KH - 1:
                                    last.then_inc(y_done, 1)

                    def body(b):
                        first(b)
                        nxt = b is not LASTB
                        if nxt:
                            turns(b + 1, 0)
                        second(b, range(0, KH // 2))
                        if nxt:
                            turns(b + 1, 1)
                        second(b, range(KH // 2, KH))

                    turns(0, 0)
                    turns(0, 1)
                    body(0)
                    with pe.Fori(1, LASTB - 1) as b:
                        body(b)
                    body(LASTB - 1)
                    body(LASTB)

                @block.scalar
                def _(act):
                    act.wait_ge(cst, 48)

                    def turns(b, j):
                        turn.hi(act, TS * b + 2 * j, b, XH, (2 * j, 2 * j + 1), 2 * j if b is 0 else 0)

                    def body(b):
                        c = sum(rows_of(b))
                        for m in range(KH):
                            act.wait_ge(h_done, KH * b + m + 1)
                            wait(act, lo_set, KH * b + m - 1)
                            nc.scalar.activation(HF[:, m % 2, 0:c], HBANK[m % 2][:, 0:c], ACT.Relu, bias=b1c[:, m:m + 1]).then_inc(f_set, 1)
                            act.wait_ge(f_set, KH * b + m + 1)
                            nc.scalar.copy(HH[:, m, 0:c], HF[:, m % 2, 0:c]).then_inc(hi_set, 1)
                        if b is not LASTB:
                            turns(b + 1, 0)
                            turns(b + 1, 1)

                    turns(0, 0)
                    turns(0, 1)
                    body(0)
                    with act.Fori(1, LASTB - 1) as b:
                        body(b)
                    body(LASTB - 1)
                    body(LASTB)

                @block.gpsimd
                def _(pool):
                    nc.gpsimd.memset(zb[:, :, :], 0.0).then_inc(zb_set, 1)
                    pool.wait_ge(cst, 48)

                    def prep(b):
                        nt = len(rows_of(b))
                        pool.wait_ge(yx_in, loaded(b))
                        nc.gpsimd.tensor_tensor(YX[:, 0:nt, :], YX[:, 0:nt, :], YX[:, 0:nt, :], ALU.add).then_inc(x2_set, 1)
                        pool.wait_ge(x2_set, b + 1)
                        for r in range(nt):
                            i = nc.gpsimd.tensor_tensor(YX[:, r, :], YX[:, r, :], b2r[:, :], ALU.add)
                        i.then_inc(yp_set, 1)

                    def body(b):
                        c = sum(rows_of(b))
                        for m in range(KH):
                            pool.wait_ge(hi_set, KH * b + m + 1)
                            nc.gpsimd.tensor_tensor(HL[:, m, 0:c], HF[:, m % 2, 0:c], HH[:, m, 0:c].bitcast(F32), ALU.subtract).then_inc(lo_set, 1)
                        prep(b)
                    blocks(pool, body)

                @block.vector
                def _(dve):
                    norm.blank()
                    dve.wait_ge(cst, 48)
                    nc.vector.tensor_scalar(eps1[:, :], eps1[:, :], 1.0, None, ALU.add).then_inc(e1_set, 1)
                    dve.wait_ge(e1_set, 1)

                    def rst(b):
                        dve.wait_ge(xb_in, loaded(b))
                        dve.wait_ge(rs_in, loaded(b))
                        for n, t0, t1 in spans_of(b):
                            xb = XB0 if b is 0 else XB
                            i = nc.vector.scalar_tensor_tensor(RS[0:n, t0:t1, :], xb[0:n, t0:t1, :], eps1[0:n, 0:1], RS[0:n, t0:t1, :], ALU.mult, ALU.add)
                        i.then_inc(rst_set, 1)

                    def turns(b, j):
                        turn.lo(dve, TS * b + 2 * j, b, XH, XL, (2 * j, 2 * j + 1), 2 * j if b is 0 else 0)

                    def ys(b):
                        nt = len(rows_of(b))
                        dve.wait_ge(yp_set, b + 1)
                        stats = norm.stats(YX)
                        for r in range(nt):
                            dve.wait_ge(y_done, TPB * b + r + 1)
                            nc.vector.tensor_tensor(YX[:, r, :], YBANK[r][:, :], YX[:, r, :], ALU.add).then_inc(y_read, 1)
                            if r:
                                dve.wait_ge(y_read, TPB * b + r)
                                stats(r - 1)
                        dve.wait_ge(y_read, TPB * b + nt)
                        stats(nt - 1).then_inc(norm.st_set, 1)
                        dve.wait_ge(norm.st_set, b + 1)
                        norm.rstd(dve, b, nt)
                        for r in range(nt):
                            i = nc.vector.tensor_scalar(YX[:, r, :], YX[:, r, :], norm.mv[:, r, 0:1], norm.y[:, r:r + 1], ALU.subtract, ALU.mult)
                        i.then_inc(y_set, 1)

                    rst(0)
                    turns(0, 0)
                    turns(0, 1)

                    def body(b):
                        if b is not 0:
                            ys(b - 1)
                        if b is not LASTB:
                            rst(b + 1)
                            turns(b + 1, 0)
                            turns(b + 1, 1)
                    body(0)
                    with dve.Fori(1, LASTB - 1) as b:
                        body(b)
                    body(LASTB - 1)
                    body(LASTB)
                    ys(LASTB)
        layer0.close()

        with ExitStack() as ph:
            sb, sem = maker(ph)
            UE, U2 = 8, 9
            TS = 2 * KD + 1
            STEPS = KD
            XH, XL = [sb("e" + n, [P, 2 * KD, BLK], F32R) for n in ("XH", "XL")]
            ES = sb("ES", [P, BLK], F32R)
            G = [sb(n, [P, TPB, D]) for n in ("GS", "GD")]
            EB = sb("EB", [P, TPB, 2, DE])
            HH, HL = [sb("e" + n, [P, KD, BLK], F32R) for n in ("HH", "HL")]
            MH, ML = [sb(n, [P, TPB, D], F32R) for n in ("MH", "ML")]
            SG = sb("eSG", [P, TPB, D])
            EQ = sb("eEQ", [P, TPB, P], F32R)
            DR = sb("eDR", [P, BLK], I32)
            b1c, b2r = sb("eb1c", [P, KD]), sb("eb2r", [P, D])
            gidx, sidx = sb("egidx", [P, 2, TPB], I32), sb("esidx", [P, TPB], I32)
            hid, msg = Mish(sb, sem, "hid", RAW[:, 11:13, :]), Mish(sb, sem, "msg")
            turn = Turn(sem, "t1")
            cst, eb_in, dr_in, gidx_set, sidx_set = [sem("e_" + n) for n in ("cst", "eb_in", "dr_in", "gidx_set", "sidx_set")]
            g_in = [[sem(f"g{j}_in{r}") for r in range(TPB)] for j in range(2)]
            scat = [sem(f"scat1_{r}") for r in range(TPB)]
            w_hi, w_lo, w2_hi = sem("e_w_hi"), sem("e_w_lo"), sem("e_w2_hi")
            h_done, y_done, s_done, sg_set, eq_set, msg_read = [sem("e_" + n) for n in ("h_done", "y_done", "s_done", "sg_set", "eq_set", "msg_read")]
            CHUNKS = [(0, 3), (3, 6), (6, 9), (9, 13)]
            CHUNKS2 = [(0, 3), (3, 6), (6, 9), (9, 12)]

            def hi_(b, m):
                return KD * b + m

            def qi_(b, r):
                return TPB * b + r

            def turn_src(i):
                return G[i // 2], (2 * (i % 2), 2 * (i % 2) + 1), (2 * i, 2 * i + 1)

            def loop(eng, f):
                f(0)
                f(1)
                f(2)
                with eng.Fori(3, LASTB - 1) as b:
                    f(b)
                for b in range(LASTB - 1, NBLK + 1):
                    f(b)

            def live(b):
                return not isinstance(b, int) or 0 <= b < NBLK

            with nc.Block() as block:
                @block.sync
                def _(sp):
                    with nc.allow_non_contiguous_dma(reason="a bias as a column"):
                        sp.dma_start(b1c[:, :], b1.rearrange("(k p) -> p k", p=P)).then_inc(cst, 16)
                    sp.dma_start(b2r[:, :], b2.partition_broadcast(P)).then_inc(cst, 16)

                    def attrs(b):
                        at = 0
                        for n, t0, t1 in spans_of(b):
                            c = n * (t1 - t0)
                            for j in range(2):
                                sp.dma_start(EB[0:n, t0:t1, j, :], edge_attr[bass.ds(b * BLK + at, c), :].rearrange("(t p) d -> p t d", p=n)).then_inc(eb_in, 16)
                            at += c

                    def body(b):
                        if live(b + 1):
                            wait(sp, turn.done, TS * (b + 1))
                            attrs(b + 1)
                        if live(b):
                            wait(sp, eq_set, TPB * b)
                            n = sum(rows_of(b))
                            sp.dma_start(DR[:, 0:n], dst[bass.ds(b * BLK, n)].partition_broadcast(P)).then_inc(dr_in, 16)
                        if b is 0:
                            sp.wait_ge(w_lo, len(CHUNKS))
                            sp.dma_start(RAW[:, 0:8, :], w3.rearrange("(k p) n -> p k n", p=P)).then_inc(raw2_in, 16)
                            sp.dma_start(RAW[:, 8:11, :], w4[0:3 * P, :].rearrange("(k p) n -> p k n", p=P)).then_inc(raw2_in, 16)
                    attrs(0)
                    loop(sp, body)
                    sp.wait_ge(hid.m_set, KD * NBLK)
                    sp.dma_start(RAW[:, 11, :], w4[3 * P:4 * P, :]).then_inc(raw2_in, 16)

                @block.gpsimd
                def _(pool):
                    pool.wait_ge(raw1_in, 64)

                    def stage_idx(b):
                        nt = len(rows_of(b))
                        for j in range(2):
                            for r in range(TPB):
                                wait(pool, g_in[j][r], 16 * b)
                            i = nc.gpsimd.tensor_copy(gidx[:, j, 0:nt], (srcI, dstI)[j][:, bass.ds(b * TPB, nt)])
                        i.then_inc(gidx_set, 1)

                    def gather(b, j, r):
                        rows = rows_of(b)
                        if r >= len(rows):
                            return
                        n = rows[r]
                        if r == 0:
                            wait(pool, turn.done, TS * (b - 1) + KD * (j + 1))
                            pool.wait_ge(gidx_set, b + 1)
                            settle(pool)
                        nc.gpsimd.indirect_dma_start(G[j][0:n, r, :], None, x1[:, :],
                                                     bass.IndirectOffsetOnAxis(gidx[0:n, j, r:r + 1], 0)).then_inc(g_in[j][r], 16)

                    def scatter(b, r):
                        rows = rows_of(b)
                        if r >= len(rows):
                            return
                        n = rows[r]
                        if r == 0:
                            wait(pool, scat[TPB - 1], 16 * b)
                            nc.gpsimd.tensor_copy(sidx[:, 0:len(rows)], tgt1[:, bass.ds(b * TPB, len(rows))]).then_inc(sidx_set, 1)
                            pool.wait_ge(sidx_set, b + 1)
                        else:
                            pool.wait_ge(scat[r - 1], 16 * (b + 1))
                        pool.wait_ge(sg_set, qi_(b, r) + 1)
                        settle(pool)
                        nc.gpsimd.indirect_dma_start(seg1[:, :], bass.IndirectOffsetOnAxis(sidx[0:n, r:r + 1], 0),
                                                     SG[0:n, r, :], None, compute_op=ALU.add).then_inc(scat[r], 16)

                    def hid_t(b, m):
                        if live(b):
                            hid.t(pool, hi_(b, m), m % 2, sum(rows_of(b)))

                    def hid_lo(b, m):
                        if live(b):
                            c = sum(rows_of(b))
                            hid.lo(pool, hi_(b, m), m % 2, HL[:, m, 0:c], HH[:, m, 0:c], c)

                    def msg_t(b, r):
                        if live(b) and r < len(rows_of(b)):
                            msg.t(pool, qi_(b, r), r % 2, D)

                    def body(b):
                        nxt = live(b + 1)

                        def g(j, r):
                            if nxt:
                                gather(b + 1, j, r)

                        def sc(blk, r):
                            if live(blk):
                                scatter(blk, r)
                        if nxt:
                            stage_idx(b + 1)
                        g(0, 0)
                        msg_t(b - 1, 0)
                        g(0, 1)
                        msg_t(b - 1, 1)
                        g(0, 2)
                        sc(b - 2, 3)
                        hid_t(b, 0)
                        g(0, 3)
                        g(1, 0)
                        msg_t(b - 1, 2)
                        hid_lo(b, 0)
                        hid_t(b, 1)
                        g(1, 1)
                        msg_t(b - 1, 3)
                        hid_lo(b, 1)
                        g(1, 2)
                        hid_t(b, 2)
                        g(1, 3)
                        sc(b - 1, 0)
                        hid_t(b, 3)
                        hid_lo(b, 2)
                        sc(b - 1, 1)
                        hid_lo(b, 3)
                        sc(b - 1, 2)

                    stage_idx(0)
                    for j in range(2):
                        for r in range(TPB):
                            gather(0, j, r)
                    for n, (u0, u1) in enumerate(CHUNKS):
                        if n % 2:
                            pool.wait_ge(w_hi, n + 1)
                            nc.gpsimd.tensor_tensor(WLO[:, u0:u1, :], RAW[:, u0:u1, :], WHI[:, u0:u1, :].bitcast(F32), ALU.subtract).then_inc(w_lo, 1)
                    loop(pool, body)
                    for r in range(TPB):
                        pool.wait_ge(scat[r], 16 * (NBLK if r < len(rows_of(LASTB)) else LASTB))

                @block.scalar
                def _(act):
                    nc.scalar.preload_act_table_set("natural_log_exp_and_others")
                    act.wait_ge(raw1_in, 64)
                    for u0, u1 in CHUNKS:
                        nc.scalar.copy(WHI[:, u0:u1, :], RAW[:, u0:u1, :]).then_inc(w_hi, 1)

                    def turns(b, i):
                        if live(b):
                            turn.hi(act, TS * b + 2 * i, b, XH, turn_src(i)[2], 2 * i if b is 0 else 0)

                    def attr_hi(b):
                        if live(b):
                            c = sum(rows_of(b))
                            act.wait_ge(turn.done, TS * b + TS)
                            nc.scalar.copy(ES[:, 0:c], bank[0][:, 0:c]).then_inc(turn.hi_set, 1)

                    def h_(f, b, m):
                        if live(b):
                            c = sum(rows_of(b))
                            if f == "hi":
                                hid.hi(act, hi_(b, m), m % 2, HH[:, m, 0:c], c)
                            else:
                                (hid.e if f == "e" else hid.r)(act, hi_(b, m), m % 2, c)

                    def q_(f, b, r):
                        if live(b) and r < len(rows_of(b)):
                            if f == "hi":
                                msg.hi(act, qi_(b, r), r % 2, MH[:, r, :], D)
                            else:
                                (msg.e if f == "e" else msg.r)(act, qi_(b, r), r % 2, D)

                    def sums(b, r):
                        if live(b) and r < len(rows_of(b)):
                            act.wait_ge(s_done, qi_(b, r) + 1)
                            wait(act, scat[r], 16 * b)
                            nc.scalar.copy(SG[:, r, :], bank[r % 2][:, :]).then_inc(sg_set, 1)

                    def next_w(b, n):
                        if b is NBLK:
                            if n == 0:
                                act.wait_ge(y_done, qi_(LASTB, len(rows_of(LASTB))))
                                act.wait_ge(raw2_in, 48)
                            u0, u1 = CHUNKS2[n]
                            nc.scalar.copy(WHI[:, u0:u1, :], RAW[:, u0:u1, :]).then_inc(w2_hi, 1)

                    def body(b):
                        q_("e", b - 1, 0)
                        q_("r", b - 1, 0)
                        next_w(b, 0)
                        q_("e", b - 1, 1)
                        attr_hi(b)
                        q_("r", b - 1, 1)
                        q_("hi", b - 1, 0)
                        next_w(b, 1)
                        h_("e", b, 0)
                        h_("r", b, 0)
                        q_("hi", b - 1, 1)
                        q_("e", b - 1, 2)
                        q_("r", b - 1, 2)
                        h_("hi", b, 0)
                        h_("e", b, 1)
                        sums(b - 1, 0)
                        next_w(b, 2)
                        sums(b - 1, 1)
                        h_("r", b, 1)
                        q_("hi", b - 1, 2)
                        q_("e", b - 1, 3)
                        q_("r", b - 1, 3)
                        h_("hi", b, 1)
                        h_("e", b, 2)
                        sums(b - 1, 2)
                        next_w(b, 3)
                        h_("r", b, 2)
                        q_("hi", b - 1, 3)
                        h_("e", b, 3)
                        turns(b + 1, 0)
                        h_("r", b, 3)
                        h_("hi", b, 2)
                        turns(b + 1, 1)
                        h_("hi", b, 3)
                        turns(b + 1, 2)
                        turns(b + 1, 3)
                        sums(b - 1, 3)

                    for i in range(STEPS):
                        turns(0, i)
                    loop(act, body)

                @block.vector
                def _(dve):
                    nc.vector.memset(WLO[DE:P, UE, :].bitcast(F32), 0.0)
                    for n, (u0, u1) in enumerate(CHUNKS):
                        if n % 2 == 0:
                            dve.wait_ge(w_hi, n + 1)
                            if u1 == UE + 1:
                                nc.vector.tensor_tensor(WLO[:, u0:UE, :], RAW[:, u0:UE, :], WHI[:, u0:UE, :].bitcast(F32), ALU.subtract)
                                nc.vector.tensor_tensor(WLO[0:DE, UE, :], RAW[0:DE, UE, :], WHI[0:DE, UE, :].bitcast(F32), ALU.subtract).then_inc(w_lo, 1)
                            else:
                                nc.vector.tensor_tensor(WLO[:, u0:u1, :], RAW[:, u0:u1, :], WHI[:, u0:u1, :].bitcast(F32), ALU.subtract).then_inc(w_lo, 1)

                    def turns(b, i):
                        if live(b):
                            turn.lo(dve, TS * b + 2 * i, b, XH, XL, turn_src(i)[2], 2 * i if b is 0 else 0)

                    def attr_lo(b):
                        if live(b):
                            c = sum(rows_of(b))
                            dve.wait_ge(turn.hi_set, TS * b + TS)
                            nc.vector.tensor_tensor(ES[DE:P, 0:c], bank[0][DE:P, 0:c], ES[DE:P, 0:c].bitcast(F32), ALU.subtract).then_inc(turn.lo_set, 1)

                    def h_z(b, m):
                        if live(b):
                            c = sum(rows_of(b))
                            dve.wait_ge(h_done, hi_(b, m) + 1)
                            hid.z_col(dve, hi_(b, m), m % 2, HBANK[m % 2][:, 0:c], b1c[:, m:m + 1], c)

                    def h_n(b, m):
                        if live(b):
                            hid.n(dve, hi_(b, m), m % 2, sum(rows_of(b)))

                    def h_m(b, m):
                        if live(b):
                            hid.m(dve, hi_(b, m), m % 2, sum(rows_of(b)))

                    def q_z(b, r):
                        if live(b) and r < len(rows_of(b)):
                            dve.wait_ge(y_done, qi_(b, r) + 1)
                            msg.z_row(dve, qi_(b, r), r % 2, YBANK[r][:, :], b2r[:, :])

                    def q_n(b, r):
                        if live(b) and r < len(rows_of(b)):
                            msg.n(dve, qi_(b, r), r % 2, D)

                    def q_m(b, r):
                        if live(b) and r < len(rows_of(b)):
                            msg.m(dve, qi_(b, r), r % 2, D)

                    def q_lo(b, r):
                        if live(b) and r < len(rows_of(b)):
                            msg.lo(nc.vector, qi_(b, r), r % 2, ML[:, r, :], MH[:, r, :], D)

                    def same(b):
                        if live(b):
                            dve.wait_ge(dr_in, 16 * (b + 1))
                            wait(dve, s_done, TPB * b)
                            for r in range(len(rows_of(b))):
                                nc.vector.tensor_scalar(EQ[:, r, :], DR[:, r * P:(r + 1) * P], dstF[:, bass.ds(b * TPB + r, 1)], None, ALU.is_equal).then_inc(eq_set, 1)

                    def next_w(b, n):
                        if b is NBLK:
                            u0, u1 = CHUNKS2[n]
                            dve.wait_ge(w2_hi, n + 1)
                            nc.vector.tensor_tensor(WLO[:, u0:u1, :], RAW[:, u0:u1, :], WHI[:, u0:u1, :].bitcast(F32), ALU.subtract)

                    def body(b):
                        q_z(b - 1, 0)
                        q_n(b - 1, 0)
                        q_z(b - 1, 1)
                        attr_lo(b)
                        q_n(b - 1, 1)
                        q_m(b - 1, 0)
                        h_z(b, 0)
                        q_lo(b - 1, 0)
                        h_n(b, 0)
                        q_m(b - 1, 1)
                        same(b - 1)
                        q_z(b - 1, 2)
                        q_lo(b - 1, 1)
                        next_w(b, 0)
                        q_n(b - 1, 2)
                        h_m(b, 0)
                        h_z(b, 1)
                        h_n(b, 1)
                        q_m(b - 1, 2)
                        q_z(b - 1, 3)
                        q_lo(b - 1, 2)
                        for n in range(1, len(CHUNKS2)):
                            next_w(b, n)
                        q_n(b - 1, 3)
                        h_m(b, 1)
                        h_z(b, 2)
                        h_n(b, 2)
                        q_m(b - 1, 3)
                        h_z(b, 3)
                        q_lo(b - 1, 3)
                        h_m(b, 2)
                        h_n(b, 3)
                        turns(b + 1, 0)
                        h_m(b, 3)
                        turns(b + 1, 1)
                        turns(b + 1, 2)
                        turns(b + 1, 3)

                    for i in range(STEPS):
                        turns(0, i)
                    dve.wait_ge(cst, 32)
                    loop(dve, body)

                @block.tensor
                def _(pe):
                    def turns(b, i):
                        if not live(b):
                            return
                        buf, ks, _ = turn_src(i)
                        if i % 2 == 0:
                            for r in range(len(rows_of(b))):
                                pe.wait_ge(g_in[i // 2][r], 16 * (b + 1))
                        if i == 0:
                            wait(pe, sg_set, qi_(b - 2, 2) + 1 if live(b - 2) else 0)
                        turn.pe(pe, TS * b + 2 * i, b, buf, ks, i == 0, 2 * i if b is 0 else 0)

                    def attr_turn(b):
                        if live(b):
                            pe.wait_ge(eb_in, 2 * loaded(b))
                            wait(pe, turn.lo_set, TS * b + TS - 1)
                            for r, n in enumerate(rows_of(b)):
                                last = nc.tensor.transpose(bank[0][:, r * P:r * P + n], EB[0:n, r, :, :].rearrange("p j d -> p (j d)"), ident[0:n, 0:n])
                            last.then_inc(turn.done, 1)

                    def first(b, m, ks=(0, 2 * KD)):
                        if live(b):
                            c = sum(rows_of(b))
                            cols = slice(m * P, (m + 1) * P)
                            acc = HBANK[m % 2][:, 0:c]
                            if ks[0] == 0:
                                wait(pe, hid.v_set, hi_(b, m) - 1)
                            if b is 0 and m == 0:
                                pe.wait_ge(turn.lo_set, 4)
                            for k in range(*ks):
                                if m == 0:
                                    pe.wait_ge(turn.lo_set, TS * b + k + 1)
                                mm3(acc, WHI[:, k, cols], WLO[:, k, cols], XH[:, k, 0:c], XL[:, k, 0:c], k == 0, False)
                            if ks[1] < 2 * KD:
                                return
                            if m == 0:
                                pe.wait_ge(turn.lo_set, TS * b + TS)
                            nc.tensor.matmul(acc, WHI[:, UE, cols], ES[:, 0:c], start=False, stop=False)
                            nc.tensor.matmul(acc, WLO[:, UE, cols], ES[:, 0:c], start=False, stop=True).then_inc(h_done, 1)

                    def second(b, k):
                        if not live(b):
                            return
                        pe.wait_ge(hid.lo_set, hi_(b, k) + 1)
                        for r in range(len(rows_of(b))):
                            if k == 0:
                                wait(pe, msg.v_set, qi_(b - 1, r) + 1)
                            rows = slice(r * P, (r + 1) * P)
                            last = mm3(YBANK[r][:, :], HH[:, k, rows], HL[:, k, rows], WHI[:, U2 + k, :], WLO[:, U2 + k, :], k == 0, k == KD - 1)
                            if k == KD - 1:
                                last.then_inc(y_done, 1)

                    def sums(b, r):
                        if live(b) and r < len(rows_of(b)):
                            pe.wait_ge(msg.lo_set, qi_(b, r) + 1)
                            pe.wait_ge(eq_set, qi_(b, r) + 1)
                            if r == 3:
                                if live(b + 2):
                                    pe.wait_ge(turn.lo_set, TS * (b + 2) + TS - 1)
                            else:
                                wait(pe, sg_set, qi_(b, r) - 1)
                            acc = bank[r % 2][:, :]
                            nc.tensor.matmul(acc, EQ[:, r, :], MH[:, r, :], start=True, stop=False)
                            nc.tensor.matmul(acc, EQ[:, r, :], ML[:, r, :], start=False, stop=True).then_inc(s_done, 1)

                    def body(b):
                        first(b, 0)
                        first(b, 1)
                        sums(b - 1, 0)
                        first(b, 2, (0, KD))
                        sums(b - 1, 1)
                        first(b, 2, (KD, 2 * KD))
                        first(b, 3, (0, KD))
                        sums(b - 1, 2)
                        first(b, 3, (KD, 2 * KD))
                        for k in range(KD):
                            turns(b + 1, k)
                            second(b, k)
                        attr_turn(b + 1)
                        sums(b - 1, 3)

                    for i in range(STEPS):
                        turns(0, i)
                    attr_turn(0)
                    pe.wait_ge(w_lo, len(CHUNKS))
                    loop(pe, body)

        with ExitStack() as ph:
            sb, sem = maker(ph)
            U4 = 8
            TS = 2 * KD
            STEPS = KD
            ROWS = [sb(n, [P, TPB, D]) for n in ("NB", "AB")]
            YX, YO, Y, OUT = [sb("n" + n, [P, TPB, D]) for n in ("YX", "YO", "Y", "OUT")]
            XH, XL = [sb("n" + n, [P, 2 * KD, BLK], F32R) for n in ("XH", "XL")]
            HH, HL = [sb("n" + n, [P, KD, BLK], F32R) for n in ("HH", "HL")]
            b3c, b4r, gam, bet = sb("b3c", [P, KD]), sb("b4r", [P, D]), sb("gam", [P, D]), sb("bet", [P, D])
            hid = Mish(sb, sem, "nhid")
            norm, norm2 = Norm(sb, sem, "n1"), Norm(sb, sem, "n2")
            turn = Turn(sem, "t2")
            cst, yx_in, y_out = [sem("n_" + n) for n in ("cst", "yx_in", "y_out")]
            rows_in = [sem(f"n_rows{j}_in") for j in range(2)]
            h_done, y_done, y_read, yo_set, yx_set, y_set, g_set, s_set, norm_set = [
                sem("n_" + n) for n in ("h_done", "y_done", "y_read", "yo_set", "yx_set", "y_set", "g_set", "s_set", "norm_set")]

            def hi_(b, m):
                return KD * b + m

            def turn_src(i):
                return ROWS[i // 2], (2 * (i % 2), 2 * (i % 2) + 1), (2 * i, 2 * i + 1)

            def loop(eng, f):
                f(0)
                f(1)
                with eng.Fori(2, LASTB - 1) as b:
                    f(b)
                for b in range(LASTB - 1, NBLK + 1):
                    f(b)

            def live(b):
                return not isinstance(b, int) or 0 <= b < NBLK

            def rows_done(b, r=None):
                return TPB * b + (len(rows_of(b)) if r is None else r + 1)

            with nc.Block() as block:
                @block.sync
                def _(sp):
                    def load(b):
                        for j, a in enumerate((x1, seg1)):
                            wait(sp, turn.done, TS * (b - 1) + KD * (j + 1))
                            if j == 0:
                                settle(sp)
                                wait(sp, yo_set, b)
                            settle(sp)
                            load_rows(sp, ROWS[j], a, b, rows_in[j])

                    def body(b):
                        if live(b + 1):
                            load(b + 1)
                        if live(b - 1) and live(b):
                            sp.wait_ge(s_set, rows_done(b - 1))
                            settle(sp)
                            load_rows(sp, YX, x1, b, yx_in)
                        if live(b - 1):
                            sp.wait_ge(y_set, rows_done(b - 1))
                            store_rows(sp, OUT, out, b - 1, y_out)
                    load(0)
                    with nc.allow_non_contiguous_dma(reason="a bias as a column"):
                        sp.dma_start(b3c[:, :], b3.rearrange("(k p) -> p k", p=P)).then_inc(cst, 16)
                    for row, a in ((b4r, b4), (gam, gamma), (bet, beta)):
                        sp.dma_start(row[:, :], a.partition_broadcast(P)).then_inc(cst, 16)
                    load_rows(sp, YX, x1, 0, yx_in)
                    loop(sp, body)
                    sp.wait_ge(y_out, loaded(LASTB))

                @block.gpsimd
                def _(pool):
                    pool.wait_ge(cst, 64)

                    def with_b4(b):
                        if live(b):
                            pool.wait_ge(rows_in[0], loaded(b))
                            for r in range(len(rows_of(b))):
                                wait(pool, y_read, rows_done(b - 1, r))
                                i = nc.gpsimd.tensor_tensor(YO[:, r, :], ROWS[0][:, r, :], b4r[:, :], ALU.add)
                            i.then_inc(yo_set, 1)

                    def with_beta(b):
                        if live(b):
                            pool.wait_ge(yx_in, loaded(b))
                            for r in range(len(rows_of(b))):
                                i = nc.gpsimd.tensor_tensor(YX[:, r, :], YX[:, r, :], bet[:, :], ALU.add)
                            i.then_inc(yx_set, 1)

                    def times_gamma(b, rs):
                        if live(b):
                            for r in rs[:len(rows_of(b)) - rs[0]]:
                                pool.wait_ge(norm_set, rows_done(b, r))
                                nc.gpsimd.tensor_tensor(Y[:, r, :], Y[:, r, :], gam[:, :], ALU.mult).then_inc(g_set, 1)

                    def t(b, m):
                        if live(b):
                            hid.t(pool, hi_(b, m), m % 2, sum(rows_of(b)))

                    def lo(b, m):
                        if live(b):
                            c = sum(rows_of(b))
                            hid.lo(nc.gpsimd, hi_(b, m), m % 2, HL[:, m, 0:c], HH[:, m, 0:c], c)

                    def body(b):
                        with_b4(b)
                        t(b, 0)
                        times_gamma(b - 1, (0, 1))
                        lo(b, 0)
                        t(b, 1)
                        times_gamma(b - 1, (2, 3))
                        lo(b, 1)
                        t(b, 2)
                        lo(b, 2)
                        t(b, 3)
                        lo(b, 3)
                        with_beta(b)
                    loop(pool, body)

                @block.scalar
                def _(act):
                    def turns(b, i):
                        if live(b):
                            turn.hi(act, TS * b + 2 * i, b, XH, turn_src(i)[2], 2 * i if b is 0 else 0)

                    def h_(f, b, m):
                        if live(b):
                            c = sum(rows_of(b))
                            if f == "hi":
                                hid.hi(act, hi_(b, m), m % 2, HH[:, m, 0:c], c)
                            else:
                                (hid.e if f == "e" else hid.r)(act, hi_(b, m), m % 2, c)

                    def normed(b, nrm, sem_, to, n, rs):
                        if live(b):
                            act.wait_ge(nrm.set, b + 1)
                            if n == 2:
                                wait(act, y_out, 16 * b)
                            for r in rs[:len(rows_of(b)) - rs[0]]:
                                nc.scalar.activation(to[:, r, :], Y[:, r, :], ACT.Identity, bias=nrm.nm[:, r:r + 1], scale=nrm.y[:, r:r + 1]).then_inc(sem_, 1)

                    def body(b):
                        h_("e", b, 0)
                        h_("r", b, 0)
                        normed(b - 1, norm, norm_set, Y, 1, (0, 1))
                        h_("e", b, 1)
                        h_("hi", b, 0)
                        h_("r", b, 1)
                        normed(b - 1, norm, norm_set, Y, 1, (2, 3))
                        h_("e", b, 2)
                        h_("hi", b, 1)
                        h_("r", b, 2)
                        if live(b):
                            turns(b + 1, 0)
                        h_("e", b, 3)
                        h_("hi", b, 2)
                        h_("r", b, 3)
                        if live(b):
                            turns(b + 1, 1)
                        h_("hi", b, 3)
                        if live(b):
                            turns(b + 1, 2)
                            turns(b + 1, 3)
                        normed(b - 1, norm2, y_set, OUT, 2, (0, 1, 2, 3))

                    for i in range(STEPS):
                        turns(0, i)
                    loop(act, body)

                @block.vector
                def _(dve):
                    norm.blank()
                    norm2.blank()

                    def turns(b, i):
                        if live(b):
                            turn.lo(dve, TS * b + 2 * i, b, XH, XL, turn_src(i)[2], 2 * i if b is 0 else 0)

                    def y_tiles(b):
                        if live(b):
                            dve.wait_ge(yo_set, b + 1)
                            nt = len(rows_of(b))
                            for r in range(nt + 1):
                                if r < nt:
                                    wait(dve, y_set, rows_done(b - 1, r))
                                    dve.wait_ge(y_done, rows_done(b, r))
                                    nc.vector.tensor_tensor(Y[:, r, :], YBANK[r][:, :], YO[:, r, :], ALU.add).then_inc(y_read, 1)
                                if r:
                                    dve.wait_ge(y_read, rows_done(b, r - 1))
                                    nc.vector.bn_stats(norm.st[:, r - 1, :], Y[:, r - 1, :]).then_inc(norm.st_set, 1)

                    def scales(b, nrm):
                        if live(b):
                            dve.wait_ge(nrm.st_set, rows_done(b))
                            nrm.rstd(dve, b, len(rows_of(b)))

                    def added(b, rs):
                        if live(b):
                            nt = len(rows_of(b))
                            if rs[0] == 0:
                                dve.wait_ge(yx_set, b + 1)
                            for r in rs:
                                if r < nt:
                                    dve.wait_ge(g_set, rows_done(b, r))
                                    nc.vector.tensor_tensor(Y[:, r, :], Y[:, r, :], YX[:, r, :], ALU.add).then_inc(s_set, 1)
                            for r in rs:
                                if r < nt:
                                    dve.wait_ge(s_set, rows_done(b, r))
                                    nc.vector.bn_stats(norm2.st[:, r, :], Y[:, r, :]).then_inc(norm2.st_set, 1)

                    def z(b, m):
                        if live(b):
                            c = sum(rows_of(b))
                            dve.wait_ge(h_done, hi_(b, m) + 1)
                            hid.z_col(dve, hi_(b, m), m % 2, HBANK[m % 2][:, 0:c], b3c[:, m:m + 1], c)

                    def n(b, m):
                        if live(b):
                            hid.n(dve, hi_(b, m), m % 2, sum(rows_of(b)))

                    def m_(b, m):
                        if live(b):
                            hid.m(dve, hi_(b, m), m % 2, sum(rows_of(b)))

                    def body(b):
                        y_tiles(b - 1)
                        z(b, 0)
                        n(b, 0)
                        scales(b - 1, norm)
                        z(b, 1)
                        m_(b, 0)
                        n(b, 1)
                        z(b, 2)
                        m_(b, 1)
                        n(b, 2)
                        added(b - 1, (0, 1))
                        z(b, 3)
                        m_(b, 2)
                        if live(b):
                            turns(b + 1, 0)
                        n(b, 3)
                        added(b - 1, (2, 3))
                        if live(b):
                            turns(b + 1, 1)
                        m_(b, 3)
                        if live(b):
                            turns(b + 1, 2)
                        scales(b - 1, norm2)
                        if live(b):
                            turns(b + 1, 3)

                    for i in range(STEPS):
                        turns(0, i)
                    dve.wait_ge(cst, 64)
                    loop(dve, body)

                @block.tensor
                def _(pe):
                    def turns(b, i):
                        if live(b):
                            buf, ks, _ = turn_src(i)
                            pe.wait_ge(rows_in[i // 2], loaded(b))
                            turn.pe(pe, TS * b + 2 * i, b, buf, ks, i == 0, 2 * i if b is 0 else 0)

                    def body(b):
                        if not live(b):
                            return
                        c = sum(rows_of(b))
                        for m in range(KD):
                            cols = slice(m * P, (m + 1) * P)
                            wait(pe, hid.v_set, hi_(b, m) - 1)
                            if b is 0 and m == 0:
                                pe.wait_ge(turn.lo_set, 4)
                            for k in range(2 * KD):
                                if m == 0:
                                    pe.wait_ge(turn.lo_set, TS * b + k + 1)
                                last = mm3(HBANK[m % 2][:, 0:c], WHI[:, k, cols], WLO[:, k, cols], XH[:, k, 0:c], XL[:, k, 0:c], k == 0, k == 2 * KD - 1)
                            last.then_inc(h_done, 1)
                        for k in range(KD):
                            turns(b + 1, k)
                            pe.wait_ge(hid.lo_set, hi_(b, k) + 1)
                            for r in range(len(rows_of(b))):
                                if k == 0:
                                    wait(pe, y_read, rows_done(b - 1, r))
                                rows = slice(r * P, (r + 1) * P)
                                last = mm3(YBANK[r][:, :], HH[:, k, rows], HL[:, k, rows], WHI[:, U4 + k, :], WLO[:, U4 + k, :], k == 0, k == KD - 1)
                                if k == KD - 1:
                                    last.then_inc(y_done, 1)

                    for i in range(STEPS):
                        turns(0, i)
                    loop(pe, body)


_INS = ['x', 'src', 'dst', 'edge_attr_64', 'L0_gnn_W1', 'L0_gnn_b1', 'L0_gnn_W2', 'L0_gnn_b2', 'L0_gnn_eps',
        'L1_gnn_W1', 'L1_gnn_b1', 'L1_gnn_W2', 'L1_gnn_b2', 'L1_gnn_W3', 'L1_gnn_b3', 'L1_gnn_W4', 'L1_gnn_b4',
        'L1_gnn_gamma', 'L1_gnn_beta']
_OUTS = [((N, D), 'float32')]


def kernel(**inputs):
    import numpy as _np
    import concourse.bacc as _bacc
    from concourse import mybir as _mybir
    from concourse.bass_utils import run_bass_kernel_spmd as _run

    nc = _bacc.Bacc("TRN2", target_bir_lowering=False, num_devices=1)
    arrays, args = {}, []
    for name in _INS:
        a = _np.ascontiguousarray(inputs[name])
        arrays[f"in_{name}_dram"] = a
        args.append(nc.dram_tensor(f"in_{name}_dram", a.shape, _mybir.dt.from_np(a.dtype), kind="ExternalInput").ap())
    for i, (shape, dtype) in enumerate(_OUTS):
        dt = _mybir.dt.from_np(_np.dtype(dtype))
        args.append(nc.dram_tensor(f"out_{i}_dram", shape, dt, kind="ExternalOutput").ap())
    gnn_resnorm_kernel(nc, *args)
    r = _run(nc, [arrays], core_ids=[0])
    got = tuple(r.results[0][f"out_{i}_dram"] for i in range(len(_OUTS)))
    return got[0]
```
